# Optimizing a Trainium2 kernel written in Bass

```python
import numpy as np
import jax
import jax.numpy as jnp

def _softmax(x, axis=-1):
    return jax.nn.softmax(x, axis=axis)

def _gelu(x):
    return jax.nn.gelu(x, approximate=True)

def _silu(x):
    return jax.nn.silu(x)

def _sigmoid(x):
    return jax.nn.sigmoid(x)

def _layernorm(x, axis=-1, eps=1e-05):
    m = jnp.mean(x, axis=axis, keepdims=True)
    v = jnp.var(x, axis=axis, keepdims=True)
    return (x - m) / jnp.sqrt(v + eps)

def _scatter_add(tgt, idx, src, axis=0):
    return tgt.at[idx].add(src)

def _segment_sum(src, seg, n):
    return jax.ops.segment_sum(src, seg, n)
kernel_name = 'mk_gnn_resnorm_d1_gnn_r8_388573'

def setup_inputs(seed: int=0):
    np.random.seed(seed)
    _w = jnp.asarray

    def _rec_inputs():
        import jax
        import jax.numpy as jnp
        _gk = jax.random.key(seed)
        x = -6.415e-05 + 1 * jax.random.normal(jax.random.fold_in(_gk, 1), (6250, 512), jnp.float32)
        _s = jax.random.randint(jax.random.fold_in(_gk, 2), (50000,), 0, 6250, jnp.int32)
        _d = jax.random.randint(jax.random.fold_in(_gk, 3), (50000,), 0, 6250, jnp.int32)
        _loop = jnp.arange(6250, dtype=jnp.int32)
        src = jnp.concatenate([_s, _d, _loop])
        dst = jnp.concatenate([_d, _s, _loop])
        _o = jnp.argsort(dst, stable=True)
        src = src[_o]
        dst = dst[_o]
        return (x, src, dst)
    x, src, dst = _rec_inputs()

    def _L0_gnn_setup():
        import jax, jax.numpy as jnp
        import numpy as np
        N, E, DM, H, DFF = (2500, 80000, 512, 8, 256)
        DK = DM // H

        def _layernorm(x, g, b, eps=1e-05):
            mu = jnp.mean(x, axis=-1, keepdims=True)
            var = jnp.mean(jnp.square(x - mu), axis=-1, keepdims=True)
            return (x - mu) * jax.lax.rsqrt(var + eps) * g + b
        key = jax.random.key(seed)
        ks = jax.random.split(key, 12)
        s = 0.02
        h = jax.random.normal(ks[0], (N, DM), dtype=jnp.float32)
        src = jax.random.randint(ks[1], (E,), 0, N, dtype=jnp.int32)
        dst = jnp.sort(jax.random.randint(ks[2], (E,), 0, N, dtype=jnp.int32))
        return {'h': h, 'src': src, 'dst': dst, 'Wq': jax.random.normal(ks[3], (DM, DM), dtype=jnp.float32) * s, 'Wk': jax.random.normal(ks[4], (DM, DM), dtype=jnp.float32) * s, 'Wv': jax.random.normal(ks[5], (DM, DM), dtype=jnp.float32) * s, 'Wo': jax.random.normal(ks[6], (DM, DM), dtype=jnp.float32) * s, 'ln1_g': jnp.ones((DM,), jnp.float32), 'ln1_b': jnp.zeros((DM,), jnp.float32), 'ln2_g': jnp.ones((DM,), jnp.float32), 'ln2_b': jnp.zeros((DM,), jnp.float32), 'W1': jax.random.normal(ks[7], (DM, DFF), dtype=jnp.float32) * s, 'b1': jnp.zeros((DFF,), jnp.float32), 'W2': jax.random.normal(ks[8], (DFF, DM), dtype=jnp.float32) * s, 'b2': jnp.zeros((DM,), jnp.float32)}
    _L0_gnn_all = _L0_gnn_setup()
    _L0_gnn_in = {k: v for k, v in _L0_gnn_all.items() if k in ('Wq', 'Wk', 'Wv', 'Wo', 'ln1_g', 'ln1_b', 'ln2_g', 'ln2_b', 'W1', 'b1', 'W2', 'b2')}
    del _L0_gnn_all
    return {'x': x, 'src': src, 'dst': dst, 'L0_gnn_Wq': _L0_gnn_in['Wq'], 'L0_gnn_Wk': _L0_gnn_in['Wk'], 'L0_gnn_Wv': _L0_gnn_in['Wv'], 'L0_gnn_Wo': _L0_gnn_in['Wo'], 'L0_gnn_ln1_g': _L0_gnn_in['ln1_g'], 'L0_gnn_ln1_b': _L0_gnn_in['ln1_b'], 'L0_gnn_ln2_g': _L0_gnn_in['ln2_g'], 'L0_gnn_ln2_b': _L0_gnn_in['ln2_b'], 'L0_gnn_W1': _L0_gnn_in['W1'], 'L0_gnn_b1': _L0_gnn_in['b1'], 'L0_gnn_W2': _L0_gnn_in['W2'], 'L0_gnn_b2': _L0_gnn_in['b2']}

def reference(x, src, dst, L0_gnn_Wq, L0_gnn_Wk, L0_gnn_Wv, L0_gnn_Wo, L0_gnn_ln1_g, L0_gnn_ln1_b, L0_gnn_ln2_g, L0_gnn_ln2_b, L0_gnn_W1, L0_gnn_b1, L0_gnn_W2, L0_gnn_b2):
    import jax
    import jax.numpy as jnp

    def _L0_gnn_ref(h, src, dst, Wq, Wk, Wv, Wo, ln1_g, ln1_b, ln2_g, ln2_b, W1, b1, W2, b2):
        import jax, jax.numpy as jnp
        import numpy as np
        N, E, DM, H, DFF = (2500, 80000, 512, 8, 256)
        DK = DM // H

        def _layernorm(x, g, b, eps=1e-05):
            mu = jnp.mean(x, axis=-1, keepdims=True)
            var = jnp.mean(jnp.square(x - mu), axis=-1, keepdims=True)
            return (x - mu) * jax.lax.rsqrt(var + eps) * g + b
        n = h.shape[0]
        q = (h @ Wq).reshape(n, H, DK)
        k = (h @ Wk).reshape(n, H, DK)
        v = (h @ Wv).reshape(n, H, DK)
        e = jnp.einsum('ehd,ehd->eh', k[src], q[dst]) / np.sqrt(DK).astype(np.float32)
        m = jax.ops.segment_max(e, dst, num_segments=n)
        ex = jnp.exp(e - m[dst])
        z = jax.ops.segment_sum(ex, dst, num_segments=n)
        attn = ex / z[dst]
        a = jax.ops.segment_sum(attn[:, :, None] * v[src], dst, num_segments=n)
        a = a.reshape(n, DM)
        o = a @ Wo
        x = _layernorm(h + o, ln1_g, ln1_b)
        f = jax.nn.relu(x @ W1 + b1) @ W2 + b2
        return _layernorm(x + f, ln2_g, ln2_b)
    x = _layernorm(x + _L0_gnn_ref(x, src, dst, L0_gnn_Wq, L0_gnn_Wk, L0_gnn_Wv, L0_gnn_Wo, L0_gnn_ln1_g, L0_gnn_ln1_b, L0_gnn_ln2_g, L0_gnn_ln2_b, L0_gnn_W1, L0_gnn_b1, L0_gnn_W2, L0_gnn_b2), axis=-1)
    return x

_drawn_inputs = setup_inputs


def setup_inputs(seed=0):
    import zlib

    import numpy as np

    out = dict(_drawn_inputs(seed))
    spreads = {'L0_gnn_ln1_g': (1.0, 0.2),
     'L0_gnn_ln1_b': (0.0, 0.1),
     'L0_gnn_ln2_g': (1.0, 0.2),
     'L0_gnn_ln2_b': (0.0, 0.1),
     'L0_gnn_b1': (0.0, 0.752),
     'L0_gnn_b2': (0.0, 0.1)}
    factors = {'L0_gnn_Wq': 8.0, 'L0_gnn_Wk': 8.0}
    for name, (base, spread) in spreads.items():
        noise = np.random.default_rng([zlib.crc32(name.encode()), seed]).standard_normal(out[name].shape)
        drawn = base * np.exp(spread * noise) if base else spread * noise
        out[name] = jnp.asarray(drawn.astype(out[name].dtype))
    for name, factor in factors.items():
        out[name] = (out[name] * factor).astype(out[name].dtype)
    return out
```

```python
import concourse.bass as bass
from concourse import mybir
from contextlib import ExitStack

N, E, DM, H, DFF = 6250, 106250, 512, 8, 256
DK = DM // H
P = 128

GT = 8
NSLOT = 3
GROUPS = 105
TILES = GROUPS * GT
BLOCKS, BROWS = 7, 120
FULL_ROWS = E // P
TAIL = E % P
LAST_ROWS = FULL_ROWS - (BLOCKS - 1) * BROWS
NT = (N + P - 1) // P
LAST_START = N - P
W = DM + 2 * H
FEW = 32
MORE = P - FEW
NULL_A = TILES * FEW
NULL_MORE = TILES * MORE
NULL_B = TILES
BIG = 1.0e30
FAR = 1.0e6
EPS = 1e-5
assert TILES * P >= E and GROUPS % NSLOT == 0 and BLOCKS * BROWS == TILES


class Chain:

    def __init__(self, eng, sem):
        self.eng, self.sem, self.base, self.n = eng, sem, 0, 0

    def __call__(self, ins):
        ins.then_inc(self.sem, 1)
        self.n += 1
        self.eng.wait_ge(self.sem, self.base + self.n)


def build(nc, x, src, dst, Wq, Wk, Wv, Wo, ln1_g, ln1_b, ln2_g, ln2_b, W1, b1, W2, b2, out):
    f32, i32 = mybir.dt.float32, mybir.dt.int32
    ALU, ACT, AX = mybir.AluOpType, mybir.ActivationFunctionType, mybir.AxisListType
    ds = bass.ds

    with ExitStack() as ctx:
        def sb(name, shape, dt=f32, scope=ctx):
            return scope.enter_context(nc.sbuf_tensor(name, shape, dt))

        def sem(name):
            return ctx.enter_context(nc.semaphore(name))

        def dram(name, shape):
            return nc.dram_tensor(name, shape, f32).ap()

        q_rows = dram("q_rows", [N, DM])
        kv_rows = dram("kv_rows", [N, 2 * DM])
        breaks_rows = dram("breaks_rows", [TILES * H, 132])
        starts_rows = dram("starts_rows", [TILES, P])
        parts = dram("parts", [TILES * FEW + 1, W])
        more_parts = dram("more_parts", [TILES * MORE, W])
        firsts = dram("firsts", [TILES + 1, W])

        bank = [ctx.enter_context(nc.psum_tensor(f"bank{i}", [P, 512], f32)) for i in range(8)]
        ident = sb("ident", [P, P])
        ones_row = sb("ones_row", [1, P])
        iota_row = sb("iota_row", [P, P])
        edge_nodes = sb("edge_nodes", [P, TILES, 2], i32)
        edge_runs = sb("edge_runs", [P, TILES, 2])
        last_run = sb("last_run", [P, TILES], i32)
        first_dst = sb("first_dst", [P, TILES])
        node_id = sb("node_id", [P, NT])
        node_rows = sb("node_rows", [P, NT, 3], i32)
        most_runs = sb("most_runs", [P, 1], i32)

        with ExitStack() as st:
            dst_i = sb("dst_i", [BROWS, BLOCKS, P], i32, st)
            src_i = sb("src_i", [BROWS, BLOCKS, P], i32, st)
            dst_f = sb("dst_f", [BROWS, BLOCKS, P], f32, st)
            src_f = sb("src_f", [BROWS, BLOCKS, P], f32, st)
            begins = sb("begins", [BROWS, BLOCKS, 132], f32, st)
            breaks = sb("breaks", [BROWS, BLOCKS, 132], f32, st)
            runs = sb("runs", [BROWS, BLOCKS, P], f32, st)
            starts = sb("starts", [BROWS, BLOCKS, P], f32, st)
            ones = sb("ones", [BROWS, P], f32, st)
            first_row = sb("first_row", [1, TILES], f32, st)
            null_row = sb("null_row", [1, W], f32, st)
            padded = sem("padded")
            edges_in = sem("edges_in")
            consts = sem("consts")
            tabled = sem("tabled")
            rows_ready = sem("rows_ready")
            turned = sem("turned")
            turned_used = sem("turned_used")
            first_ready = sem("first_ready")
            spread = sem("spread")
            d1 = sem("d1")
            with nc.Block() as block:
                @block.sync
                def _(sp):
                    sp.wait_ge(padded, 2)
                    for dram_list, rows in ((src, src_i), (dst, dst_i)):
                        whole = (BLOCKS - 1) * BROWS * P
                        sp.dma_start(rows[:, 0:BLOCKS - 1, :], dram_list[0:whole].rearrange(
                            "(b p j) -> p b j", p=BROWS, j=P)).then_inc(edges_in, 16)
                        sp.dma_start(rows[0:LAST_ROWS, BLOCKS - 1, :], dram_list[whole:FULL_ROWS * P].rearrange(
                            "(p j) -> p j", j=P)).then_inc(edges_in, 16)
                        sp.dma_start(rows[LAST_ROWS:LAST_ROWS + 1, BLOCKS - 1, 0:TAIL],
                                     dram_list[FULL_ROWS * P:E].rearrange("(p j) -> p j", p=1)).then_inc(edges_in, 16)
                    sp.wait_ge(rows_ready, 3)
                    by_head = breaks_rows.rearrange("(b p h) f -> h p b f", p=BROWS, h=H)
                    for h in range(H):
                        sp.dma_start(by_head[h], breaks[:, :, :]).then_inc(tabled, 16)
                    sp.dma_start(starts_rows.rearrange("(b p) f -> p b f", p=BROWS), starts[:, :, :]).then_inc(tabled, 16)
                    sp.dma_start(parts[NULL_A:NULL_A + 1, :], null_row[:, :]).then_inc(tabled, 16)
                    sp.dma_start(firsts[NULL_B:NULL_B + 1, :], null_row[:, :]).then_inc(tabled, 16)
                    sp.wait_ge(tabled, 11 * 16)

                @block.gpsimd
                def _(g):
                    chain = Chain(g, consts)
                    chain(g.memset(ident[:, :], 0.0))
                    chain(g.affine_select(out=ident[:, :], in_=ident[:, :], compare_op=ALU.not_equal, fill=1.0,
                                          base=0, pattern=[[-1, P]], channel_multiplier=1))
                    chain(g.memset(ones_row[:, :], 1.0))
                    chain(g.iota(iota_row[:, :], pattern=[[1, P]], base=0, channel_multiplier=0,
                                 allow_small_or_imprecise_dtypes=True))
                    chain(g.iota(node_id[:, 0:NT - 1], pattern=[[P, NT - 1]], base=0, channel_multiplier=1,
                                 allow_small_or_imprecise_dtypes=True))
                    chain(g.iota(node_id[:, NT - 1:NT], pattern=[[0, 1]], base=LAST_START, channel_multiplier=1,
                                 allow_small_or_imprecise_dtypes=True))

                @block.vector
                def _(v):
                    chain = Chain(v, d1)
                    v.memset(src_i[:, BLOCKS - 1, :], 0).then_inc(padded, 1)
                    v.memset(dst_i[:, BLOCKS - 1, :], N).then_inc(padded, 1)
                    chain(v.memset(null_row[:, :], 0.0))
                    v.memset(null_row[:, DM + H:W], -BIG).then_inc(rows_ready, 1)
                    chain(v.memset(ones[:, :], 1.0))
                    chain(v.memset(begins[:, :, :], 1.0))
                    v.wait_ge(edges_in, 96)
                    chain(v.tensor_copy(src_f[:, :, :], src_i[:, :, :]))
                    chain(v.tensor_copy(dst_f[:, :, :], dst_i[:, :, :]))
                    chain(v.tensor_tensor(out=begins[:, :, 1:P], in0=dst_f[:, :, 1:P], in1=dst_f[:, :, 0:P - 1],
                                          op=ALU.not_equal))
                    v.tensor_scalar(out=breaks[:, :, :], in0=begins[:, :, :], scalar1=-BIG, scalar2=None,
                                    op0=ALU.mult).then_inc(rows_ready, 1)
                    chain(v.tensor_scalar(out=starts[:, :, :], in0=begins[:, :, 0:P], scalar1=-FAR, scalar2=FAR,
                                          op0=ALU.mult, op1=ALU.add))
                    chain(v.tensor_tensor(out=starts[:, :, :], in0=starts[:, :, :], in1=dst_f[:, :, :], op=ALU.add))
                    v.memset(starts[:, :, 0:1], FAR).then_inc(rows_ready, 1)
                    for b in range(BLOCKS):
                        chain(v.tensor_tensor_scan(out=runs[:, b, :], data0=ones[:, :], data1=begins[:, b, 0:P],
                                                   initial=-1.0, op0=ALU.mult, op1=ALU.add))
                    for b in range(BLOCKS):
                        v.wait_ge(turned, b + 1)
                        t = bank[b % 2][:, 0:4 * BROWS].rearrange("p (a t) -> p a t", a=4)
                        cols = slice(b * BROWS, (b + 1) * BROWS)
                        chain(v.tensor_copy(edge_nodes[:, cols, 0], t[:, 0, :]))
                        chain(v.tensor_scalar(out=edge_nodes[:, cols, 1], in0=t[:, 1, :], scalar1=float(N - 1),
                                              scalar2=None, op0=ALU.min))
                        chain(v.tensor_copy(edge_runs[:, cols, 0], t[:, 2, :]))
                        chain(v.tensor_copy(edge_runs[:, cols, 1], t[:, 3, :]))
                        chain(v.tensor_copy(last_run[96:P, cols], t[96:P, 2, :]))
                        v.tensor_copy(first_row[:, cols], t[0:1, 1, :]).then_inc(turned_used, 1)
                    v.wait_ge(spread, 1)
                    half = TILES // 2
                    chain(v.tensor_copy(first_dst[:, 0:half], bank[2][:, 0:half]))
                    chain(v.tensor_copy(first_dst[:, half:TILES], bank[3][:, 0:half]))
                    chain(v.tensor_reduce(out=most_runs[96:P, :], in_=edge_runs[96:P, :, 0], axis=AX.X, op=ALU.max))

                @block.tensor
                def _(pe):
                    pe.wait_ge(consts, 6)
                    pe.wait_ge(d1, 8 + BLOCKS)
                    for b in range(BLOCKS):
                        if b >= 2:
                            pe.wait_ge(turned_used, b - 1)
                        for a, rows in enumerate((src_f[:, b, :], dst_f[:, b, :], runs[:, b, :], begins[:, b, 0:P])):
                            last = pe.transpose(bank[b % 2][:, a * BROWS:(a + 1) * BROWS], rows, ident[0:BROWS, 0:BROWS])
                        last.then_inc(turned, 1)
                    pe.wait_ge(turned_used, BLOCKS)
                    half = TILES // 2
                    pe.matmul(bank[2][:, 0:half], ones_row[:, :], first_row[:, 0:half], start=True, stop=True)
                    pe.matmul(bank[3][:, 0:half], ones_row[:, :], first_row[:, half:TILES], start=True,
                              stop=True).then_inc(spread, 1)

        with ExitStack() as st:
            w_sb = [sb(n, [P, 4, DM], f32, st) for n in ("wq_sb", "wk_sb", "wv_sb")]
            xt = [sb(f"xt{i}", [P, DM], f32, st) for i in range(2)]
            xT = [sb(f"xT{i}", [P, 4, P], f32, st) for i in range(2)]
            q_out = [sb(f"q_out{i}", [P, DM], f32, st) for i in range(2)]
            kv_out = [sb(f"kv_out{i}", [P, 2 * DM], f32, st) for i in range(2)]
            below = sb("below", [P, TILES], f32, st)
            nid = [sb(f"nid{i}", [P, 1], f32, st) for i in range(2)]
            cnt = [sb(f"cnt{i}", [P, 2], f32, st) for i in range(2)]
            tile_i = [sb(f"tile_i{i}", [P, 1], i32, st) for i in range(2)]
            tile_f = [sb(f"tile_f{i}", [P, 1], f32, st) for i in range(2)]
            row_of = [sb(f"row_of{i}", [P, P], f32, st) for i in range(2)]
            counts = sb("counts", [P, NT, 4], f32, st)
            used = sb("used", [P, NT, 3], f32, st)
            over = sb("over", [P, NT], f32, st)
            row_f = sb("row_f", [P, NT, 3], f32, st)
            weights_in = sem("weights_in")
            x_in = [sem(f"x_in{i}") for i in range(2)]
            x_turned = sem("x_turned")
            xT_ready = sem("xT_ready")
            qkv_done = sem("qkv_done")
            q_ready = sem("q_ready")
            k_ready = sem("k_ready")
            v_ready = sem("v_ready")
            q_stored = [sem(f"q_stored{i}") for i in range(2)]
            kv_stored = [sem(f"kv_stored{i}") for i in range(2)]
            tile_ready = sem("tile_ready")
            go = sem("go")
            row_in = [sem(f"row_in{i}") for i in range(2)]
            d2 = sem("d2")

            def rows_at(t):
                return slice(LAST_START, N) if isinstance(t, int) and t == NT - 1 else ds(t * P, P)

            def steps(eng, one):
                one(0, 0)
                one(1, 1)
                with eng.Fori(2, NT - 2, 2) as t:
                    one(t, 0)
                    one(t + 1, 1)
                one(NT - 1, 0)

            def nth(t, par):
                return t - par + 2

            with nc.Block() as block:
                @block.sync
                def _(sp):
                    for w, s in zip((Wq, Wk, Wv), w_sb):
                        sp.dma_start(s[:, :, :], w.rearrange("(c p) n -> p c n", p=P)).then_inc(weights_in, 16)

                    def load(t, par):
                        if not isinstance(t, int) or t >= 2:
                            sp.wait_ge(x_turned, t - 1)
                        sp.dma_start(xt[par][:, :], x[rows_at(t), :]).then_inc(x_in[par], 16)

                    def store(t, par):
                        if isinstance(t, int) and t == NT - 1:
                            sp.wait_ge(q_stored[1], 8 * (NT - 1))
                            sp.wait_ge(kv_stored[1], 8 * (NT - 1))
                        sp.wait_ge(q_ready, t + 1)
                        sp.dma_start(q_rows[rows_at(t), :], q_out[par][:, :]).then_inc(q_stored[par], 16)
                        sp.wait_ge(k_ready, t + 1)
                        sp.wait_ge(v_ready, t + 1)
                        sp.dma_start(kv_rows[rows_at(t), :], kv_out[par][:, :]).then_inc(kv_stored[par], 16)

                    load(0, 0)
                    load(1, 1)
                    with sp.Fori(2, NT - 2, 2) as t:
                        load(t, 0)
                        store(t - 2, 0)
                        load(t + 1, 1)
                        store(t - 1, 1)
                    load(NT - 1, 0)
                    store(NT - 3, 0)
                    store(NT - 2, 1)
                    store(NT - 1, 0)
                    sp.wait_ge(q_stored[0], 16 * (NT // 2 + 1))
                    sp.wait_ge(kv_stored[0], 16 * (NT // 2 + 1))

                @block.tensor
                def _(pe):
                    pe.wait_ge(weights_in, 48)

                    def turn(t, par):
                        pe.wait_ge(x_in[par], 8 * nth(t, par))
                        if not isinstance(t, int) or t >= 2:
                            pe.wait_ge(xT_ready, t - 1)
                        for c in range(4):
                            last = pe.transpose(bank[par][:, c * P:(c + 1) * P], xt[par][:, c * P:(c + 1) * P], ident[:, :])
                        last.then_inc(x_turned, 1)

                    def project(t, par):
                        pe.wait_ge(xT_ready, t + 1)
                        if not isinstance(t, int) or t >= 2:
                            pe.wait_ge(q_ready, t - 1)
                            pe.wait_ge(k_ready, t - 1)
                            pe.wait_ge(v_ready, t - 1)
                        for m in range(3):
                            for c in range(4):
                                last = pe.matmul(bank[2 + 3 * par + m][:, :], xT[par][:, c, :], w_sb[m][:, c, :],
                                                 start=c == 0, stop=c == 3)
                            last.then_inc(qkv_done, 1)

                    turn(0, 0)
                    turn(1, 1)
                    project(0, 0)
                    with pe.Fori(2, NT - 2, 2) as t:
                        turn(t, 0)
                        project(t - 1, 1)
                        turn(t + 1, 1)
                        project(t, 0)
                    turn(NT - 1, 0)
                    project(NT - 2, 1)
                    project(NT - 1, 0)

                @block.scalar
                def _(act):
                    def evacuate(t, par):
                        late = not isinstance(t, int) or t >= 2
                        act.wait_ge(qkv_done, 3 * t + 1)
                        if late:
                            act.wait_ge(q_stored[par], 8 * nth(t, par) - 16)
                        act.activation(q_out[par][:, :], bank[2 + 3 * par][:, :], ACT.Copy,
                                       scale=1.0 / DK ** 0.5).then_inc(q_ready, 1)
                        act.wait_ge(qkv_done, 3 * t + 2)
                        if late:
                            act.wait_ge(kv_stored[par], 8 * nth(t, par) - 16)
                        act.activation(kv_out[par][:, 0:DM], bank[3 + 3 * par][:, :], ACT.Copy).then_inc(k_ready, 1)
                        act.wait_ge(qkv_done, 3 * t + 3)
                        act.activation(kv_out[par][:, DM:2 * DM], bank[4 + 3 * par][:, :], ACT.Copy).then_inc(v_ready, 1)

                    steps(act, evacuate)

                @block.vector
                def _(v):
                    chain = Chain(v, d2)

                    def copy_xT(t, par):
                        v.wait_ge(x_turned, t + 1)
                        if not isinstance(t, int) or t >= 2:
                            v.wait_ge(qkv_done, 3 * t - 3)
                        v.tensor_copy(xT[par][:, :, :], bank[par][:, :].rearrange("p (c n) -> p c n", c=4)).then_inc(xT_ready, 1)

                    def count_tiles(t, par):
                        chain(v.tensor_copy(nid[par][:, :], node_id[:, ds(t, 1)]))
                        for a, op in ((0, ALU.is_lt), (1, ALU.is_le)):
                            chain(v.tensor_scalar(out=below[:, :], in0=first_dst[:, :], scalar1=nid[par][:, 0:1],
                                                  scalar2=None, op0=op))
                            chain(v.tensor_reduce(out=cnt[par][:, a:a + 1], in_=below[:, :], axis=AX.X, op=ALU.add))
                        chain(v.tensor_copy(counts[:, ds(t, 1), 0:2], cnt[par][:, :].unsqueeze(1)))
                        chain(v.tensor_scalar(out=tile_f[par][:, :], in0=cnt[par][:, 0:1], scalar1=-1.0, scalar2=0.0,
                                              op0=ALU.add, op1=ALU.max))
                        chain(v.tensor_copy(tile_i[par][:, :], tile_f[par][:, :]))
                        v.tensor_copy(tile_f[par][:, :], tile_f[par][:, :]).then_inc(tile_ready, 1)

                    def count_runs(t, par):
                        v.wait_ge(row_in[par], 8 * nth(t, par))
                        for a, op in ((0, ALU.is_lt), (1, ALU.is_le)):
                            chain(v.tensor_scalar(out=below[:, 0:P], in0=row_of[par][:, :], scalar1=nid[par][:, 0:1],
                                                  scalar2=None, op0=op))
                            chain(v.tensor_reduce(out=cnt[par][:, a:a + 1], in_=below[:, 0:P], axis=AX.X, op=ALU.add))
                        chain(v.tensor_copy(counts[:, ds(t, 1), 2:4], cnt[par][:, :].unsqueeze(1)))

                    COUNT = 8 + 5
                    copy_xT(0, 0)
                    count_tiles(0, 0)
                    copy_xT(1, 1)
                    count_tiles(1, 1)
                    count_runs(0, 0)
                    before = chain.n
                    with v.Fori(2, NT - 2, 2) as t:
                        for k in range(2):
                            chain.base, chain.n = (t + k - 2) * COUNT + before, 0
                            copy_xT(t + k, k)
                            count_tiles(t + k, k)
                            count_runs(t + k - 1, 1 - k)
                            assert chain.n == COUNT
                    chain.base, chain.n = 0, before + (NT - 3) * COUNT
                    copy_xT(NT - 1, 0)
                    count_tiles(NT - 1, 0)
                    count_runs(NT - 2, 1)
                    count_runs(NT - 1, 0)
                    chain(v.tensor_tensor(out=used[:, :, 0], in0=counts[:, :, 3], in1=counts[:, :, 2], op=ALU.is_gt))
                    chain(v.tensor_tensor(out=used[:, :, 1], in0=counts[:, :, 1], in1=counts[:, :, 0], op=ALU.is_gt))
                    chain(v.tensor_scalar(out=over[:, :], in0=counts[:, :, 3], scalar1=float(FEW), scalar2=None,
                                          op0=ALU.is_ge))
                    chain(v.tensor_tensor(out=used[:, :, 2], in0=used[:, :, 0], in1=over[:, :], op=ALU.mult))
                    chain(v.tensor_tensor(out=used[:, :, 0], in0=used[:, :, 0], in1=used[:, :, 2], op=ALU.subtract))
                    for a, rows, run_0, none in ((0, FEW, 0, NULL_A), (2, MORE, FEW, NULL_MORE)):
                        chain(v.tensor_scalar(out=row_f[:, :, a], in0=counts[:, :, 0], scalar1=float(rows),
                                              scalar2=float(-rows - run_0 - none), op0=ALU.mult, op1=ALU.add))
                        chain(v.tensor_tensor(out=row_f[:, :, a], in0=row_f[:, :, a], in1=counts[:, :, 3], op=ALU.add))
                    chain(v.tensor_scalar(out=row_f[:, :, 1], in0=counts[:, :, 1], scalar1=float(-1 - NULL_B),
                                          scalar2=None, op0=ALU.add))
                    chain(v.tensor_tensor(out=row_f[:, :, :], in0=row_f[:, :, :], in1=used[:, :, :], op=ALU.mult))
                    for a, none in ((0, NULL_A), (1, NULL_B), (2, NULL_MORE)):
                        chain(v.tensor_scalar(out=row_f[:, :, a], in0=row_f[:, :, a], scalar1=float(none), scalar2=None,
                                              op0=ALU.add))
                    chain(v.tensor_copy(node_rows[:, :, :], row_f[:, :, :]))

                @block.gpsimd
                def _(g):
                    top = g.to_reg(TILES - 1)

                    def fetch(t, par):
                        g.wait_ge(tile_ready, t + 1)
                        g.sem_inc(go, 1)
                        g.indirect_dma_start(out=row_of[par][:, :], out_offset=None, in_=starts_rows[:, :],
                                             in_offset=bass.IndirectOffsetOnAxis(ap=tile_i[par][:, 0:1], axis=0),
                                             bounds_check=top, oob_is_err=False).then_inc(row_in[par], 16)

                    steps(g, fetch)

        with ExitStack() as st:
            kv = [sb(f"kv{i}", [P, GT, 2 * DM], f32, st) for i in range(NSLOT)]
            qd = [sb(f"qd{i}", [P, DM], f32, st) for i in range(4)]
            prod = [sb(f"prod{i}", [P, DM], f32, st) for i in range(3)]
            score = [sb(f"score{i}", [P, GT, H], f32, st) for i in range(NSLOT)]
            idx = [sb(f"idx{i}", [P, GT, 2], i32, st) for i in range(NSLOT)]
            runs_g = [sb(f"runs_g{i}", [P, GT, 2], f32, st) for i in range(NSLOT)]
            breaks_g = [sb(f"breaks_g{i}", [GT * H, 132], f32, st) for i in range(NSLOT)]
            up = [sb(f"up{i}", [GT * H, P], f32, st) for i in range(2)]
            peak = [sb(f"peak{i}", [GT * H, P], f32, st) for i in range(2)]
            below_peak = [sb(f"below_peak{i}", [P, GT, H], f32, st) for i in range(NSLOT)]
            zm = [sb(f"zm{i}", [P, GT, 2 * H], f32, st) for i in range(NSLOT)]
            wv = [sb(f"wv{i}", [P, DM], f32, st) for i in range(4)]
            pick = [sb(f"pick{i}", [P, P], f32, st) for i in range(4)]
            part_sb = [sb(f"part_sb{i}", [P, W], f32, st) for i in range(4)]

            kv_in = [[sem(f"kv_in{s}_{j}") for j in range(GT)] for s in range(NSLOT)]
            q_in = [sem(f"q_in{i}") for i in range(4)]
            breaks_in = [sem(f"breaks_in{i}") for i in range(NSLOT)]
            idx_ready = sem("idx_ready")
            issue = sem("issue")
            prod_done = sem("prod_done")
            score_done = sem("score_done")
            score_turned = sem("score_turned")
            up_done = sem("up_done")
            peak_done = sem("peak_done")
            peak_back = sem("peak_back")
            below_ready = sem("below_ready")
            m_ready = sem("m_ready")
            z_ready = sem("z_ready")
            runs_ready = sem("runs_ready")
            pick_ready = sem("pick_ready")
            wv_ready = sem("wv_ready")
            sums_done = sem("sums_done")
            zsum_done = sem("zsum_done")
            part_ready = sem("part_ready")
            part_out = [sem(f"part_out{i}") for i in range(4)]
            part_more = [sem(f"part_more{i}") for i in range(4)]
            pe_turn = sem("pe_turn")

            def late(s, k):
                return not isinstance(s, int) or s >= k

            def group_steps(eng, one):
                for s in range(NSLOT):
                    one(s, s)
                with eng.Fori(NSLOT, GROUPS - NSLOT + 1, NSLOT) as s:
                    for k in range(NSLOT):
                        one(s + k, k)

            def uses(s, k):
                if isinstance(s, int):
                    return 16 * (s // NSLOT + 1)
                return None

            with nc.Block() as block:
                @block.gpsimd
                def _(g):
                    top = g.to_reg(N - 1)

                    def gather(s, k):
                        if late(s, NSLOT):
                            g.wait_ge(wv_ready, (s - (NSLOT - 1)) * GT)
                            g.sem_inc(issue, 1)
                        g.tensor_copy(idx[k][:, :, :], edge_nodes[:, ds(s * GT, GT), :]).then_inc(idx_ready, 1)
                        g.wait_ge(idx_ready, s + 1)
                        g.sem_inc(issue, 1)
                        for j in range(GT):
                            g.indirect_dma_start(out=kv[k][:, j, :], out_offset=None, in_=kv_rows[:, :],
                                                 in_offset=bass.IndirectOffsetOnAxis(ap=idx[k][:, j, 0:1], axis=0),
                                                 bounds_check=top, oob_is_err=False).then_inc(kv_in[k][j], 16)
                            if late(s, 1) or j >= 4:
                                g.wait_ge(prod_done, s * GT + (j - 3))
                                g.sem_inc(issue, 1)
                            g.indirect_dma_start(out=qd[j % 4][:, :], out_offset=None, in_=q_rows[:, :],
                                                 in_offset=bass.IndirectOffsetOnAxis(ap=idx[k][:, j, 1:2], axis=0),
                                                 bounds_check=top, oob_is_err=False).then_inc(q_in[j % 4], 16)

                    group_steps(g, gather)

                @block.vector
                def _(v):
                    def product(s, k, j, r):
                        v.wait_ge(kv_in[k][j], r)
                        v.wait_ge(q_in[j % 4], s * 32 + (16 * (j // 4) + 16))
                        if late(s, 1) or j >= 3:
                            v.wait_ge(score_done, s * GT + (j - 2))
                        v.tensor_tensor(out=prod[(k * GT + j) % 3][:, :], in0=kv[k][:, j, 0:DM], in1=qd[j % 4][:, :],
                                        op=ALU.mult).then_inc(prod_done, 1)

                    def reduce(s, k, j):
                        v.wait_ge(prod_done, s * GT + (j + 1))
                        if j == 0 and late(s, NSLOT):
                            v.wait_ge(below_ready, s - (NSLOT - 1))
                        v.tensor_reduce(out=score[k][:, j, :],
                                        in_=prod[(k * GT + j) % 3][:, :].rearrange("p (h d) -> p h d", h=H),
                                        axis=AX.X, op=ALU.add).then_inc(score_done, 1)

                    def scans(s, k, r):
                        turned = bank[3 + s % 2 if isinstance(s, int) else 3][0:GT * H, 0:P]
                        turned = bank[3][0:GT * H, 0:P]
                        v.wait_ge(score_turned, s + 1)
                        v.wait_ge(breaks_in[k], r)
                        if late(s, 1):
                            v.wait_ge(peak_done, s)
                        v.tensor_tensor_scan(out=up[0][:, :], data0=breaks_g[k][:, 0:P], data1=turned, initial=-BIG,
                                             op0=ALU.add, op1=ALU.max).then_inc(up_done, 1)
                        v.wait_ge(up_done, s + 1)
                        if late(s, 1):
                            v.wait_ge(peak_back, s)
                        v.tensor_tensor_scan(out=peak[0][:, ::-1], data0=breaks_g[k][:, 1:P + 1][:, ::-1],
                                             data1=up[0][:, ::-1], initial=-BIG,
                                             op0=ALU.add, op1=ALU.max).then_inc(peak_done, 1)

                    def subtract(s, k):
                        m = bank[4][:, 0:GT * H].rearrange("p (t h) -> p t h", t=GT)
                        v.wait_ge(peak_back, s + 1)
                        if late(s, NSLOT):
                            v.wait_ge(z_ready, s - (NSLOT - 1))
                            v.wait_ge(zsum_done, (s - (NSLOT - 1)) * GT)
                        v.tensor_tensor(out=below_peak[k][:, :, :], in0=score[k][:, :, :], in1=m,
                                        op=ALU.subtract).then_inc(below_ready, 1)
                        v.tensor_copy(runs_g[k][:, :, :], edge_runs[:, ds(s * GT, GT), :]).then_inc(runs_ready, 1)
                        v.wait_ge(runs_ready, s + 1)
                        v.tensor_tensor(out=zm[k][:, :, H:2 * H], in0=m,
                                        in1=runs_g[k][:, :, 1:2].to_broadcast([P, GT, H]), op=ALU.mult).then_inc(m_ready, 1)

                    def weigh(s, k, j):
                        if late(s, 1) or j >= 4:
                            v.wait_ge(zsum_done, s * GT + (j - 3))
                        v.tensor_scalar(out=pick[j % 4][:, :], in0=iota_row[:, :], scalar1=runs_g[k][:, j, 0:1],
                                        scalar2=None, op0=ALU.is_equal).then_inc(pick_ready, 1)
                        if j == 0:
                            v.wait_ge(z_ready, s + 1)
                        v.tensor_tensor(out=wv[j % 4][:, :].rearrange("p (h d) -> p h d", h=H),
                                        in0=kv[k][:, j, DM:2 * DM].rearrange("p (h d) -> p h d", h=H),
                                        in1=zm[k][:, j, 0:H].unsqueeze(2).to_broadcast([P, H, DK]),
                                        op=ALU.mult).then_inc(wv_ready, 1)

                    def step(s, k, r, rp):
                        score_it = not isinstance(s, int) or s < GROUPS
                        weigh_it = late(s, 1)
                        p = (k - 1) % NSLOT
                        after = {1: lambda: scans(s - 1, p, rp), 3: lambda: subtract(s - 1, p)}
                        take = {5: (0, 1), 6: (2, 3, 4), 7: (5, 6, 7)}
                        if score_it:
                            product(s, k, 0, r)
                        for j in range(GT):
                            if score_it:
                                if j + 1 < GT:
                                    product(s, k, j + 1, r)
                                reduce(s, k, j)
                            if weigh_it:
                                if j in after:
                                    after[j]()
                                for i in take.get(j, ()):
                                    weigh(s - 1, p, i)

                    for s in range(NSLOT):
                        step(s, s, 16, 16)
                    with v.Fori(1, GROUPS // NSLOT) as i:
                        for k in range(NSLOT):
                            step(i * NSLOT + k, k, i * 16 + 16, i * 16 if k == 0 else i * 16 + 16)
                    step(GROUPS, 0, 0, 16 * (GROUPS // NSLOT))

                @block.tensor
                def _(pe):
                    def turn_scores(s, k):
                        pe.wait_ge(score_done, s * GT + GT)
                        if late(s, 1):
                            pe.wait_ge(up_done, s)
                        pe.sem_inc(pe_turn, 1)
                        pe.transpose(bank[3][0:GT * H, 0:P], score[k][:, :, :].rearrange("p t h -> p (t h)"),
                                     ident[:, :]).then_inc(score_turned, 1)

                    def turn_back(s, k):
                        pe.wait_ge(peak_done, s + 1)
                        if late(s, 1):
                            pe.wait_ge(m_ready, s)
                        pe.sem_inc(pe_turn, 1)
                        pe.transpose(bank[4][:, 0:GT * H], peak[0][:, :], ident[0:GT * H, 0:GT * H]).then_inc(peak_back, 1)

                    def sums(s, k, j):
                        pe.wait_ge(wv_ready, s * GT + (j + 1))
                        if late(s, 1) or j >= 2:
                            pe.wait_ge(part_ready, s * (2 * GT) + (2 * j - 2))
                        if j == 0:
                            pe.wait_ge(m_ready, s + 1)
                        pe.matmul(bank[j % 2][:, :], pick[j % 4][:, :], wv[j % 4][:, :], start=True,
                                  stop=True).then_inc(sums_done, 1)
                        pe.matmul(bank[5 + j % 2][:, 0:2 * H], pick[j % 4][:, :], zm[k][:, j, :], start=True,
                                  stop=True).then_inc(zsum_done, 1)

                    def step(s, k):
                        if not isinstance(s, int) or s < GROUPS:
                            pass
                        p = (k - 1) % NSLOT
                        if late(s, 1):
                            turn_scores(s - 1, p)
                            turn_back(s - 1, p)
                            for j in range(GT):
                                sums(s - 1, p, j)

                    for s in range(NSLOT):
                        step(s, s)
                    with pe.Fori(NSLOT, GROUPS - NSLOT + 1, NSLOT) as s:
                        for k in range(NSLOT):
                            step(s + k, k)
                    step(GROUPS, 0)

                @block.scalar
                def _(act):
                    def exps(s, k):
                        act.wait_ge(below_ready, s + 1)
                        if late(s, NSLOT):
                            act.wait_ge(zsum_done, (s - (NSLOT - 1)) * GT)
                        act.activation(zm[k][:, :, 0:H], below_peak[k][:, :, :], ACT.Exp).then_inc(z_ready, 1)

                    def evacuate(s, k, j, r):
                        act.wait_ge(sums_done, s * GT + (j + 1))
                        if r is not None:
                            act.wait_ge(part_out[j % 4], r)
                            act.wait_ge(part_more[j % 4], r)
                        act.activation(part_sb[j % 4][:, 0:DM], bank[j % 2][:, :], ACT.Copy).then_inc(part_ready, 1)
                        act.wait_ge(zsum_done, s * GT + (j + 1))
                        act.activation(part_sb[j % 4][:, DM:W], bank[5 + j % 2][:, 0:2 * H], ACT.Copy).then_inc(part_ready, 1)

                    def step(s, k):
                        exps(s, k)
                        for j in range(GT):
                            r = s * 32 + 16 * (j // 4) if late(s, 1) or j >= 4 else None
                            evacuate(s, k, j, r)

                    group_steps(act, step)

                @block.sync
                def _(sp):
                    def load_breaks(s, k):
                        if late(s, NSLOT):
                            sp.wait_ge(peak_done, s - (NSLOT - 1))
                        sp.dma_start(breaks_g[k][:, :], breaks_rows[ds(s * (GT * H), GT * H), :]).then_inc(breaks_in[k], 16)

                    def store(s, k, j):
                        run = sp.value_load(last_run[P - 1:P, ds(s * GT + j, 1)])
                        sp.wait_ge(part_ready, s * (2 * GT) + (2 * j + 2))
                        sp.dma_start(parts[ds((s * GT + j) * FEW, FEW), :], part_sb[j % 4][0:FEW, :]).then_inc(part_out[j % 4], 16)
                        sp.dma_start(more_parts[ds((s * GT + j) * MORE, MORE), :], part_sb[j % 4][FEW:P, :],
                                     cond=run >= FEW, cond_hint=False).then_inc(part_more[j % 4], 16)

                    load_breaks(0, 0)

                    def step(s, k):
                        nxt = (k + 1) % NSLOT
                        if not isinstance(s, int) or s + 1 < GROUPS:
                            load_breaks(s + 1, nxt)
                        for j in range(GT):
                            store(s, k, j)

                    for s in range(NSLOT):
                        step(s, s)
                    with sp.Fori(NSLOT, GROUPS - 2 * NSLOT + 1, NSLOT) as s:
                        for k in range(NSLOT):
                            step(s + k, k)
                    for k in range(NSLOT):
                        step(GROUPS - NSLOT + k, k)
                    for i in range(4):
                        sp.wait_ge(part_out[i], 16 * (TILES // 4))
                        sp.wait_ge(part_more[i], 16 * (TILES // 4))

        with ExitStack() as st:
            crow = sb("crow", [BROWS, BLOCKS, W], f32, st)
            orow = sb("orow", [BROWS, BLOCKS, W], f32, st)
            CT = [sb(f"CT{c}", [P, TILES], f32, st) for c in range(4)]
            zT = sb("zT", [H, TILES], f32, st)
            mT = sb("mT", [H, TILES], f32, st)
            same = sb("same", [H, TILES], f32, st)
            penal = sb("penal", [H, TILES], f32, st)
            mrun = sb("mrun", [H, TILES], f32, st)
            keep = sb("keep", [H, TILES], f32, st)
            take = sb("take", [H, TILES], f32, st)
            zrun = sb("zrun", [H, TILES], f32, st)
            head_of = sb("head_of", [H, DM], f32, st)
            c_in = sem("c_in")
            head_ready = sem("head_ready")
            c_turned = sem("c_turned")
            c_taken = sem("c_taken")
            diff_ready = sem("diff_ready")
            exp_ready = sem("exp_ready")
            spread4 = sem("spread4")
            run_ready = sem("run_ready")
            back = sem("back")
            back_taken = sem("back_taken")
            c_out = sem("c_out")
            d4 = sem("d4")
            half = TILES // 2
            with nc.Block() as block:
                @block.sync
                def _(sp):
                    first_of = parts[0:TILES * FEW, :].rearrange("(b p r) f -> r p b f", p=BROWS, r=FEW)
                    sp.dma_start(crow[:, :, :], first_of[0]).then_inc(c_in, 16)
                    sp.wait_ge(back_taken, BLOCKS)
                    sp.dma_start(firsts[0:TILES, :].rearrange("(b p) f -> p b f", p=BROWS), orow[:, :, :]).then_inc(c_out, 16)
                    sp.wait_ge(c_out, 16)

                @block.gpsimd
                def _(g):
                    chain = Chain(g, head_ready)
                    chain(g.memset(head_of[:, :], 1.0))
                    chain(g.affine_select(out=head_of[:, :], in_=head_of[:, :], compare_op=ALU.is_ge, fill=0.0,
                                          base=0, pattern=[[1, DM]], channel_multiplier=-DK))
                    chain(g.affine_select(out=head_of[:, :], in_=head_of[:, :], compare_op=ALU.is_ge, fill=0.0,
                                          base=DK - 1, pattern=[[-1, DM]], channel_multiplier=DK))

                @block.tensor
                def _(pe):
                    pe.wait_ge(c_in, 16)
                    for b in range(BLOCKS):
                        if b >= 2:
                            pe.wait_ge(c_taken, b - 1)
                        for c in range(4):
                            pe.transpose(bank[b % 2][:, c * BROWS:(c + 1) * BROWS], crow[:, b, c * P:(c + 1) * P],
                                         ident[0:BROWS, 0:BROWS])
                        pe.transpose(bank[2 + b % 2][0:H, 0:BROWS], crow[:, b, DM:DM + H], ident[0:BROWS, 0:BROWS])
                        pe.transpose(bank[2 + b % 2][0:H, 256:256 + BROWS], crow[:, b, DM + H:W],
                                     ident[0:BROWS, 0:BROWS]).then_inc(c_turned, 1)
                    pe.wait_ge(head_ready, 3)
                    pe.wait_ge(c_taken, BLOCKS)
                    pe.wait_ge(exp_ready, 3)
                    for c in range(4):
                        if c >= 1:
                            pe.wait_ge(run_ready, c)
                        for a, rows in enumerate((keep, take)):
                            for i in range(2):
                                last = pe.matmul(bank[4 + 2 * a + i][:, 0:half], head_of[:, c * P:(c + 1) * P],
                                                 rows[:, i * half:(i + 1) * half], start=True, stop=True)
                        last.then_inc(spread4, 1)
                    pe.wait_ge(run_ready, 5)
                    for b in range(BLOCKS):
                        if b >= 2:
                            pe.wait_ge(back_taken, b - 1)
                        cols = slice(b * BROWS, (b + 1) * BROWS)
                        for c in range(4):
                            pe.transpose(bank[b % 2][0:BROWS, c * P:(c + 1) * P], CT[c][:, cols], ident[:, :])
                        pe.transpose(bank[2 + b % 2][0:BROWS, 0:H], zrun[:, cols], ident[0:H, 0:H])
                        pe.transpose(bank[2 + b % 2][0:BROWS, H:2 * H], mrun[:, cols], ident[0:H, 0:H]).then_inc(back, 1)

                @block.scalar
                def _(act):
                    act.wait_ge(diff_ready, 2)
                    act.activation(keep[:, :], keep[:, :], ACT.Exp).then_inc(exp_ready, 1)
                    act.activation(take[:, :], take[:, :], ACT.Exp).then_inc(exp_ready, 1)

                @block.vector
                def _(v):
                    chain = Chain(v, d4)
                    for b in range(BLOCKS):
                        v.wait_ge(c_turned, b + 1)
                        cols = slice(b * BROWS, (b + 1) * BROWS)
                        for c in range(4):
                            chain(v.tensor_copy(CT[c][:, cols], bank[b % 2][:, c * BROWS:(c + 1) * BROWS]))
                        chain(v.tensor_copy(zT[:, cols], bank[2 + b % 2][0:H, 0:BROWS]))
                        chain(v.tensor_copy(mT[:, cols], bank[2 + b % 2][0:H, 256:256 + BROWS]))
                        v.sem_inc(c_taken, 1)
                    chain(v.memset(same[:, 0:1], 0.0))
                    chain(v.tensor_tensor(out=same[:, 1:TILES], in0=first_dst[0:H, 1:TILES],
                                          in1=first_dst[0:H, 0:TILES - 1], op=ALU.is_equal))
                    chain(v.tensor_scalar(out=penal[:, :], in0=same[:, :], scalar1=-1.0, scalar2=BIG, op0=ALU.add,
                                          op1=ALU.mult))
                    chain(v.tensor_tensor_scan(out=mrun[:, :], data0=penal[:, :], data1=mT[:, :], initial=-BIG,
                                               op0=ALU.add, op1=ALU.max))
                    chain(v.memset(keep[:, 0:1], 0.0))
                    chain(v.tensor_tensor(out=keep[:, 1:TILES], in0=mrun[:, 0:TILES - 1], in1=mrun[:, 1:TILES],
                                          op=ALU.subtract))
                    v.tensor_scalar(out=keep[:, :], in0=keep[:, :], scalar1=0.0, scalar2=None,
                                    op0=ALU.min).then_inc(diff_ready, 1)
                    v.tensor_tensor(out=take[:, :], in0=mT[:, :], in1=mrun[:, :], op=ALU.subtract).then_inc(diff_ready, 1)
                    v.wait_ge(exp_ready, 2)
                    v.tensor_tensor(out=keep[:, :], in0=keep[:, :], in1=same[:, :], op=ALU.mult).then_inc(exp_ready, 1)
                    v.wait_ge(exp_ready, 3)
                    chain(v.tensor_tensor(out=zT[:, :], in0=zT[:, :], in1=take[:, :], op=ALU.mult))
                    for c in range(4):
                        v.wait_ge(spread4, c + 1)
                        for i in range(2):
                            cols = slice(i * half, (i + 1) * half)
                            chain(v.tensor_tensor(out=CT[c][:, cols], in0=CT[c][:, cols], in1=bank[6 + i][:, 0:half],
                                                  op=ALU.mult))
                        chain(v.tensor_tensor_scan(out=CT[c][:, 0:half], data0=bank[4][:, 0:half], data1=CT[c][:, 0:half],
                                                   initial=0.0, op0=ALU.mult, op1=ALU.add))
                        v.tensor_tensor_scan(out=CT[c][:, half:TILES], data0=bank[5][:, 0:half],
                                             data1=CT[c][:, half:TILES], initial=CT[c][:, half - 1:half],
                                             op0=ALU.mult, op1=ALU.add).then_inc(run_ready, 1)
                    v.tensor_tensor_scan(out=zrun[:, :], data0=keep[:, :], data1=zT[:, :], initial=0.0,
                                         op0=ALU.mult, op1=ALU.add).then_inc(run_ready, 1)
                    for b in range(BLOCKS):
                        v.wait_ge(back, b + 1)
                        chain(v.tensor_copy(orow[:, b, 0:DM], bank[b % 2][0:BROWS, :]))
                        v.tensor_copy(orow[:, b, DM:W], bank[2 + b % 2][0:BROWS, 0:2 * H]).then_inc(back_taken, 1)

        with ExitStack() as st:
            wo_sb = sb("wo_sb", [P, 4, DM], f32, st)
            w1_sb = sb("w1_sb", [P, 4, DFF], f32, st)
            w2_sb = sb("w2_sb", [P, 2, DM], f32, st)
            b1_sb = sb("b1_sb", [P, 2], f32, st)
            vec = {n: sb(f"{n}_sb", [P, DM], f32, st) for n in ("g1", "h1", "g2", "h2", "b2")}
            half_neg = sb("half_neg", [P, 1], f32, st)
            pair = lambda name, shape, dt=f32: [sb(f"{name}{i}", shape, dt, st) for i in range(2)]
            rows5 = pair("rows5_", [P, 3], i32)
            pa, pb = pair("pa", [P, W]), pair("pb", [P, W])
            x5 = [sb(f"x5_{i}", [P, DM], f32, st) for i in range(4)]
            top_m = pair("top_m", [P, H])
            diff = pair("diff", [P, 2, H])
            wgt = pair("wgt", [P, 2, H])
            zz = pair("zz", [P, 2, H])
            attn = pair("attn", [P, DM])
            aT = pair("aT", [P, 4, P])
            x1, x1b, x1T = pair("x1", [P, DM]), pair("x1b", [P, DM]), pair("x1T", [P, 4, P])
            hT = pair("hT", [P, 2, P])
            y = pair("y", [P, DM])
            o_sb = pair("o_sb", [P, DM])
            st6, mv, rstd = pair("st6", [P, 6]), pair("mv", [P, 2]), pair("rstd", [P, 1])
            st6b, mvb, rstdb = pair("st6b", [P, 6]), pair("mvb", [P, 2]), pair("rstdb", [P, 1])
            w5_in = sem("w5_in")
            rows5_ready = sem("rows5_ready")
            go5 = sem("go5")
            a_in = [sem(f"a_in{i}") for i in range(2)]
            b_in = [sem(f"b_in{i}") for i in range(2)]
            more_in = [sem(f"more_in{i}") for i in range(2)]
            x5_in = [sem(f"x5_in{i}") for i in range(4)]
            diff5 = sem("diff5")
            exp5 = sem("exp5")
            attn_ready = sem("attn_ready")
            a_turned, aT_ready = sem("a_turned"), sem("aT_ready")
            o_done = sem("o_done")
            ln_in = [sem(f"ln_in{i}") for i in range(3)]
            ln_pow = [sem(f"ln_pow{i}") for i in range(3)]
            ln_add = [sem(f"ln_add{i}") for i in range(3)]
            scaled1, x1_ready = sem("scaled1"), sem("x1_ready")
            x1b_ready = sem("x1b_ready")
            x1_turned, x1T_ready = sem("x1_turned"), sem("x1T_ready")
            h_done, hT_ready = sem("h_done"), sem("hT_ready")
            f_done = sem("f_done")
            scaled2, y_ready = sem("scaled2"), sem("y_ready")
            o_ready = sem("o_ready")
            o_stored = [sem(f"o_stored{i}") for i in range(2)]
            pconst = sem("pconst")
            g5 = sem("g5")
            d5 = sem("d5")
            d5_turn = sem("d5_turn")

            STEPS = NT + 2

            def loop5(eng, one, chain=None, per=0):
                for s in range(4):
                    one(s, s % 4)
                before = chain.n if chain else 0
                with eng.Fori(4, 45, 4) as s:
                    for k in range(4):
                        if chain:
                            chain.base, chain.n = (s + k - 4) * per + before, 0
                        one(s + k, k)
                        assert not chain or chain.n == per, chain.n
                if chain:
                    chain.base, chain.n = 0, before + 44 * per
                for s in range(48, STEPS):
                    one(s, s % 4)

            def on(t):
                return not isinstance(t, int) or 0 <= t < NT

            def rows_of(t):
                return slice(LAST_START, N) if isinstance(t, int) and t == NT - 1 else ds(t * P, P)

            def seen(t, k):
                return (t - k % 2) * 8 + 16

            with nc.Block() as block:
                @block.sync
                def _(sp):
                    sp.dma_start(wo_sb[:, :, :], Wo.rearrange("(c p) n -> p c n", p=P)).then_inc(w5_in, 16)
                    sp.dma_start(w1_sb[:, :, :], W1.rearrange("(c p) n -> p c n", p=P)).then_inc(w5_in, 16)
                    sp.dma_start(w2_sb[:, :, :], W2.rearrange("(c p) n -> p c n", p=P)).then_inc(w5_in, 16)
                    with nc.allow_non_contiguous_dma(reason="256 biases, once"):
                        sp.dma_start(b1_sb[:, :], b1.rearrange("(c p) -> p c", p=P)).then_inc(w5_in, 16)
                    for n, a in (("g1", ln1_g), ("h1", ln1_b), ("g2", ln2_g), ("h2", ln2_b), ("b2", b2)):
                        sp.dma_start(vec[n][:, :], a.unsqueeze(0).to_broadcast([P, DM])).then_inc(w5_in, 16)

                    def step(s, k):
                        if on(s):
                            if not isinstance(s, int) or s >= 4:
                                sp.wait_ge(o_ready, s - 3)
                            uses4 = (s // 4 + 1) * 16 if isinstance(s, int) else None
                            sp.dma_start(x5[k][:, :], x[rows_of(s), :]).then_inc(x5_in[k], 16)
                        if on(s - 2):
                            if isinstance(s, int) and s - 2 == NT - 1:
                                sp.wait_ge(o_stored[1], 8 * (NT - 1))
                            sp.wait_ge(o_ready, s - 1)
                            sp.dma_start(out[rows_of(s - 2), :], o_sb[k % 2][:, :]).then_inc(o_stored[k % 2], 16)

                    loop5(sp, step)
                    sp.wait_ge(o_stored[0], 16 * (NT // 2 + 1))

                @block.gpsimd
                def _(g):
                    g.memset(half_neg[:, :], -0.5).then_inc(pconst, 1)
                    g.wait_ge(pconst, 1)
                    topa, topb, topm = g.to_reg(NULL_A), g.to_reg(NULL_B), g.to_reg(NULL_MORE - 1)
                    most = g.value_load(most_runs[P - 1:P, 0:1])
                    g.wait_ge(w5_in, 9 * 16)
                    chain = Chain(g, g5)

                    def fetch(t, k):
                        q = k % 2
                        if not isinstance(t, int) or t >= 2:
                            g.wait_ge(attn_ready, t - 1)
                            g.sem_inc(go5, 1)
                        chain(g.tensor_copy(rows5[q][:, :], node_rows[:, ds(t, 1), :].rearrange("p a b -> p (a b)")))
                        g.sem_inc(go5, 1)
                        g.indirect_dma_start(out=pa[q][:, :], out_offset=None, in_=parts[:, :],
                                             in_offset=bass.IndirectOffsetOnAxis(ap=rows5[q][:, 0:1], axis=0),
                                             bounds_check=topa, oob_is_err=False).then_inc(a_in[q], 16)
                        with g.If(most >= FEW):
                            g.wait_ge(a_in[q], seen(t, k))
                            g.sem_inc(go5, 1)
                            g.indirect_dma_start(out=pa[q][:, :], out_offset=None, in_=more_parts[:, :],
                                                 in_offset=bass.IndirectOffsetOnAxis(ap=rows5[q][:, 2:3], axis=0),
                                                 bounds_check=topm, oob_is_err=False).then_inc(more_in[q], 16)
                        with g.Else():
                            g.sem_inc(more_in[q], 16)
                        g.indirect_dma_start(out=pb[q][:, :], out_offset=None, in_=firsts[:, :],
                                             in_offset=bass.IndirectOffsetOnAxis(ap=rows5[q][:, 1:2], axis=0),
                                             bounds_check=topb, oob_is_err=False).then_inc(b_in[q], 16)

                    def inverse_root(i, t, m, r):
                        g.wait_ge(ln_add[i], t + 1)
                        g.tensor_tensor(out=r[:, :], in0=m[:, 1:2], in1=half_neg[:, :], op=ALU.pow).then_inc(ln_pow[i], 1)

                    def gain(t, a, g_, b_, scaled, ready):
                        g.wait_ge(scaled, t + 1)
                        chain(g.tensor_tensor(out=a[:, :], in0=a[:, :], in1=g_[:, :], op=ALU.mult))
                        g.tensor_tensor(out=a[:, :], in0=a[:, :], in1=b_[:, :], op=ALU.add).then_inc(ready, 1)

                    def step(s, k):
                        if on(s):
                            fetch(s, k)
                        if on(s - 1):
                            q = (k - 1) % 2
                            inverse_root(0, s - 1, mv[q], rstd[q])
                            gain(s - 1, x1[q], vec["g1"], vec["h1"], scaled1, x1_ready)
                            g.wait_ge(x1_ready, s)
                            g.tensor_tensor(out=x1b[q][:, :], in0=x1[q][:, :], in1=vec["b2"][:, :],
                                            op=ALU.add).then_inc(x1b_ready, 1)
                        if on(s - 2):
                            q = k % 2
                            inverse_root(1, s - 2, mvb[q], rstdb[q])
                            gain(s - 2, y[q], vec["g2"], vec["h2"], scaled2, y_ready)
                            inverse_root(2, s - 2, mvb[q], rstdb[q])

                    loop5(g, step, chain, 3)

                @block.tensor
                def _(pe):
                    pe.wait_ge(w5_in, 9 * 16)

                    def step(s, k):
                        if on(s - 1):
                            t, q = s - 1, (k - 1) % 2
                            pe.wait_ge(attn_ready, t + 1)
                            if not isinstance(t, int) or t >= 1:
                                pe.wait_ge(aT_ready, t)
                            for c in range(4):
                                last = pe.transpose(bank[0][:, c * P:(c + 1) * P], attn[q][:, c * P:(c + 1) * P], ident[:, :])
                            last.then_inc(a_turned, 1)
                        if on(s - 2):
                            t, q = s - 2, k % 2
                            pe.wait_ge(x1_ready, t + 1)
                            if not isinstance(t, int) or t >= 1:
                                pe.wait_ge(x1T_ready, t)
                            for c in range(4):
                                last = pe.transpose(bank[1][:, c * P:(c + 1) * P], x1[q][:, c * P:(c + 1) * P], ident[:, :])
                            last.then_inc(x1_turned, 1)
                        if on(s - 1):
                            t, q = s - 1, (k - 1) % 2
                            pe.wait_ge(aT_ready, t + 1)
                            if not isinstance(t, int) or t >= 2:
                                pe.wait_ge(ln_in[0], t - 1)
                            for c in range(4):
                                last = pe.matmul(bank[2 + q][:, :], aT[q][:, c, :], wo_sb[:, c, :], start=c == 0, stop=c == 3)
                            last.then_inc(o_done, 1)
                        if on(s - 2):
                            t, q = s - 2, k % 2
                            pe.wait_ge(x1T_ready, t + 1)
                            if not isinstance(t, int) or t >= 1:
                                pe.wait_ge(hT_ready, 2 * t)
                            for f in range(2):
                                for c in range(4):
                                    last = pe.matmul(bank[4][:, f * P:(f + 1) * P], w1_sb[:, c, f * P:(f + 1) * P],
                                                     x1T[q][:, c, :], start=c == 0, stop=c == 3)
                            last.then_inc(h_done, 1)
                            pe.wait_ge(hT_ready, 2 * t + 2)
                            if not isinstance(t, int) or t >= 1:
                                pe.wait_ge(ln_in[1], t)
                            for f in range(2):
                                last = pe.matmul(bank[5][:, :], hT[q][:, f, :], w2_sb[:, f, :], start=f == 0, stop=f == 1)
                            last.then_inc(f_done, 1)

                    loop5(pe, step)

                @block.scalar
                def _(act):
                    act.wait_ge(w5_in, 9 * 16)

                    def step(s, k):
                        if on(s - 1):
                            t, q = s - 1, (k - 1) % 2
                            act.wait_ge(a_turned, t + 1)
                            if not isinstance(t, int) or t >= 2:
                                act.wait_ge(o_done, t - 1)
                            act.activation(aT[q][:, :, :], bank[0][:, :].rearrange("p (c n) -> p c n", c=4),
                                           ACT.Copy).then_inc(aT_ready, 1)
                        if on(s - 2):
                            t, q = s - 2, k % 2
                            act.wait_ge(x1_turned, t + 1)
                            if not isinstance(t, int) or t >= 2:
                                act.wait_ge(h_done, t - 1)
                            act.activation(x1T[q][:, :, :], bank[1][:, :].rearrange("p (c n) -> p c n", c=4),
                                           ACT.Copy).then_inc(x1T_ready, 1)
                            act.wait_ge(h_done, t + 1)
                            if not isinstance(t, int) or t >= 2:
                                act.wait_ge(f_done, t - 1)
                            for f in range(2):
                                act.activation(hT[q][:, f, :], bank[4][:, f * P:(f + 1) * P], ACT.Relu,
                                               bias=b1_sb[:, f:f + 1]).then_inc(hT_ready, 1)
                        if on(s):
                            q = k % 2
                            act.wait_ge(diff5, s + 1)
                            if not isinstance(s, int) or s >= 2:
                                act.wait_ge(attn_ready, s - 1)
                            act.activation(wgt[q][:, :, :], diff[q][:, :, :], ACT.Exp).then_inc(exp5, 1)

                    loop5(act, step)

                @block.vector
                def _(v):
                    chain = Chain(v, d5)

                    def norm(i, t, a, o, s6, m, r, done):
                        chain(v.bn_stats(out=s6[:, :], in_=a[:, :]))
                        v.sem_inc(d5_turn, 1)
                        chain(v.bn_aggr(out=m[:, :], in_=s6[:, :]))
                        v.tensor_scalar(out=m[:, 1:2], in0=m[:, 1:2], scalar1=EPS, scalar2=None,
                                        op0=ALU.add).then_inc(ln_add[i], 1)
                        v.wait_ge(ln_pow[i], t + 1)
                        v.tensor_scalar(out=o[:, :], in0=a[:, :], scalar1=m[:, 0:1], scalar2=r[:, 0:1],
                                        op0=ALU.subtract, op1=ALU.mult).then_inc(done, 1)

                    def merge(t, k):
                        q = k % 2
                        heads = lambda a: a.rearrange("p (h d) -> p h d", h=H)
                        wide = lambda a: a.unsqueeze(2).to_broadcast([P, H, DK])
                        v.wait_ge(a_in[q], seen(t, k))
                        v.wait_ge(more_in[q], seen(t, k))
                        v.wait_ge(b_in[q], seen(t, k))
                        chain(v.tensor_tensor(out=top_m[q][:, :], in0=pa[q][:, DM + H:W], in1=pb[q][:, DM + H:W], op=ALU.max))
                        chain(v.tensor_tensor(out=diff[q][:, 0, :], in0=pa[q][:, DM + H:W], in1=top_m[q][:, :],
                                              op=ALU.subtract))
                        v.tensor_tensor(out=diff[q][:, 1, :], in0=pb[q][:, DM + H:W], in1=top_m[q][:, :],
                                        op=ALU.subtract).then_inc(diff5, 1)
                        v.wait_ge(exp5, t + 1)
                        chain(v.tensor_tensor(out=zz[q][:, 0, :], in0=pa[q][:, DM:DM + H], in1=wgt[q][:, 0, :], op=ALU.mult))
                        chain(v.tensor_tensor(out=zz[q][:, 1, :], in0=pb[q][:, DM:DM + H], in1=wgt[q][:, 1, :], op=ALU.mult))
                        chain(v.tensor_tensor(out=zz[q][:, 0, :], in0=zz[q][:, 0, :], in1=zz[q][:, 1, :], op=ALU.add))
                        chain(v.tensor_scalar(out=zz[q][:, 0, :], in0=zz[q][:, 0, :], scalar1=1e-30, scalar2=None, op0=ALU.max))
                        chain(v.reciprocal(zz[q][:, 1, :], zz[q][:, 0, :]))
                        chain(v.tensor_tensor(out=wgt[q][:, :, :], in0=wgt[q][:, :, :],
                                              in1=zz[q][:, 1:2, :].to_broadcast([P, 2, H]), op=ALU.mult))
                        chain(v.tensor_tensor(out=heads(pa[q][:, 0:DM]), in0=heads(pa[q][:, 0:DM]),
                                              in1=wide(wgt[q][:, 0, :]), op=ALU.mult))
                        chain(v.tensor_tensor(out=heads(pb[q][:, 0:DM]), in0=heads(pb[q][:, 0:DM]),
                                              in1=wide(wgt[q][:, 1, :]), op=ALU.mult))
                        if not isinstance(t, int) or t >= 2:
                            v.wait_ge(a_turned, t - 1)
                        v.tensor_tensor(out=attn[q][:, :], in0=pa[q][:, 0:DM], in1=pb[q][:, 0:DM],
                                        op=ALU.add).then_inc(attn_ready, 1)

                    def step(s, k):
                        if on(s):
                            merge(s, k)
                        if on(s - 1):
                            t, q, r = s - 1, (k - 1) % 2, (k - 1) % 4
                            v.wait_ge(o_done, t + 1)
                            x_uses = (t // 4 + 1) * 16 if isinstance(t, int) else (t - r) * 4 + 16
                            v.wait_ge(x5_in[r], x_uses)
                            if not isinstance(t, int) or t >= 2:
                                v.wait_ge(x1_turned, t - 1)
                                v.wait_ge(ln_in[1], t - 1)
                            v.tensor_tensor(out=x1[q][:, :], in0=x5[r][:, :], in1=bank[2 + q][:, :], op=ALU.add).then_inc(ln_in[0], 1)
                            v.wait_ge(ln_in[0], t + 1)
                            norm(0, t, x1[q], x1[q], st6[q], mv[q], rstd[q], scaled1)
                        if on(s - 2):
                            t, q, r = s - 2, k % 2, (k - 2) % 4
                            v.wait_ge(f_done, t + 1)
                            v.wait_ge(x1b_ready, t + 1)
                            v.tensor_tensor(out=y[q][:, :], in0=x1b[q][:, :], in1=bank[5][:, :], op=ALU.add).then_inc(ln_in[1], 1)
                            v.wait_ge(ln_in[1], t + 1)
                            norm(1, t, y[q], y[q], st6b[q], mvb[q], rstdb[q], scaled2)
                            v.wait_ge(y_ready, t + 1)
                            v.tensor_tensor(out=y[q][:, :], in0=y[q][:, :], in1=x5[r][:, :], op=ALU.add).then_inc(ln_in[2], 1)
                            v.wait_ge(ln_in[2], t + 1)
                            if not isinstance(t, int) or t >= 2:
                                v.wait_ge(o_stored[q], seen(t, q) - 16)
                            norm(2, t, y[q], o_sb[q], st6b[q], mvb[q], rstdb[q], o_ready)

                    loop5(v, step, chain, 10 + 2 + 4)


_INS = ['x', 'src', 'dst', 'L0_gnn_Wq', 'L0_gnn_Wk', 'L0_gnn_Wv', 'L0_gnn_Wo', 'L0_gnn_ln1_g', 'L0_gnn_ln1_b',
        'L0_gnn_ln2_g', 'L0_gnn_ln2_b', 'L0_gnn_W1', 'L0_gnn_b1', 'L0_gnn_W2', 'L0_gnn_b2']
_OUTS = [((6250, 512), 'float32')]


def kernel(**inputs):
    import numpy as _np
    import concourse.bacc as _bacc
    from concourse import mybir as _mybir
    from concourse.bass_utils import run_bass_kernel_spmd as _run

    nc = _bacc.Bacc("TRN2", target_bir_lowering=False, num_devices=1)
    arrays, args = {}, []
    for name in _INS:
        a = _np.ascontiguousarray(inputs[name])
        arrays[f"in_{name}_dram"] = a
        args.append(nc.dram_tensor(f"in_{name}_dram", a.shape, _mybir.dt.from_np(a.dtype), kind="ExternalInput").ap())
    for i, (shape, dtype) in enumerate(_OUTS):
        dt = _mybir.dt.from_np(_np.dtype(dtype))
        args.append(nc.dram_tensor(f"out_{i}_dram", shape, dt, kind="ExternalOutput").ap())
    build(nc, *args)
    r = _run(nc, [arrays], core_ids=[0])
    return r.results[0]["out_0_dram"]
```

```python
import concourse.bass as bass
from concourse import mybir
from contextlib import ExitStack

N, E, DM, H, DFF = 6250, 106250, 512, 8, 256
DK = DM // H
P = 128

GT = 8
NSLOT = 3
GROUPS = 105
TILES = GROUPS * GT
BLOCKS, BROWS = 7, 120
FULL_ROWS = E // P
TAIL = E % P
LAST_ROWS = FULL_ROWS - (BLOCKS - 1) * BROWS
NT = (N + P - 1) // P
LAST_START = N - P
W = DM + 2 * H
FEW = P // GT
MORE = P - FEW
NULL_A = TILES * FEW
NULL_MORE = TILES * MORE
NULL_B = TILES
BIG = 1.0e30
FAR = 1.0e6
EPS = 1e-5
assert TILES * P >= E and GROUPS % NSLOT == 0 and BLOCKS * BROWS == TILES


class Chain:

    def __init__(self, eng, sem):
        self.eng, self.sem, self.base, self.n = eng, sem, 0, 0

    def __call__(self, ins):
        ins.then_inc(self.sem, 1)
        self.n += 1
        self.eng.wait_ge(self.sem, self.base + self.n)


def build(nc, x, src, dst, Wq, Wk, Wv, Wo, ln1_g, ln1_b, ln2_g, ln2_b, W1, b1, W2, b2, out):
    f32, i32, f32r, bf16 = mybir.dt.float32, mybir.dt.int32, mybir.dt.float32r, mybir.dt.bfloat16
    ALU, ACT, AX = mybir.AluOpType, mybir.ActivationFunctionType, mybir.AxisListType
    ds = bass.ds

    with ExitStack() as ctx:
        def sb(name, shape, dt=f32, scope=ctx):
            return scope.enter_context(nc.sbuf_tensor(name, shape, dt))

        in_use = []

        def sem(name):
            in_use.append(nc.alloc_semaphore(name=name))
            return in_use[-1]

        def end_of_stage():
            nc.clear_and_free_semaphores(list(in_use))
            in_use.clear()
            nc.all_engine_barrier()

        def dram(name, shape, dt=f32):
            return nc.dram_tensor(name, shape, dt).ap()

        q_rows = dram("q_rows", [N, 2 * DM])
        kv_rows = dram("kv_rows", [N, 2 * DM])
        breaks_rows = dram("breaks_rows", [TILES * H, 132])
        starts_rows = dram("starts_rows", [TILES, P])
        key_rows = dram("key_rows", [TILES, P], bf16)
        run_rows = dram("run_rows", [TILES, FEW])
        parts = dram("parts", [TILES * FEW + 1, W])
        more_parts = dram("more_parts", [TILES * MORE, W])
        firsts = dram("firsts", [TILES + 1, W])

        bank = [ctx.enter_context(nc.psum_tensor(f"bank{i}", [P, 512], f32)) for i in range(8)]
        ident = sb("ident", [P, P])
        ones_row = sb("ones_row", [1, P])
        ones_b = sb("ones_b", [1, P], bf16)
        iota_row = sb("iota_row", [P, P])
        edge_nodes = sb("edge_nodes", [P, TILES, 2], i32)
        edge_runs = sb("edge_runs", [P, TILES, 2])
        run_nodes = sb("run_nodes", [P, GROUPS], i32)
        group_runs = sb("group_runs", [P, GT])
        minus_p = sb("minus_p", [P, 1])
        last_run = sb("last_run", [P, TILES], i32)
        first_dst = sb("first_dst", [P, TILES])
        node_id = sb("node_id", [P, NT])
        node_rows = sb("node_rows", [P, NT, 3], i32)
        most_runs = sb("most_runs", [P, 1], i32)

        with ExitStack() as st:
            dst_i = sb("dst_i", [BROWS, BLOCKS, P], i32, st)
            src_i = sb("src_i", [BROWS, BLOCKS, P], i32, st)
            dst_f = sb("dst_f", [BROWS, BLOCKS, P], f32, st)
            src_f = sb("src_f", [BROWS, BLOCKS, P], f32, st)
            begins = sb("begins", [BROWS, BLOCKS, 132], f32, st)
            breaks = sb("breaks", [BROWS, BLOCKS, 132], f32, st)
            runs = sb("runs", [BROWS, BLOCKS, P], f32, st)
            keys = sb("keys", [BROWS, BLOCKS, P], f32, st)
            keys_b = sb("keys_b", [BROWS, BLOCKS, P], bf16, st)
            begin_dst = sb("begin_dst", [BROWS, BLOCKS, P], f32, st)
            hit = sb("hit", [BROWS, BLOCKS, P], f32, st)
            run_dst = sb("run_dst", [BROWS, BLOCKS, FEW], f32, st)
            run_id = sb("run_id", [BROWS, FEW], f32, st)
            missing = sb("missing", [BROWS, BLOCKS, FEW], f32, st)
            run_turn = sb("run_turn", [GROUPS, P], f32, st)
            row_i = sb("row_i", [BROWS, 1], i32, st)
            row_key = sb("row_key", [BROWS, 1], f32, st)
            most_f = sb("most_f", [P, 1], f32, st)
            last_f = sb("last_f", [P, GROUPS, GT], f32, st)
            starts = sb("starts", [BROWS, BLOCKS, P], f32, st)
            ones = sb("ones", [BROWS, P], f32, st)
            first_row = sb("first_row", [1, TILES], f32, st)
            null_row = sb("null_row", [1, W], f32, st)
            padded = sem("padded")
            edges_in = sem("edges_in")
            consts = sem("consts")
            tabled = sem("tabled")
            rows_ready = sem("rows_ready")
            turned = sem("turned")
            turned_used = sem("turned_used")
            first_ready = sem("first_ready")
            spread = sem("spread")
            d1 = sem("d1")
            runs_stored = sem("runs_stored")
            runs_back = sem("runs_back")
            runs_turned = sem("runs_turned")
            with nc.Block() as block:
                @block.sync
                def _(sp):
                    sp.wait_ge(padded, 2)
                    for dram_list, rows in ((src, src_i), (dst, dst_i)):
                        whole = (BLOCKS - 1) * BROWS * P
                        sp.dma_start(rows[:, 0:BLOCKS - 1, :], dram_list[0:whole].rearrange(
                            "(b p j) -> p b j", p=BROWS, j=P)).then_inc(edges_in, 16)
                        sp.dma_start(rows[0:LAST_ROWS, BLOCKS - 1, :], dram_list[whole:FULL_ROWS * P].rearrange(
                            "(p j) -> p j", j=P)).then_inc(edges_in, 16)
                        sp.dma_start(rows[LAST_ROWS:LAST_ROWS + 1, BLOCKS - 1, 0:TAIL],
                                     dram_list[FULL_ROWS * P:E].rearrange("(p j) -> p j", p=1)).then_inc(edges_in, 16)
                    sp.wait_ge(rows_ready, 5)
                    sp.dma_start(run_rows.rearrange("(b p) f -> p b f", p=BROWS), run_dst[:, :, :]).then_inc(runs_stored, 16)
                    sp.wait_ge(runs_stored, 16)
                    sp.dma_start(run_turn[:, :], run_rows.rearrange("(g t) f -> g (t f)", t=GT)).then_inc(runs_back, 16)
                    sp.dma_start(key_rows.rearrange("(b p) f -> p b f", p=BROWS), keys_b[:, :, :]).then_inc(tabled, 16)
                    by_head = breaks_rows.rearrange("(b p h) f -> h p b f", p=BROWS, h=H)
                    for h in range(H):
                        sp.dma_start(by_head[h], breaks[:, :, :]).then_inc(tabled, 16)
                    sp.dma_start(starts_rows.rearrange("(b p) f -> p b f", p=BROWS), starts[:, :, :]).then_inc(tabled, 16)
                    sp.dma_start(parts[NULL_A:NULL_A + 1, :], null_row[:, :]).then_inc(tabled, 16)
                    sp.dma_start(firsts[NULL_B:NULL_B + 1, :], null_row[:, :]).then_inc(tabled, 16)
                    sp.wait_ge(tabled, 12 * 16)

                @block.gpsimd
                def _(g):
                    chain = Chain(g, consts)
                    chain(g.memset(ident[:, :], 0.0))
                    chain(g.affine_select(out=ident[:, :], in_=ident[:, :], compare_op=ALU.not_equal, fill=1.0,
                                          base=0, pattern=[[-1, P]], channel_multiplier=1))
                    chain(g.memset(ones_row[:, :], 1.0))
                    chain(g.memset(ones_b[:, :], 1.0))
                    chain(g.iota(iota_row[:, :], pattern=[[1, P]], base=0, channel_multiplier=0,
                                 allow_small_or_imprecise_dtypes=True))
                    chain(g.iota(node_id[:, 0:NT - 1], pattern=[[P, NT - 1]], base=0, channel_multiplier=1,
                                 allow_small_or_imprecise_dtypes=True))
                    chain(g.iota(node_id[:, NT - 1:NT], pattern=[[0, 1]], base=LAST_START, channel_multiplier=1,
                                 allow_small_or_imprecise_dtypes=True))
                    chain(g.iota(row_i[:, :], pattern=[[0, 1]], base=0, channel_multiplier=1))
                    chain(g.iota(run_id[:, :], pattern=[[1, FEW]], base=0, channel_multiplier=0,
                                 allow_small_or_imprecise_dtypes=True))
                    chain(g.iota(group_runs[:, :], pattern=[[FEW, GT]], base=0, channel_multiplier=0,
                                 allow_small_or_imprecise_dtypes=True))
                    chain(g.iota(minus_p[:, :], pattern=[[0, 1]], base=0, channel_multiplier=-1,
                                 allow_small_or_imprecise_dtypes=True))

                @block.vector
                def _(v):
                    chain = Chain(v, d1)
                    v.memset(src_i[:, BLOCKS - 1, :], 0).then_inc(padded, 1)
                    v.memset(dst_i[:, BLOCKS - 1, :], N).then_inc(padded, 1)
                    chain(v.memset(null_row[:, :], 0.0))
                    v.memset(null_row[:, DM + H:W], -BIG).then_inc(rows_ready, 1)
                    chain(v.memset(ones[:, :], 1.0))
                    chain(v.memset(begins[:, :, :], 1.0))
                    v.wait_ge(edges_in, 96)
                    chain(v.tensor_copy(src_f[:, :, :], src_i[:, :, :]))
                    chain(v.tensor_copy(dst_f[:, :, :], dst_i[:, :, :]))
                    chain(v.tensor_tensor(out=begins[:, :, 1:P], in0=dst_f[:, :, 1:P], in1=dst_f[:, :, 0:P - 1],
                                          op=ALU.not_equal))
                    v.tensor_scalar(out=breaks[:, :, :], in0=begins[:, :, :], scalar1=-BIG, scalar2=None,
                                    op0=ALU.mult).then_inc(rows_ready, 1)
                    chain(v.tensor_scalar(out=starts[:, :, :], in0=begins[:, :, 0:P], scalar1=-FAR, scalar2=FAR,
                                          op0=ALU.mult, op1=ALU.add))
                    chain(v.tensor_tensor(out=starts[:, :, :], in0=starts[:, :, :], in1=dst_f[:, :, :], op=ALU.add))
                    v.memset(starts[:, :, 0:1], FAR).then_inc(rows_ready, 1)
                    for b in range(BLOCKS):
                        chain(v.tensor_tensor_scan(out=runs[:, b, :], data0=ones[:, :], data1=begins[:, b, 0:P],
                                                   initial=-1.0, op0=ALU.mult, op1=ALU.add))
                    v.wait_ge(consts, 11)
                    chain(v.tensor_scalar(out=row_i[:, :], in0=row_i[:, :], scalar1=GT - 1, scalar2=None,
                                          op0=ALU.bitwise_and))
                    chain(v.tensor_copy(row_key[:, :], row_i[:, :]))
                    chain(v.tensor_scalar(out=row_key[:, :], in0=row_key[:, :], scalar1=float(FEW), scalar2=None,
                                          op0=ALU.mult))
                    chain(v.tensor_scalar(out=keys[:, :, :], in0=runs[:, :, :], scalar1=row_key[:, 0:1], scalar2=None,
                                          op0=ALU.add))
                    v.tensor_copy(keys_b[:, :, :], keys[:, :, :]).then_inc(rows_ready, 1)
                    chain(v.tensor_tensor(out=begin_dst[:, :, :], in0=begins[:, :, 0:P], in1=dst_f[:, :, :], op=ALU.mult))
                    for r in range(FEW):
                        chain(v.scalar_tensor_tensor(out=hit[:, :, :], in0=runs[:, :, :], scalar=float(r),
                                                     in1=begin_dst[:, :, :], op0=ALU.is_equal, op1=ALU.mult))
                        chain(v.tensor_reduce(out=run_dst[:, :, r], in_=hit[:, :, :], axis=AX.X, op=ALU.add))
                    for b in range(BLOCKS):
                        chain(v.tensor_scalar(out=missing[:, b, :], in0=run_id[:, :], scalar1=runs[:, b, P - 1:P],
                                              scalar2=FAR, op0=ALU.is_gt, op1=ALU.mult))
                    v.tensor_tensor(out=run_dst[:, :, :], in0=run_dst[:, :, :], in1=missing[:, :, :],
                                    op=ALU.add).then_inc(rows_ready, 1)
                    for b in range(BLOCKS):
                        v.wait_ge(turned, b + 1)
                        t = bank[b % 2][:, 0:4 * BROWS].rearrange("p (a t) -> p a t", a=4)
                        cols = slice(b * BROWS, (b + 1) * BROWS)
                        chain(v.tensor_copy(edge_nodes[:, cols, 0], t[:, 0, :]))
                        chain(v.tensor_scalar(out=edge_nodes[:, cols, 1], in0=t[:, 1, :], scalar1=float(N - 1),
                                              scalar2=None, op0=ALU.min))
                        chain(v.tensor_copy(edge_runs[:, cols, 0], t[:, 2, :]))
                        chain(v.tensor_copy(edge_runs[:, cols, 1], t[:, 3, :]))
                        v.tensor_copy(first_row[:, cols], t[0:1, 1, :]).then_inc(turned_used, 1)
                    v.wait_ge(spread, 1)
                    half = TILES // 2
                    chain(v.tensor_copy(first_dst[:, 0:half], bank[2][:, 0:half]))
                    chain(v.tensor_copy(first_dst[:, half:TILES], bank[3][:, 0:half]))
                    chain(v.tensor_tensor(out=last_f[96:P, :, :],
                                          in0=edge_runs[96:P, :, 0].rearrange("p (g t) -> p g t", t=GT),
                                          in1=group_runs[96:P, :].unsqueeze(1).to_broadcast([32, GROUPS, GT]),
                                          op=ALU.subtract))
                    chain(v.tensor_copy(last_run[96:P, :], last_f[96:P, :, :].rearrange("p g t -> p (g t)")))
                    chain(v.tensor_reduce(out=most_f[96:P, :], in_=last_f[96:P, :, :], axis=AX.XY, op=ALU.max))
                    chain(v.tensor_copy(most_runs[96:P, :], most_f[96:P, :]))
                    v.wait_ge(runs_turned, 1)
                    chain(v.tensor_copy(run_nodes[:, :], bank[4][:, 0:GROUPS]))

                @block.tensor
                def _(pe):
                    pe.wait_ge(consts, 11)
                    pe.wait_ge(d1, 12 + BLOCKS)
                    for b in range(BLOCKS):
                        if b >= 2:
                            pe.wait_ge(turned_used, b - 1)
                        for a, rows in enumerate((src_f[:, b, :], dst_f[:, b, :], keys[:, b, :], begins[:, b, 0:P])):
                            last = pe.transpose(bank[b % 2][:, a * BROWS:(a + 1) * BROWS], rows, ident[0:BROWS, 0:BROWS])
                        last.then_inc(turned, 1)
                    pe.wait_ge(turned_used, BLOCKS)
                    half = TILES // 2
                    pe.matmul(bank[2][:, 0:half], ones_row[:, :], first_row[:, 0:half], start=True, stop=True)
                    pe.matmul(bank[3][:, 0:half], ones_row[:, :], first_row[:, half:TILES], start=True,
                              stop=True).then_inc(spread, 1)
                    pe.wait_ge(runs_back, 16)
                    pe.transpose(bank[4][:, 0:GROUPS], run_turn[:, :], ident[0:GROUPS, 0:GROUPS]).then_inc(runs_turned, 1)

        end_of_stage()

        with ExitStack() as st:
            w_sb = [sb(n, [P, 4, DM], f32, st) for n in ("wq_sb", "wk_sb", "wv_sb")]
            xt = [sb(f"xt{i}", [P, DM], f32, st) for i in range(2)]
            xT = [sb(f"xT{i}", [P, 4, P], f32, st) for i in range(2)]
            q_out = [sb(f"q_out{i}", [P, 2 * DM], f32r, st) for i in range(2)]
            kv_out = [sb(f"kv_out{i}", [P, 2 * DM], f32, st) for i in range(2)]
            below = sb("below", [P, TILES], f32, st)
            nid = [sb(f"nid{i}", [P, 1], f32, st) for i in range(2)]
            cnt = [sb(f"cnt{i}", [P, 2], f32, st) for i in range(2)]
            tile_i = [sb(f"tile_i{i}", [P, 1], i32, st) for i in range(2)]
            tile_f = [sb(f"tile_f{i}", [P, 1], f32, st) for i in range(2)]
            row_of = [sb(f"row_of{i}", [P, P], f32, st) for i in range(2)]
            counts = sb("counts", [P, NT, 4], f32, st)
            used = sb("used", [P, NT, 3], f32, st)
            over = sb("over", [P, NT], f32, st)
            row_f = sb("row_f", [P, NT, 3], f32, st)
            weights_in = sem("weights_in")
            x_in = [sem(f"x_in{i}") for i in range(2)]
            x_turned = sem("x_turned")
            xT_ready = sem("xT_ready")
            qkv_done = sem("qkv_done")
            q_ready = sem("q_ready")
            q_rest = sem("q_rest")
            k_ready = sem("k_ready")
            v_ready = sem("v_ready")
            q_stored = [sem(f"q_stored{i}") for i in range(2)]
            kv_stored = [sem(f"kv_stored{i}") for i in range(2)]
            tile_ready = sem("tile_ready")
            go = sem("go")
            row_in = [sem(f"row_in{i}") for i in range(2)]
            d2 = sem("d2")

            def rows_at(t):
                return slice(LAST_START, N) if isinstance(t, int) and t == NT - 1 else ds(t * P, P)

            def steps(eng, one):
                one(0, 0)
                one(1, 1)
                with eng.Fori(2, NT - 2, 2) as t:
                    one(t, 0)
                    one(t + 1, 1)
                one(NT - 1, 0)

            def nth(t, par):
                return t - par + 2

            with nc.Block() as block:
                @block.sync
                def _(sp):
                    for w, s in zip((Wq, Wk, Wv), w_sb):
                        sp.dma_start(s[:, :, :], w.rearrange("(c p) n -> p c n", p=P)).then_inc(weights_in, 16)

                    def load(t, par):
                        if not isinstance(t, int) or t >= 2:
                            sp.wait_ge(x_turned, t - 1)
                        sp.dma_start(xt[par][:, :], x[rows_at(t), :]).then_inc(x_in[par], 16)

                    def store(t, par):
                        if isinstance(t, int) and t == NT - 1:
                            sp.wait_ge(q_stored[1], 8 * (NT - 1))
                            sp.wait_ge(kv_stored[1], 8 * (NT - 1))
                        sp.wait_ge(q_rest, t + 1)
                        sp.dma_start(q_rows[rows_at(t), :], q_out[par][:, :].bitcast(f32)).then_inc(q_stored[par], 16)
                        sp.wait_ge(k_ready, t + 1)
                        sp.wait_ge(v_ready, t + 1)
                        sp.dma_start(kv_rows[rows_at(t), :], kv_out[par][:, :]).then_inc(kv_stored[par], 16)

                    load(0, 0)
                    load(1, 1)
                    with sp.Fori(2, NT - 2, 2) as t:
                        load(t, 0)
                        store(t - 2, 0)
                        load(t + 1, 1)
                        store(t - 1, 1)
                    load(NT - 1, 0)
                    store(NT - 3, 0)
                    store(NT - 2, 1)
                    store(NT - 1, 0)
                    sp.wait_ge(q_stored[0], 16 * (NT // 2 + 1))
                    sp.wait_ge(kv_stored[0], 16 * (NT // 2 + 1))

                @block.tensor
                def _(pe):
                    pe.wait_ge(weights_in, 48)

                    def turn(t, par):
                        pe.wait_ge(x_in[par], 8 * nth(t, par))
                        if not isinstance(t, int) or t >= 2:
                            pe.wait_ge(xT_ready, t - 1)
                        for c in range(4):
                            last = pe.transpose(bank[par][:, c * P:(c + 1) * P], xt[par][:, c * P:(c + 1) * P], ident[:, :])
                        last.then_inc(x_turned, 1)

                    def project(t, par):
                        pe.wait_ge(xT_ready, t + 1)
                        if not isinstance(t, int) or t >= 2:
                            pe.wait_ge(q_rest, t - 1)
                            pe.wait_ge(k_ready, t - 1)
                            pe.wait_ge(v_ready, t - 1)
                        for m in range(3):
                            for c in range(4):
                                last = pe.matmul(bank[2 + 3 * par + m][:, :], xT[par][:, c, :], w_sb[m][:, c, :],
                                                 start=c == 0, stop=c == 3)
                            last.then_inc(qkv_done, 1)

                    turn(0, 0)
                    turn(1, 1)
                    project(0, 0)
                    with pe.Fori(2, NT - 2, 2) as t:
                        turn(t, 0)
                        project(t - 1, 1)
                        turn(t + 1, 1)
                        project(t, 0)
                    turn(NT - 1, 0)
                    project(NT - 2, 1)
                    project(NT - 1, 0)

                @block.scalar
                def _(act):
                    def evacuate(t, par):
                        late = not isinstance(t, int) or t >= 2
                        act.wait_ge(qkv_done, 3 * t + 1)
                        if late:
                            act.wait_ge(q_stored[par], 8 * nth(t, par) - 16)
                        act.activation(q_out[par][:, 0:DM], bank[2 + 3 * par][:, :], ACT.Copy,
                                       scale=1.0 / DK ** 0.5).then_inc(q_ready, 1)
                        act.wait_ge(qkv_done, 3 * t + 2)
                        if late:
                            act.wait_ge(kv_stored[par], 8 * nth(t, par) - 16)
                        act.activation(kv_out[par][:, 0:DM], bank[3 + 3 * par][:, :], ACT.Copy).then_inc(k_ready, 1)
                        act.wait_ge(qkv_done, 3 * t + 3)
                        act.activation(kv_out[par][:, DM:2 * DM], bank[4 + 3 * par][:, :], ACT.Copy).then_inc(v_ready, 1)

                    steps(act, evacuate)

                @block.vector
                def _(v):
                    chain = Chain(v, d2)

                    def copy_xT(t, par):
                        v.wait_ge(x_turned, t + 1)
                        if not isinstance(t, int) or t >= 2:
                            v.wait_ge(qkv_done, 3 * t - 3)
                        v.tensor_copy(xT[par][:, :, :], bank[par][:, :].rearrange("p (c n) -> p c n", c=4)).then_inc(xT_ready, 1)

                    def q_remainder(t, par):
                        v.wait_ge(q_ready, t + 1)
                        v.scalar_tensor_tensor(out=q_out[par][:, DM:2 * DM], in0=bank[2 + 3 * par][:, :],
                                               scalar=1.0 / DK ** 0.5, in1=q_out[par][:, 0:DM].bitcast(f32),
                                               op0=ALU.mult, op1=ALU.subtract).then_inc(q_rest, 1)

                    def count_tiles(t, par):
                        chain(v.tensor_copy(nid[par][:, :], node_id[:, ds(t, 1)]))
                        for a, op in ((0, ALU.is_lt), (1, ALU.is_le)):
                            chain(v.tensor_scalar(out=below[:, :], in0=first_dst[:, :], scalar1=nid[par][:, 0:1],
                                                  scalar2=None, op0=op))
                            chain(v.tensor_reduce(out=cnt[par][:, a:a + 1], in_=below[:, :], axis=AX.X, op=ALU.add))
                        chain(v.tensor_copy(counts[:, ds(t, 1), 0:2], cnt[par][:, :].unsqueeze(1)))
                        chain(v.tensor_scalar(out=tile_f[par][:, :], in0=cnt[par][:, 0:1], scalar1=-1.0, scalar2=0.0,
                                              op0=ALU.add, op1=ALU.max))
                        chain(v.tensor_copy(tile_i[par][:, :], tile_f[par][:, :]))
                        v.tensor_copy(tile_f[par][:, :], tile_f[par][:, :]).then_inc(tile_ready, 1)

                    def count_runs(t, par):
                        v.wait_ge(row_in[par], 8 * nth(t, par))
                        for a, op in ((0, ALU.is_lt), (1, ALU.is_le)):
                            chain(v.tensor_scalar(out=below[:, 0:P], in0=row_of[par][:, :], scalar1=nid[par][:, 0:1],
                                                  scalar2=None, op0=op))
                            chain(v.tensor_reduce(out=cnt[par][:, a:a + 1], in_=below[:, 0:P], axis=AX.X, op=ALU.add))
                        chain(v.tensor_copy(counts[:, ds(t, 1), 2:4], cnt[par][:, :].unsqueeze(1)))

                    COUNT = 8 + 5
                    copy_xT(0, 0)
                    count_tiles(0, 0)
                    copy_xT(1, 1)
                    q_remainder(0, 0)
                    count_tiles(1, 1)
                    count_runs(0, 0)
                    before = chain.n
                    with v.Fori(2, NT - 2, 2) as t:
                        for k in range(2):
                            chain.base, chain.n = (t + k - 2) * COUNT + before, 0
                            copy_xT(t + k, k)
                            q_remainder(t + k - 1, 1 - k)
                            count_tiles(t + k, k)
                            count_runs(t + k - 1, 1 - k)
                            assert chain.n == COUNT
                    chain.base, chain.n = 0, before + (NT - 3) * COUNT
                    copy_xT(NT - 1, 0)
                    q_remainder(NT - 2, 1)
                    q_remainder(NT - 1, 0)
                    count_tiles(NT - 1, 0)
                    count_runs(NT - 2, 1)
                    count_runs(NT - 1, 0)
                    chain(v.tensor_tensor(out=used[:, :, 0], in0=counts[:, :, 3], in1=counts[:, :, 2], op=ALU.is_gt))
                    chain(v.tensor_tensor(out=used[:, :, 1], in0=counts[:, :, 1], in1=counts[:, :, 0], op=ALU.is_gt))
                    chain(v.tensor_scalar(out=over[:, :], in0=counts[:, :, 3], scalar1=float(FEW), scalar2=None,
                                          op0=ALU.is_ge))
                    chain(v.tensor_tensor(out=used[:, :, 2], in0=used[:, :, 0], in1=over[:, :], op=ALU.mult))
                    chain(v.tensor_tensor(out=used[:, :, 0], in0=used[:, :, 0], in1=used[:, :, 2], op=ALU.subtract))
                    for a, rows, run_0, none in ((0, FEW, 0, NULL_A), (2, MORE, FEW, NULL_MORE)):
                        chain(v.tensor_scalar(out=row_f[:, :, a], in0=counts[:, :, 0], scalar1=float(rows),
                                              scalar2=float(-rows - run_0 - none), op0=ALU.mult, op1=ALU.add))
                        chain(v.tensor_tensor(out=row_f[:, :, a], in0=row_f[:, :, a], in1=counts[:, :, 3], op=ALU.add))
                    chain(v.tensor_scalar(out=row_f[:, :, 1], in0=counts[:, :, 1], scalar1=float(-1 - NULL_B),
                                          scalar2=None, op0=ALU.add))
                    chain(v.tensor_tensor(out=row_f[:, :, :], in0=row_f[:, :, :], in1=used[:, :, :], op=ALU.mult))
                    for a, none in ((0, NULL_A), (1, NULL_B), (2, NULL_MORE)):
                        chain(v.tensor_scalar(out=row_f[:, :, a], in0=row_f[:, :, a], scalar1=float(none), scalar2=None,
                                              op0=ALU.add))
                    chain(v.tensor_copy(node_rows[:, :, :], row_f[:, :, :]))

                @block.gpsimd
                def _(g):
                    top = g.to_reg(TILES - 1)

                    def fetch(t, par):
                        g.wait_ge(tile_ready, t + 1)
                        g.sem_inc(go, 1)
                        g.indirect_dma_start(out=row_of[par][:, :], out_offset=None, in_=starts_rows[:, :],
                                             in_offset=bass.IndirectOffsetOnAxis(ap=tile_i[par][:, 0:1], axis=0),
                                             bounds_check=top, oob_is_err=False).then_inc(row_in[par], 16)

                    steps(g, fetch)

        end_of_stage()

        with ExitStack() as st:
            kv = [sb(f"g_kv{i}", [P, GT, 2 * DM], f32, st) for i in range(NSLOT)]
            qd = [sb(f"g_qd{i}", [P, 2 * DM], f32r, st) for i in range(4)]
            q_sum = sb("g_q_sum", [P, DM], f32, st)
            prod = [sb(f"g_prod{i}", [P, DM], f32, st) for i in range(3)]
            score = [sb(f"g_score{i}", [P, GT, H], f32, st) for i in range(NSLOT)]
            idx = [sb(f"g_idx{i}", [P, GT, 2], i32, st) for i in range(NSLOT)]
            runs_g = [sb(f"g_runs_g{i}", [P, GT, 2], f32, st) for i in range(NSLOT)]
            breaks_g = [sb(f"g_breaks_g{i}", [GT * H, 132], f32, st) for i in range(NSLOT)]
            up = [sb(f"g_up{i}", [GT * H, P], f32, st) for i in range(2)]
            peak = [sb(f"g_peak{i}", [GT * H, P], f32, st) for i in range(2)]
            below_peak = [sb(f"g_below_peak{i}", [P, GT, H], f32, st) for i in range(NSLOT)]
            zm = [sb(f"g_zm{i}", [P, GT, 2 * H], f32, st) for i in range(NSLOT)]
            wv = [sb(f"g_wv{i}", [P, DM], f32, st) for i in range(4)]
            pick = [sb(f"g_pick{i}", [P, P], f32, st) for i in range(4)]
            part_sb = [sb(f"g_part_sb{i}", [P, W], f32, st) for i in range(4)]

            kv_in = [sem(f"g_kv_in{s}") for s in range(NSLOT)]
            q_in = [sem(f"g_q_in{i}") for i in range(4)]
            breaks_in = [sem(f"g_breaks_in{i}") for i in range(NSLOT)]
            idx_ready = sem("g_idx_ready")
            issue = sem("g_issue")
            prod_done = sem("g_prod_done")
            q_added = sem("g_q_added")
            score_done = sem("g_score_done")
            score_turned = sem("g_score_turned")
            up_done = sem("g_up_done")
            peak_done = sem("g_peak_done")
            peak_back = sem("g_peak_back")
            below_ready = sem("g_below_ready")
            m_ready = sem("g_m_ready")
            z_ready = sem("g_z_ready")
            runs_ready = sem("g_runs_ready")
            pick_ready = sem("g_pick_ready")
            wv_ready = sem("g_wv_ready")
            sums_done = sem("g_sums_done")
            zsum_done = sem("g_zsum_done")
            part_ready = sem("g_part_ready")
            part_out = [sem(f"g_part_out{i}") for i in range(4)]
            part_more = [sem(f"g_part_more{i}") for i in range(4)]
            pe_turn = sem("g_pe_turn")

            def late(s, k):
                return not isinstance(s, int) or s >= k

            def group_steps(eng, one):
                for s in range(NSLOT):
                    one(s, s)
                with eng.Fori(NSLOT, GROUPS - NSLOT + 1, NSLOT) as s:
                    for k in range(NSLOT):
                        one(s + k, k)

            def uses(s, k):
                if isinstance(s, int):
                    return 16 * (s // NSLOT + 1)
                return None

            with nc.Block() as block:
                @block.gpsimd
                def _(g):
                    with g.If(g.value_load(most_runs[P - 1:P, 0:1]) >= FEW):
                        top = g.to_reg(N - 1)

                        def gather(s, k):
                            if late(s, NSLOT):
                                g.wait_ge(wv_ready, (s - (NSLOT - 1)) * GT)
                                g.sem_inc(issue, 1)
                            g.tensor_copy(idx[k][:, :, :], edge_nodes[:, ds(s * GT, GT), :]).then_inc(idx_ready, 1)
                            g.wait_ge(idx_ready, s + 1)
                            g.sem_inc(issue, 1)
                            for j in range(GT):
                                g.indirect_dma_start(out=kv[k][:, j, :], out_offset=None, in_=kv_rows[:, :],
                                                     in_offset=bass.IndirectOffsetOnAxis(ap=idx[k][:, j, 0:1], axis=0),
                                                     bounds_check=top, oob_is_err=False).then_inc(kv_in[k], 16)
                                if late(s, 1) or j >= 4:
                                    g.wait_ge(prod_done, s * GT + (j - 3))
                                    g.sem_inc(issue, 1)
                                g.indirect_dma_start(out=qd[j % 4][:, :].bitcast(f32), out_offset=None, in_=q_rows[:, :],
                                                     in_offset=bass.IndirectOffsetOnAxis(ap=idx[k][:, j, 1:2], axis=0),
                                                     bounds_check=top, oob_is_err=False).then_inc(q_in[j % 4], 16)

                        group_steps(g, gather)

                @block.vector
                def _(v):
                    with v.If(v.value_load(most_runs[P - 1:P, 0:1]) >= FEW):
                        def product(s, k, j, r):
                            v.wait_ge(kv_in[k], r * GT)
                            v.wait_ge(q_in[j % 4], s * 32 + (16 * (j // 4) + 16))
                            if late(s, 1) or j >= 3:
                                v.wait_ge(score_done, s * GT + (j - 2))
                            if late(s, 1) or j >= 1:
                                v.wait_ge(prod_done, s * GT + j)
                            v.tensor_tensor(out=q_sum[:, :], in0=qd[j % 4][:, 0:DM].bitcast(f32),
                                            in1=qd[j % 4][:, DM:2 * DM].bitcast(f32), op=ALU.add).then_inc(q_added, 1)
                            v.wait_ge(q_added, s * GT + (j + 1))
                            v.tensor_tensor(out=prod[(k * GT + j) % 3][:, :], in0=kv[k][:, j, 0:DM], in1=q_sum[:, :],
                                            op=ALU.mult).then_inc(prod_done, 1)

                        def reduce(s, k, j):
                            v.wait_ge(prod_done, s * GT + (j + 1))
                            if j == 0 and late(s, NSLOT):
                                v.wait_ge(below_ready, s - (NSLOT - 1))
                            v.tensor_reduce(out=score[k][:, j, :],
                                            in_=prod[(k * GT + j) % 3][:, :].rearrange("p (h d) -> p h d", h=H),
                                            axis=AX.X, op=ALU.add).then_inc(score_done, 1)

                        def scans(s, k, r):
                            turned = bank[3][0:GT * H, 0:P]
                            v.wait_ge(score_turned, s + 1)
                            v.wait_ge(breaks_in[k], r)
                            if late(s, 1):
                                v.wait_ge(peak_done, s)
                            v.tensor_tensor_scan(out=up[0][:, :], data0=breaks_g[k][:, 0:P], data1=turned, initial=-BIG,
                                                 op0=ALU.add, op1=ALU.max).then_inc(up_done, 1)
                            v.wait_ge(up_done, s + 1)
                            if late(s, 1):
                                v.wait_ge(peak_back, s)
                            v.tensor_tensor_scan(out=peak[0][:, ::-1], data0=breaks_g[k][:, 1:P + 1][:, ::-1],
                                                 data1=up[0][:, ::-1], initial=-BIG,
                                                 op0=ALU.add, op1=ALU.max).then_inc(peak_done, 1)

                        def subtract(s, k):
                            m = bank[4][:, 0:GT * H].rearrange("p (t h) -> p t h", t=GT)
                            v.wait_ge(peak_back, s + 1)
                            if late(s, NSLOT):
                                v.wait_ge(z_ready, s - (NSLOT - 1))
                                v.wait_ge(zsum_done, (s - (NSLOT - 1)) * GT)
                            v.tensor_tensor(out=below_peak[k][:, :, :], in0=score[k][:, :, :], in1=m,
                                            op=ALU.subtract).then_inc(below_ready, 1)
                            v.tensor_copy(runs_g[k][:, :, :], edge_runs[:, ds(s * GT, GT), :]).then_inc(runs_ready, 1)
                            v.wait_ge(runs_ready, s + 1)
                            v.tensor_tensor(out=zm[k][:, :, H:2 * H], in0=m,
                                            in1=runs_g[k][:, :, 1:2].to_broadcast([P, GT, H]), op=ALU.mult).then_inc(m_ready, 1)

                        def weigh(s, k, j):
                            if late(s, 1) or j >= 4:
                                v.wait_ge(zsum_done, s * GT + (j - 3))
                            v.tensor_scalar(out=pick[j % 4][:, :], in0=iota_row[:, :], scalar1=float(FEW * j),
                                            scalar2=runs_g[k][:, j, 0:1], op0=ALU.add, op1=ALU.is_equal).then_inc(pick_ready, 1)
                            if j == 0:
                                v.wait_ge(z_ready, s + 1)
                            v.tensor_tensor(out=wv[j % 4][:, :].rearrange("p (h d) -> p h d", h=H),
                                            in0=kv[k][:, j, DM:2 * DM].rearrange("p (h d) -> p h d", h=H),
                                            in1=zm[k][:, j, 0:H].unsqueeze(2).to_broadcast([P, H, DK]),
                                            op=ALU.mult).then_inc(wv_ready, 1)

                        def step(s, k, r, rp):
                            score_it = not isinstance(s, int) or s < GROUPS
                            weigh_it = late(s, 1)
                            p = (k - 1) % NSLOT
                            after = {1: lambda: scans(s - 1, p, rp), 3: lambda: subtract(s - 1, p)}
                            take = {5: (0, 1), 6: (2, 3, 4), 7: (5, 6, 7)}
                            if score_it:
                                product(s, k, 0, r)
                            for j in range(GT):
                                if score_it:
                                    if j + 1 < GT:
                                        product(s, k, j + 1, r)
                                    reduce(s, k, j)
                                if weigh_it:
                                    if j in after:
                                        after[j]()
                                    for i in take.get(j, ()):
                                        weigh(s - 1, p, i)

                        for s in range(NSLOT):
                            step(s, s, 16, 16)
                        with v.Fori(1, GROUPS // NSLOT) as i:
                            for k in range(NSLOT):
                                step(i * NSLOT + k, k, i * 16 + 16, i * 16 if k == 0 else i * 16 + 16)
                        step(GROUPS, 0, 0, 16 * (GROUPS // NSLOT))

                @block.tensor
                def _(pe):
                    with pe.If(pe.value_load(most_runs[P - 1:P, 0:1]) >= FEW):
                        def turn_scores(s, k):
                            pe.wait_ge(score_done, s * GT + GT)
                            if late(s, 1):
                                pe.wait_ge(up_done, s)
                            pe.sem_inc(pe_turn, 1)
                            pe.transpose(bank[3][0:GT * H, 0:P], score[k][:, :, :].rearrange("p t h -> p (t h)"),
                                         ident[:, :]).then_inc(score_turned, 1)

                        def turn_back(s, k):
                            pe.wait_ge(peak_done, s + 1)
                            if late(s, 1):
                                pe.wait_ge(m_ready, s)
                            pe.sem_inc(pe_turn, 1)
                            pe.transpose(bank[4][:, 0:GT * H], peak[0][:, :], ident[0:GT * H, 0:GT * H]).then_inc(peak_back, 1)

                        def sums(s, k, j):
                            pe.wait_ge(wv_ready, s * GT + (j + 1))
                            if late(s, 1) or j >= 2:
                                pe.wait_ge(part_ready, s * (2 * GT) + (2 * j - 2))
                            if j == 0:
                                pe.wait_ge(m_ready, s + 1)
                            pe.matmul(bank[j % 2][:, :], pick[j % 4][:, :], wv[j % 4][:, :], start=True,
                                      stop=True).then_inc(sums_done, 1)
                            pe.matmul(bank[5 + j % 2][:, 0:2 * H], pick[j % 4][:, :], zm[k][:, j, :], start=True,
                                      stop=True).then_inc(zsum_done, 1)

                        def step(s, k):
                            if not isinstance(s, int) or s < GROUPS:
                                pass
                            p = (k - 1) % NSLOT
                            if late(s, 1):
                                turn_scores(s - 1, p)
                                turn_back(s - 1, p)
                                for j in range(GT):
                                    sums(s - 1, p, j)

                        for s in range(NSLOT):
                            step(s, s)
                        with pe.Fori(NSLOT, GROUPS - NSLOT + 1, NSLOT) as s:
                            for k in range(NSLOT):
                                step(s + k, k)
                        step(GROUPS, 0)

                @block.scalar
                def _(act):
                    with act.If(act.value_load(most_runs[P - 1:P, 0:1]) >= FEW):
                        def exps(s, k):
                            act.wait_ge(below_ready, s + 1)
                            if late(s, NSLOT):
                                act.wait_ge(zsum_done, (s - (NSLOT - 1)) * GT)
                            act.activation(zm[k][:, :, 0:H], below_peak[k][:, :, :], ACT.Exp).then_inc(z_ready, 1)

                        def evacuate(s, k, j, r):
                            act.wait_ge(sums_done, s * GT + (j + 1))
                            if r is not None:
                                act.wait_ge(part_out[j % 4], r)
                                act.wait_ge(part_more[j % 4], r)
                            act.activation(part_sb[j % 4][:, 0:DM], bank[j % 2][:, :], ACT.Copy).then_inc(part_ready, 1)
                            act.wait_ge(zsum_done, s * GT + (j + 1))
                            act.activation(part_sb[j % 4][:, DM:W], bank[5 + j % 2][:, 0:2 * H], ACT.Copy).then_inc(part_ready, 1)

                        def step(s, k):
                            exps(s, k)
                            for j in range(GT):
                                r = s * 32 + 16 * (j // 4) if late(s, 1) or j >= 4 else None
                                evacuate(s, k, j, r)

                        group_steps(act, step)

                @block.sync
                def _(sp):
                    with sp.If(sp.value_load(most_runs[P - 1:P, 0:1]) >= FEW):
                        def load_breaks(s, k):
                            if late(s, NSLOT):
                                sp.wait_ge(peak_done, s - (NSLOT - 1))
                            sp.dma_start(breaks_g[k][:, :], breaks_rows[ds(s * (GT * H), GT * H), :]).then_inc(breaks_in[k], 16)

                        def store(s, k, j):
                            run = sp.value_load(last_run[P - 1:P, ds(s * GT + j, 1)])
                            sp.wait_ge(part_ready, s * (2 * GT) + (2 * j + 2))
                            sp.dma_start(parts[ds((s * GT + j) * FEW, FEW), :], part_sb[j % 4][0:FEW, :]).then_inc(part_out[j % 4], 16)
                            sp.dma_start(more_parts[ds((s * GT + j) * MORE, MORE), :], part_sb[j % 4][FEW:P, :],
                                         cond=run >= FEW, cond_hint=False).then_inc(part_more[j % 4], 16)

                        load_breaks(0, 0)

                        def step(s, k):
                            nxt = (k + 1) % NSLOT
                            if not isinstance(s, int) or s + 1 < GROUPS:
                                load_breaks(s + 1, nxt)
                            for j in range(GT):
                                store(s, k, j)

                        for s in range(NSLOT):
                            step(s, s)
                        with sp.Fori(NSLOT, GROUPS - 2 * NSLOT + 1, NSLOT) as s:
                            for k in range(NSLOT):
                                step(s + k, k)
                        for k in range(NSLOT):
                            step(GROUPS - NSLOT + k, k)
                        for i in range(4):
                            sp.wait_ge(part_out[i], 16 * (TILES // 4))
                            sp.wait_ge(part_more[i], 16 * (TILES // 4))

        end_of_stage()

        with ExitStack() as st:
            three = lambda name, shape, dt=f32: [sb(f"{name}{i}", shape, dt, st) for i in range(NSLOT)]
            kv = three("kv", [P, GT, 2 * DM])
            q_g = three("q_g", [P, 2 * DM], f32r)
            key_row = three("key_row", [1, GT * P], bf16)
            idx = three("idx", [P, GT, 1], i32)
            q_idx = three("q_idx", [P, 1], i32)
            away = [sb(f"away{h}", [P, GT // 2 * P], bf16, st) for h in range(2)]
            expand = [[sb(f"expand{i}_{h}", [P, GT // 2 * P], f32r, st) for h in range(2)] for i in range(NSLOT)]
            prod = three("prod", [P, DM])
            score = three("score", [P, GT, H])
            runs_g = three("runs_g", [P, GT, 2])
            breaks_g = three("breaks_g", [GT * H, 132])
            up = sb("up", [GT * H, P], f32, st)
            peak = sb("peak", [GT * H, P], f32, st)
            below_peak = three("below_peak", [P, GT, H])
            zm = three("zm", [P, GT, 2 * H])
            pick = three("pick", [P, GT, P])
            wv = [sb(f"wv{j}", [P, DM], f32, st) for j in range(GT)]
            part_sb = three("part_sb", [P, W])
            KEY, TURNS, EXPANDED, SUMS, SMALL = bank[0], bank[1], bank[2:4], bank[4:6], bank[6:8]

            kv_in = [[sem(f"kv_in{i}_{j}") for j in range(GT)] for i in range(NSLOT)]
            q_in, key_in, breaks_in, part_out = (
                [sem(f"{n}{i}") for i in range(NSLOT)] for n in ("q_in", "key_in", "breaks_in", "part_out"))
            q_clear, idx_ready, issue = sem("q_clear"), sem("idx_ready"), sem("issue")
            key_spread, away_ready, expand_ready, expanded = (
                sem("key_spread"), sem("away_ready"), sem("expand_ready"), sem("expanded"))
            prod_done, score_done, score_turned = sem("prod_done"), sem("score_done"), sem("score_turned")
            up_done, peak_done, peak_back = sem("up_done"), sem("peak_done"), sem("peak_back")
            below_ready, m_ready, z_ready, runs_ready = sem("below_ready"), sem("m_ready"), sem("z_ready"), sem("runs_ready")
            pick_ready, wv_act, wv_pool, wv_dve = sem("pick_ready"), sem("wv_act"), sem("wv_pool"), sem("wv_dve")
            sums_done, zsum_done, part_ready, pe_turn = sem("sums_done"), sem("zsum_done"), sem("part_ready"), sem("pe_turn")

            ACT_TILES, POOL_TILES, DVE_TILES = (0, 2, 4, 6), (1, 3, 5), (7,)
            AHEAD, BEHIND = 2, 2
            STEPS = GROUPS + BEHIND
            UNROLL = NSLOT * 2
            heads = lambda a: a.rearrange("p (h d) -> p h d", h=H)

            class Group:

                def __init__(self, i, k, d):
                    self.s, self.slot, self.half = i * UNROLL + k + d, (k + d) % NSLOT, (k + d) % 2
                    self.round = i * 2 + (k + d) // NSLOT
                    self.exists = not isinstance(i, int) or 0 <= self.s < GROUPS
                    self.landed = self.round * 16 + 16

                def past(self, n):
                    return not isinstance(self.s, int) or self.s >= n

                def tiles(self, n):
                    return self.s * GT + n

            def run_steps(eng, one):
                for k in range(UNROLL):
                    one(0, k)
                whole = (GROUPS - AHEAD) // UNROLL
                with eng.Fori(1, whole) as i:
                    for k in range(UNROLL):
                        one(i, k)
                for s in range(whole * UNROLL, STEPS):
                    one(s // UNROLL, s % UNROLL)

            def usual(eng):
                return eng.If(eng.value_load(most_runs[P - 1:P, 0:1]) < FEW)

            with nc.Block() as block:
                @block.sync
                def _(sp):
                    def load_keys(a):
                        if a.past(NSLOT):
                            sp.wait_ge(key_spread, a.s * 2 - 2 * (NSLOT - 1))
                        sp.dma_start(key_row[a.slot][:, :], key_rows[ds(a.tiles(0), GT), :].rearrange(
                            "t e -> (t e)").unsqueeze(0)).then_inc(key_in[a.slot], 16)

                    def step(i, k):
                        a, c, e = Group(i, k, AHEAD), Group(i, k, 0), Group(i, k, -BEHIND)
                        if a.exists:
                            load_keys(a)
                        if c.exists:
                            if c.past(NSLOT):
                                sp.wait_ge(peak_done, c.s - (NSLOT - 1))
                            sp.dma_start(breaks_g[c.slot][:, :],
                                         breaks_rows[ds(c.s * (GT * H), GT * H), :]).then_inc(breaks_in[c.slot], 16)
                        if e.exists:
                            sp.wait_ge(part_ready, e.s * 2 + 2)
                            sp.dma_start(parts[ds(e.s * P, P), :], part_sb[e.slot][:, :]).then_inc(part_out[e.slot], 16)

                    with usual(sp):
                        for k in range(AHEAD):
                            load_keys(Group(0, k, 0))
                        run_steps(sp, step)
                        for n in range(NSLOT):
                            sp.wait_ge(part_out[n], 16 * (GROUPS // NSLOT))

                @block.gpsimd
                def _(g):
                    def gather_queries(a, top):
                        if a.past(NSLOT):
                            g.wait_ge(prod_done, a.tiles(-(NSLOT - 1) * GT))
                            g.sem_inc(issue, 1)
                        g.tensor_copy(q_idx[a.slot][:, :], run_nodes[:, ds(a.s, 1)]).then_inc(idx_ready, 1)
                        g.tensor_copy(idx[a.slot][:, :, :], edge_nodes[:, ds(a.tiles(0), GT), 0:1]).then_inc(idx_ready, 1)
                        g.wait_ge(idx_ready, a.s * 2 + 2)
                        g.sem_inc(issue, 1)
                        g.indirect_dma_start(out=q_g[a.slot][:, :].bitcast(f32), out_offset=None,
                                             in_=q_rows[:, :],
                                             in_offset=bass.IndirectOffsetOnAxis(ap=q_idx[a.slot][:, 0:1], axis=0),
                                             bounds_check=top, oob_is_err=False).then_inc(q_in[a.slot], 16)

                    def gather(a, j, top):
                        if a.past(NSLOT):
                            g.wait_ge(sums_done, a.tiles(j + 1 - NSLOT * GT))
                            g.sem_inc(issue, 1)
                        g.indirect_dma_start(out=kv[a.slot][:, j, :], out_offset=None, in_=kv_rows[:, :],
                                             in_offset=bass.IndirectOffsetOnAxis(ap=idx[a.slot][:, j, 0:1], axis=0),
                                             bounds_check=top, oob_is_err=False).then_inc(kv_in[a.slot][j], 16)

                    def weigh(b, j):
                        g.wait_ge(z_ready, b.s + 1)
                        if b.past(1):
                            g.wait_ge(sums_done, b.tiles(j + 1 - GT))
                        g.tensor_tensor(out=heads(wv[j][:, :]), in0=heads(kv[b.slot][:, j, DM:2 * DM]),
                                        in1=zm[b.slot][:, j, 0:H].unsqueeze(2).to_broadcast([P, H, DK]),
                                        op=ALU.mult).then_inc(wv_pool, 1)

                    def step(i, k, top):
                        a, b = Group(i, k, 1), Group(i, k, -1)
                        if a.exists:
                            gather_queries(a, top)
                        plan = (0, 1, 2, 3, "w1", 4, "w3", 5, 6, "w5", 7)
                        for p in plan:
                            if isinstance(p, int):
                                if a.exists:
                                    gather(a, p, top)
                            elif b.exists:
                                weigh(b, int(p[1]))

                    with usual(g):
                        for n in range(NSLOT):
                            g.memset(q_g[n][:, :].bitcast(f32), 0.0).then_inc(q_clear, 1)
                        g.wait_ge(q_clear, NSLOT)
                        top = g.to_reg(N - 1)
                        first = Group(0, 0, 0)
                        gather_queries(first, top)
                        for j in range(GT):
                            gather(first, j, top)
                        run_steps(g, lambda i, k: step(i, k, top))

                @block.scalar
                def _(act):
                    def make_expand(a, h):
                        act.wait_ge(key_spread, a.s * 2 + (h + 1))
                        if a.past(1):
                            act.wait_ge(expand_ready, a.s * 2 + (h - 1))
                        act.activation(away[h][:, :], KEY[:, :], ACT.Abs, bias=minus_p[:, 0:1]).then_inc(away_ready, 1)
                        act.wait_ge(away_ready, a.s * 2 + (h + 1))
                        if a.past(NSLOT):
                            act.wait_ge(expanded, a.tiles(4 * h + 4 - NSLOT * GT))
                        act.activation(expand[a.slot][h][:, :], away[h][:, :], ACT.Relu, bias=1.0,
                                       scale=-1.0).then_inc(expand_ready, 1)

                    def weigh(b, n):
                        j = ACT_TILES[n]
                        if n == 0:
                            act.wait_ge(z_ready, b.s + 1)
                        if b.past(1):
                            act.wait_ge(sums_done, b.tiles(j + 1 - GT))
                        for h in range(H):
                            cols = slice(h * DK, (h + 1) * DK)
                            last = act.activation(wv[j][:, cols], kv[b.slot][:, j, DM + h * DK:DM + (h + 1) * DK], ACT.Copy,
                                                  scale=zm[b.slot][:, j, h:h + 1])
                        last.then_inc(wv_act, 1)

                    def evacuate(e):
                        act.wait_ge(sums_done, e.tiles(GT))
                        if e.past(NSLOT):
                            act.wait_ge(part_out[e.slot], e.round * 16)
                        act.activation(part_sb[e.slot][:, 0:DM], SUMS[e.half][:, :], ACT.Copy).then_inc(part_ready, 1)
                        act.wait_ge(zsum_done, e.tiles(GT))
                        act.activation(part_sb[e.slot][:, DM:W], SMALL[e.half][:, 0:2 * H],
                                       ACT.Copy).then_inc(part_ready, 1)

                    def step(i, k):
                        a, b, e = Group(i, k, 1), Group(i, k, -1), Group(i, k, -BEHIND)
                        if a.exists:
                            make_expand(a, 0)
                            make_expand(a, 1)
                        if b.exists:
                            act.wait_ge(below_ready, b.s + 1)
                            if b.past(NSLOT):
                                act.wait_ge(zsum_done, b.tiles(-(NSLOT - 1) * GT))
                            act.activation(zm[b.slot][:, :, 0:H], below_peak[b.slot][:, :, :], ACT.Exp).then_inc(z_ready, 1)
                            weigh(b, 0)
                            weigh(b, 1)
                        if e.exists:
                            evacuate(e)
                        if b.exists:
                            weigh(b, 2)
                            weigh(b, 3)

                    with usual(act):
                        first = Group(0, 0, 0)
                        make_expand(first, 0)
                        make_expand(first, 1)
                        run_steps(act, step)

                @block.tensor
                def _(pe):
                    def spread_keys(a, h):
                        if h == 0:
                            pe.wait_ge(key_in[a.slot], a.landed)
                        if a.past(1) or h == 1:
                            pe.wait_ge(away_ready, a.s * 2 + h)
                        n = GT // 2 * P
                        pe.matmul(KEY[:, :], ones_b[:, :], key_row[a.slot][:, h * n:(h + 1) * n], start=True,
                                  stop=True).then_inc(key_spread, 1)

                    def expand_queries(c, j):
                        h, m = j // 4, j % 4
                        if m == 0:
                            pe.wait_ge(expand_ready, c.s * 2 + (h + 1))
                        if j == 0:
                            pe.wait_ge(q_in[c.slot], c.landed)
                        if c.past(1) or j >= 2:
                            pe.wait_ge(prod_done, c.tiles(j - 1))
                        pe.matmul(EXPANDED[j % 2][:, :], expand[c.slot][h][:, m * P:(m + 1) * P], q_g[c.slot][:, 0:DM],
                                  start=True, stop=False)
                        pe.matmul(EXPANDED[j % 2][:, :], expand[c.slot][h][:, m * P:(m + 1) * P], q_g[c.slot][:, DM:2 * DM],
                                  start=False, stop=True).then_inc(expanded, 1)

                    def turn_scores(b):
                        pe.wait_ge(score_done, b.tiles(GT))
                        if b.past(1):
                            pe.wait_ge(up_done, b.s)
                        pe.sem_inc(pe_turn, 1)
                        pe.transpose(TURNS[0:GT * H, 0:P], score[b.slot][:, :, :].rearrange("p t h -> p (t h)"),
                                     ident[:, :]).then_inc(score_turned, 1)

                    def turn_back(b):
                        pe.wait_ge(peak_done, b.s + 1)
                        if b.past(1):
                            pe.wait_ge(m_ready, b.s)
                        pe.sem_inc(pe_turn, 1)
                        pe.transpose(TURNS[:, P:P + GT * H], peak[:, :], ident[0:GT * H, 0:GT * H]).then_inc(peak_back, 1)

                    def sums(b, j):
                        for tiles, weighed in ((ACT_TILES, wv_act), (POOL_TILES, wv_pool), (DVE_TILES, wv_dve)):
                            if j in tiles:
                                pe.wait_ge(weighed, b.s * len(tiles) + (tiles.index(j) + 1))
                        if j == 0:
                            pe.wait_ge(pick_ready, b.s + 1)
                            pe.wait_ge(m_ready, b.s + 1)
                            if b.past(2):
                                pe.wait_ge(part_ready, b.s * 2 - 2)
                        pe.matmul(SUMS[b.half][:, :], pick[b.slot][:, j, :], wv[j][:, :], start=j == 0,
                                  stop=j == GT - 1).then_inc(sums_done, 1)
                        pe.matmul(SMALL[b.half][:, 0:2 * H], pick[b.slot][:, j, :], zm[b.slot][:, j, :], start=j == 0,
                                  stop=j == GT - 1).then_inc(zsum_done, 1)

                    def step(i, k):
                        a, b, c, e = Group(i, k, 1), Group(i, k, -1), Group(i, k, 0), Group(i, k, -BEHIND)
                        plan = "x0 k0 x1 T e4 x2 k1 B e5 x3 e6 x4 e7 x5 s0 x6 s1 x7 s2 s3"
                        for p in plan.split():
                            if p[0] == "e" and e.exists:
                                sums(e, int(p[1]))
                            if p[0] == "x" and c.exists:
                                expand_queries(c, int(p[1]))
                            if p[0] == "k" and a.exists:
                                spread_keys(a, int(p[1]))
                            if p[0] == "s" and b.exists:
                                sums(b, int(p[1]))
                            if p == "T" and b.exists:
                                turn_scores(b)
                            if p == "B" and b.exists:
                                turn_back(b)

                    with usual(pe):
                        first = Group(0, 0, 0)
                        spread_keys(first, 0)
                        spread_keys(first, 1)
                        run_steps(pe, step)

                @block.vector
                def _(v):
                    def product(c, j):
                        v.wait_ge(kv_in[c.slot][j], c.landed)
                        v.wait_ge(expanded, c.tiles(j + 1))
                        if c.past(1) or j >= 3:
                            v.wait_ge(score_done, c.tiles(j - 2))
                        v.tensor_tensor(out=prod[(c.slot * GT + j) % 3][:, :], in0=kv[c.slot][:, j, 0:DM],
                                        in1=EXPANDED[j % 2][:, :], op=ALU.mult).then_inc(prod_done, 1)

                    def reduce(c, j):
                        v.wait_ge(prod_done, c.tiles(j + 1))
                        if j == 0 and c.past(NSLOT):
                            v.wait_ge(below_ready, c.s - (NSLOT - 1))
                        v.tensor_reduce(out=score[c.slot][:, j, :], in_=heads(prod[(c.slot * GT + j) % 3][:, :]),
                                        axis=AX.X, op=ALU.add).then_inc(score_done, 1)

                    def scans(b):
                        v.wait_ge(score_turned, b.s + 1)
                        v.wait_ge(breaks_in[b.slot], b.landed)
                        if b.past(1):
                            v.wait_ge(peak_done, b.s)
                        v.tensor_tensor_scan(out=up[:, :], data0=breaks_g[b.slot][:, 0:P], data1=TURNS[0:GT * H, 0:P],
                                             initial=-BIG, op0=ALU.add, op1=ALU.max).then_inc(up_done, 1)
                        v.wait_ge(up_done, b.s + 1)
                        if b.past(1):
                            v.wait_ge(peak_back, b.s)
                        v.tensor_tensor_scan(out=peak[:, ::-1], data0=breaks_g[b.slot][:, 1:P + 1][:, ::-1],
                                             data1=up[:, ::-1], initial=-BIG,
                                             op0=ALU.add, op1=ALU.max).then_inc(peak_done, 1)

                    def subtract(b):
                        m = TURNS[:, P:P + GT * H].rearrange("p (t h) -> p t h", t=GT)
                        v.wait_ge(peak_back, b.s + 1)
                        if b.past(NSLOT):
                            v.wait_ge(z_ready, b.s - (NSLOT - 1))
                            v.wait_ge(zsum_done, b.tiles(-(NSLOT - 1) * GT))
                        v.tensor_tensor(out=below_peak[b.slot][:, :, :], in0=score[b.slot][:, :, :], in1=m,
                                        op=ALU.subtract).then_inc(below_ready, 1)
                        v.tensor_tensor(out=zm[b.slot][:, :, H:2 * H], in0=m,
                                        in1=runs_g[b.slot][:, :, 1:2].to_broadcast([P, GT, H]),
                                        op=ALU.mult).then_inc(m_ready, 1)

                    def make_picks(b):
                        if b.past(NSLOT):
                            v.wait_ge(zsum_done, b.tiles(-(NSLOT - 1) * GT))
                        v.tensor_tensor(out=pick[b.slot][:, :, :], in0=iota_row[:, :].unsqueeze(1).to_broadcast([P, GT, P]),
                                        in1=runs_g[b.slot][:, :, 0:1].to_broadcast([P, GT, P]),
                                        op=ALU.is_equal).then_inc(pick_ready, 1)

                    def weigh(b, j):
                        v.wait_ge(z_ready, b.s + 1)
                        if b.past(1):
                            v.wait_ge(sums_done, b.tiles(j + 1 - GT))
                        v.tensor_tensor(out=heads(wv[j][:, :]), in0=heads(kv[b.slot][:, j, DM:2 * DM]),
                                        in1=zm[b.slot][:, j, 0:H].unsqueeze(2).to_broadcast([P, H, DK]),
                                        op=ALU.mult).then_inc(wv_dve, 1)

                    def step(i, k):
                        b, c = Group(i, k, -1), Group(i, k, 0)
                        if c.exists:
                            product(c, 0)
                        for j in range(GT):
                            if c.exists:
                                if j + 1 < GT:
                                    product(c, j + 1)
                                reduce(c, j)
                            if not b.exists:
                                continue
                            if j == 0:
                                v.tensor_copy(runs_g[b.slot][:, :, :],
                                              edge_runs[:, ds(b.tiles(0), GT), :]).then_inc(runs_ready, 1)
                                v.wait_ge(runs_ready, b.s + 1)
                                scans(b)
                            if j == 1:
                                subtract(b)
                            if j == 2:
                                make_picks(b)
                            if j == 5:
                                for t in DVE_TILES:
                                    weigh(b, t)

                    with usual(v):
                        run_steps(v, step)

        end_of_stage()

        with ExitStack() as st:
            crow = sb("crow", [BROWS, BLOCKS, W], f32, st)
            orow = sb("orow", [BROWS, BLOCKS, W], f32, st)
            CT = [sb(f"CT{c}", [P, TILES], f32, st) for c in range(4)]
            zT = sb("zT", [H, TILES], f32, st)
            mT = sb("mT", [H, TILES], f32, st)
            same = sb("same", [H, TILES], f32, st)
            penal = sb("penal", [H, TILES], f32, st)
            mrun = sb("mrun", [H, TILES], f32, st)
            keep = sb("keep", [H, TILES], f32, st)
            take = sb("take", [H, TILES], f32, st)
            zrun = sb("zrun", [H, TILES], f32, st)
            head_of = sb("head_of", [H, DM], f32, st)
            c_in = sem("c_in")
            head_ready = sem("head_ready")
            c_turned = sem("c_turned")
            c_taken = sem("c_taken")
            diff_ready = sem("diff_ready")
            exp_ready = sem("exp_ready")
            spread4 = sem("spread4")
            run_ready = sem("run_ready")
            back = sem("back")
            back_taken = sem("back_taken")
            c_out = sem("c_out")
            d4 = sem("d4")
            half = TILES // 2
            with nc.Block() as block:
                @block.sync
                def _(sp):
                    first_of = parts[0:TILES * FEW, :].rearrange("(b p r) f -> r p b f", p=BROWS, r=FEW)
                    sp.dma_start(crow[:, :, :], first_of[0]).then_inc(c_in, 16)
                    sp.wait_ge(back_taken, BLOCKS)
                    sp.dma_start(firsts[0:TILES, :].rearrange("(b p) f -> p b f", p=BROWS), orow[:, :, :]).then_inc(c_out, 16)
                    sp.wait_ge(c_out, 16)

                @block.gpsimd
                def _(g):
                    chain = Chain(g, head_ready)
                    chain(g.memset(head_of[:, :], 1.0))
                    chain(g.affine_select(out=head_of[:, :], in_=head_of[:, :], compare_op=ALU.is_ge, fill=0.0,
                                          base=0, pattern=[[1, DM]], channel_multiplier=-DK))
                    chain(g.affine_select(out=head_of[:, :], in_=head_of[:, :], compare_op=ALU.is_ge, fill=0.0,
                                          base=DK - 1, pattern=[[-1, DM]], channel_multiplier=DK))

                @block.tensor
                def _(pe):
                    pe.wait_ge(c_in, 16)
                    for b in range(BLOCKS):
                        if b >= 2:
                            pe.wait_ge(c_taken, b - 1)
                        for c in range(4):
                            pe.transpose(bank[b % 2][:, c * BROWS:(c + 1) * BROWS], crow[:, b, c * P:(c + 1) * P],
                                         ident[0:BROWS, 0:BROWS])
                        pe.transpose(bank[2 + b % 2][0:H, 0:BROWS], crow[:, b, DM:DM + H], ident[0:BROWS, 0:BROWS])
                        pe.transpose(bank[2 + b % 2][0:H, 256:256 + BROWS], crow[:, b, DM + H:W],
                                     ident[0:BROWS, 0:BROWS]).then_inc(c_turned, 1)
                    pe.wait_ge(head_ready, 3)
                    pe.wait_ge(c_taken, BLOCKS)
                    pe.wait_ge(exp_ready, 3)
                    for c in range(4):
                        if c >= 1:
                            pe.wait_ge(run_ready, c)
                        for a, rows in enumerate((keep, take)):
                            for i in range(2):
                                last = pe.matmul(bank[4 + 2 * a + i][:, 0:half], head_of[:, c * P:(c + 1) * P],
                                                 rows[:, i * half:(i + 1) * half], start=True, stop=True)
                        last.then_inc(spread4, 1)
                    pe.wait_ge(run_ready, 5)
                    for b in range(BLOCKS):
                        if b >= 2:
                            pe.wait_ge(back_taken, b - 1)
                        cols = slice(b * BROWS, (b + 1) * BROWS)
                        for c in range(4):
                            pe.transpose(bank[b % 2][0:BROWS, c * P:(c + 1) * P], CT[c][:, cols], ident[:, :])
                        pe.transpose(bank[2 + b % 2][0:BROWS, 0:H], zrun[:, cols], ident[0:H, 0:H])
                        pe.transpose(bank[2 + b % 2][0:BROWS, H:2 * H], mrun[:, cols], ident[0:H, 0:H]).then_inc(back, 1)

                @block.scalar
                def _(act):
                    act.wait_ge(diff_ready, 2)
                    act.activation(keep[:, :], keep[:, :], ACT.Exp).then_inc(exp_ready, 1)
                    act.activation(take[:, :], take[:, :], ACT.Exp).then_inc(exp_ready, 1)

                @block.vector
                def _(v):
                    chain = Chain(v, d4)
                    for b in range(BLOCKS):
                        v.wait_ge(c_turned, b + 1)
                        cols = slice(b * BROWS, (b + 1) * BROWS)
                        for c in range(4):
                            chain(v.tensor_copy(CT[c][:, cols], bank[b % 2][:, c * BROWS:(c + 1) * BROWS]))
                        chain(v.tensor_copy(zT[:, cols], bank[2 + b % 2][0:H, 0:BROWS]))
                        chain(v.tensor_copy(mT[:, cols], bank[2 + b % 2][0:H, 256:256 + BROWS]))
                        v.sem_inc(c_taken, 1)
                    chain(v.memset(same[:, 0:1], 0.0))
                    chain(v.tensor_tensor(out=same[:, 1:TILES], in0=first_dst[0:H, 1:TILES],
                                          in1=first_dst[0:H, 0:TILES - 1], op=ALU.is_equal))
                    chain(v.tensor_scalar(out=penal[:, :], in0=same[:, :], scalar1=-1.0, scalar2=BIG, op0=ALU.add,
                                          op1=ALU.mult))
                    chain(v.tensor_tensor_scan(out=mrun[:, :], data0=penal[:, :], data1=mT[:, :], initial=-BIG,
                                               op0=ALU.add, op1=ALU.max))
                    chain(v.memset(keep[:, 0:1], 0.0))
                    chain(v.tensor_tensor(out=keep[:, 1:TILES], in0=mrun[:, 0:TILES - 1], in1=mrun[:, 1:TILES],
                                          op=ALU.subtract))
                    v.tensor_scalar(out=keep[:, :], in0=keep[:, :], scalar1=0.0, scalar2=None,
                                    op0=ALU.min).then_inc(diff_ready, 1)
                    v.tensor_tensor(out=take[:, :], in0=mT[:, :], in1=mrun[:, :], op=ALU.subtract).then_inc(diff_ready, 1)
                    v.wait_ge(exp_ready, 2)
                    v.tensor_tensor(out=keep[:, :], in0=keep[:, :], in1=same[:, :], op=ALU.mult).then_inc(exp_ready, 1)
                    v.wait_ge(exp_ready, 3)
                    chain(v.tensor_tensor(out=zT[:, :], in0=zT[:, :], in1=take[:, :], op=ALU.mult))
                    for c in range(4):
                        v.wait_ge(spread4, c + 1)
                        for i in range(2):
                            cols = slice(i * half, (i + 1) * half)
                            chain(v.tensor_tensor(out=CT[c][:, cols], in0=CT[c][:, cols], in1=bank[6 + i][:, 0:half],
                                                  op=ALU.mult))
                        chain(v.tensor_tensor_scan(out=CT[c][:, 0:half], data0=bank[4][:, 0:half], data1=CT[c][:, 0:half],
                                                   initial=0.0, op0=ALU.mult, op1=ALU.add))
                        v.tensor_tensor_scan(out=CT[c][:, half:TILES], data0=bank[5][:, 0:half],
                                             data1=CT[c][:, half:TILES], initial=CT[c][:, half - 1:half],
                                             op0=ALU.mult, op1=ALU.add).then_inc(run_ready, 1)
                    v.tensor_tensor_scan(out=zrun[:, :], data0=keep[:, :], data1=zT[:, :], initial=0.0,
                                         op0=ALU.mult, op1=ALU.add).then_inc(run_ready, 1)
                    for b in range(BLOCKS):
                        v.wait_ge(back, b + 1)
                        chain(v.tensor_copy(orow[:, b, 0:DM], bank[b % 2][0:BROWS, :]))
                        v.tensor_copy(orow[:, b, DM:W], bank[2 + b % 2][0:BROWS, 0:2 * H]).then_inc(back_taken, 1)

        end_of_stage()

        with ExitStack() as st:
            wo_sb = sb("wo_sb", [P, 4, DM], f32, st)
            w1_sb = sb("w1_sb", [P, 4, DFF], f32, st)
            w2_sb = sb("w2_sb", [P, 2, DM], f32, st)
            b1_sb = sb("b1_sb", [P, 2], f32, st)
            vec = {n: sb(f"{n}_sb", [P, DM], f32, st) for n in ("g1", "h1", "g2", "h2", "b2")}
            half_neg = sb("half_neg", [P, 1], f32, st)
            sign = sb("sign", [P, 2], f32, st)
            ring = lambda n, name, shape, dt=f32: [sb(f"{name}{i}", shape, dt, st) for i in range(n)]
            rows5 = ring(2, "rows5_", [P, 3], i32)
            pa, pb = ring(2, "pa", [P, W]), ring(2, "pb", [P, W])
            x_one, x_two = ring(2, "x_one", [P, DM]), ring(2, "x_two", [P, DM])
            top_m = ring(2, "top_m", [P, H])
            diff, wgt, zz = ring(2, "diff", [P, 2, H]), ring(2, "wgt", [P, 2, H]), ring(2, "zz", [P, 2, H])
            attn = ring(2, "attn", [P, DM])
            aT, x1T, hT = ring(2, "aT", [P, 4, P]), ring(2, "x1T", [P, 4, P]), ring(2, "hT", [P, 2, P])
            r1 = ring(2, "r1", [P, DM])
            x1 = ring(2, "x1_", [P, DM])
            x1b = ring(4, "x1b", [P, DM])
            y = ring(2, "y", [P, DM])
            y2 = ring(2, "y2_", [P, DM])
            z3 = ring(2, "z3_", [P, DM])
            o_sb = ring(2, "o_sb", [P, DM])
            stats = [ring(2, f"stats{i}", [P, 6]) for i in range(3)]
            mv = [ring(2, f"mv{i}_", [P, 2]) for i in range(3)]
            rstd = [ring(2, f"rstd{i}_", [P, 2]) for i in range(3)]
            w5_in = sem("w5_in")
            go5 = sem("go5")
            a_in, b_in, more_in, one_in, two_in, o_stored = (
                [sem(f"{n}{i}") for i in range(2)] for n in ("a_in", "b_in", "more_in", "one_in", "two_in", "o_stored"))
            diff5, exp5, attn_ready = sem("diff5"), sem("exp5"), sem("attn_ready")
            a_turned, aT_ready, o_done = sem("a_turned"), sem("aT_ready"), sem("o_done")
            added, moments, powered, rooted, normed = (
                [sem(f"{n}{i}") for i in range(3)] for n in ("added", "moments", "powered", "rooted", "normed"))
            x1_ready, x1b_ready, y2_ready = sem("x1_ready"), sem("x1b_ready"), sem("y2_ready")
            x1_turned, x1T_ready = sem("x1_turned"), sem("x1T_ready")
            h_done, hT_ready, f_done = sem("h_done"), sem("hT_ready"), sem("f_done")
            pconst = sem("pconst")
            g5, d5, d5_turn = sem("g5"), sem("d5"), sem("d5_turn")

            MERGE, ATTEND, NORM1, FEED, NORM2, NORM3 = 1, 2, 3, 4, 5, 6
            STEPS = NT + NORM3
            RING5 = 4

            def loop5(eng, one, chain=None, per=0):
                for s in range(2 * RING5):
                    one(s, s % RING5)
                before = chain.n if chain else 0
                with eng.Fori(2 * RING5, NT - RING5, RING5) as s:
                    for k in range(RING5):
                        if chain:
                            chain.base, chain.n = (s + k - 2 * RING5) * per + before, 0
                        one(s + k, k)
                        assert not chain or chain.n == per, chain.n
                if chain:
                    chain.base, chain.n = 0, before + (NT - 1 - 2 * RING5) * per
                for s in range(NT - 1, STEPS):
                    one(s, s % RING5)

            assert (NT - 1) % RING5 == 0

            def on(t):
                return not isinstance(t, int) or 0 <= t < NT

            def from_tile(t, n):
                return not isinstance(t, int) or t >= n

            def rows_of(t):
                return slice(LAST_START, N) if isinstance(t, int) and t == NT - 1 else ds(t * P, P)

            def seen(t, q):
                return (t - q) * 8 + 16

            with nc.Block() as block:
                @block.sync
                def _(sp):
                    sp.dma_start(wo_sb[:, :, :], Wo.rearrange("(c p) n -> p c n", p=P)).then_inc(w5_in, 16)
                    sp.dma_start(w1_sb[:, :, :], W1.rearrange("(c p) n -> p c n", p=P)).then_inc(w5_in, 16)
                    sp.dma_start(w2_sb[:, :, :], W2.rearrange("(c p) n -> p c n", p=P)).then_inc(w5_in, 16)
                    with nc.allow_non_contiguous_dma(reason="256 biases, once"):
                        sp.dma_start(b1_sb[:, :], b1.rearrange("(c p) -> p c", p=P)).then_inc(w5_in, 16)
                    for n, a in (("g1", ln1_g), ("h1", ln1_b), ("g2", ln2_g), ("h2", ln2_b), ("b2", b2)):
                        sp.dma_start(vec[n][:, :], a.unsqueeze(0).to_broadcast([P, DM])).then_inc(w5_in, 16)

                    def step(s, k):
                        t, q = s - ATTEND, (k - ATTEND) % 2
                        if on(t):
                            if from_tile(t, 2):
                                sp.wait_ge(added[0], t - 1)
                            sp.dma_start(x_one[q][:, :], x[rows_of(t), :]).then_inc(one_in[q], 16)
                        t, q = s - NORM2, (k - NORM2) % 2
                        if on(t):
                            if from_tile(t, 2):
                                sp.wait_ge(added[2], t - 1)
                            sp.dma_start(x_two[q][:, :], x[rows_of(t), :]).then_inc(two_in[q], 16)
                        t, q = s - NORM3, (k - NORM3) % 2
                        if on(t):
                            if isinstance(t, int) and t == NT - 1:
                                sp.wait_ge(o_stored[1], 8 * (NT - 1))
                            sp.wait_ge(normed[2], t + 1)
                            sp.dma_start(out[rows_of(t), :], o_sb[q][:, :]).then_inc(o_stored[q], 16)

                    loop5(sp, step)
                    sp.wait_ge(o_stored[0], 16 * (NT // 2 + 1))

                @block.gpsimd
                def _(g):
                    g.memset(half_neg[:, :], -0.5).then_inc(pconst, 1)
                    topa, topb, topm = g.to_reg(NULL_A), g.to_reg(NULL_B), g.to_reg(NULL_MORE - 1)
                    most = g.value_load(most_runs[P - 1:P, 0:1])
                    g.wait_ge(pconst, 1)
                    g.wait_ge(w5_in, 9 * 16)
                    chain = Chain(g, g5)

                    def fetch(t, q):
                        if from_tile(t, 2):
                            g.wait_ge(attn_ready, t - 1)
                            g.sem_inc(go5, 1)
                        chain(g.tensor_copy(rows5[q][:, :], node_rows[:, ds(t, 1), :].rearrange("p a b -> p (a b)")))
                        g.sem_inc(go5, 1)
                        g.indirect_dma_start(out=pa[q][:, :], out_offset=None, in_=parts[:, :],
                                             in_offset=bass.IndirectOffsetOnAxis(ap=rows5[q][:, 0:1], axis=0),
                                             bounds_check=topa, oob_is_err=False).then_inc(a_in[q], 16)
                        with g.If(most >= FEW):
                            g.wait_ge(a_in[q], seen(t, q))
                            g.sem_inc(go5, 1)
                            g.indirect_dma_start(out=pa[q][:, :], out_offset=None, in_=more_parts[:, :],
                                                 in_offset=bass.IndirectOffsetOnAxis(ap=rows5[q][:, 2:3], axis=0),
                                                 bounds_check=topm, oob_is_err=False).then_inc(more_in[q], 16)
                        with g.Else():
                            g.sem_inc(more_in[q], 16)
                        g.indirect_dma_start(out=pb[q][:, :], out_offset=None, in_=firsts[:, :],
                                             in_offset=bass.IndirectOffsetOnAxis(ap=rows5[q][:, 1:2], axis=0),
                                             bounds_check=topb, oob_is_err=False).then_inc(b_in[q], 16)

                    def inverse_root(i, t, q):
                        g.wait_ge(moments[i], t + 1)
                        g.tensor_tensor(out=rstd[i][q][:, 0:1], in0=mv[i][q][:, 1:2], in1=half_neg[:, :],
                                        op=ALU.pow).then_inc(powered[i], 1)
                        g.wait_ge(powered[i], t + 1)
                        g.tensor_tensor(out=rstd[i][q][:, 1:2], in0=mv[i][q][:, 0:1], in1=rstd[i][q][:, 0:1],
                                        op=ALU.mult).then_inc(rooted[i], 1)

                    def gain(i, t, a, g_, b_, ready):
                        g.wait_ge(normed[i], t + 1)
                        chain(g.tensor_tensor(out=a[:, :], in0=a[:, :], in1=g_[:, :], op=ALU.mult))
                        g.tensor_tensor(out=a[:, :], in0=a[:, :], in1=b_[:, :], op=ALU.add).then_inc(ready, 1)

                    def step(s, k):
                        for i, lag in enumerate((NORM1, NORM2, NORM3)):
                            if on(s - lag):
                                inverse_root(i, s - lag, (k - lag) % 2)
                        if on(s):
                            fetch(s, k % 2)
                        if on(s - NORM1):
                            gain(0, s - NORM1, x1[(k - NORM1) % 2], vec["g1"], vec["h1"], x1_ready)
                        if on(s - NORM2):
                            gain(1, s - NORM2, y2[(k - NORM2) % 2], vec["g2"], vec["h2"], y2_ready)

                    loop5(g, step, chain, 3)

                @block.tensor
                def _(pe):
                    pe.wait_ge(w5_in, 9 * 16)

                    def turn(src_, bk, turned):
                        for c in range(4):
                            last = pe.transpose(bank[bk][:, c * P:(c + 1) * P], src_[:, c * P:(c + 1) * P], ident[:, :])
                        last.then_inc(turned, 1)

                    def step(s, k):
                        tf, qf = s - FEED, (k - FEED) % 2
                        ta, qa = s - ATTEND, (k - ATTEND) % 2
                        if on(tf):
                            pe.wait_ge(x1_ready, tf + 1)
                            if from_tile(tf, 1):
                                pe.wait_ge(x1T_ready, tf)
                            turn(x1[qf], 1, x1_turned)
                        if on(ta):
                            pe.wait_ge(attn_ready, ta + 1)
                            if from_tile(ta, 1):
                                pe.wait_ge(aT_ready, ta)
                            turn(attn[qa], 0, a_turned)
                        if on(tf):
                            pe.wait_ge(x1T_ready, tf + 1)
                            if from_tile(tf, 1):
                                pe.wait_ge(hT_ready, 2 * tf)
                            for f in range(2):
                                for c in range(4):
                                    last = pe.matmul(bank[4][:, f * P:(f + 1) * P], w1_sb[:, c, f * P:(f + 1) * P],
                                                     x1T[qf][:, c, :], start=c == 0, stop=c == 3)
                            last.then_inc(h_done, 1)
                        if on(ta):
                            pe.wait_ge(aT_ready, ta + 1)
                            if from_tile(ta, 2):
                                pe.wait_ge(added[0], ta - 1)
                            for c in range(4):
                                last = pe.matmul(bank[2 + qa][:, :], aT[qa][:, c, :], wo_sb[:, c, :], start=c == 0, stop=c == 3)
                            last.then_inc(o_done, 1)
                        if on(tf):
                            pe.wait_ge(hT_ready, 2 * tf + 2)
                            if from_tile(tf, 2):
                                pe.wait_ge(added[1], tf - 1)
                            for f in range(2):
                                last = pe.matmul(bank[5 + qf][:, :], hT[qf][:, f, :], w2_sb[:, f, :], start=f == 0, stop=f == 1)
                            last.then_inc(f_done, 1)

                    loop5(pe, step)

                @block.scalar
                def _(act):
                    act.wait_ge(w5_in, 9 * 16)

                    def evacuate(t, dst_, bk, turned, used_, ready):
                        act.wait_ge(turned, t + 1)
                        if from_tile(t, 2):
                            act.wait_ge(used_, t - 1)
                        act.activation(dst_[:, :, :], bank[bk][:, :].rearrange("p (c n) -> p c n", c=4),
                                       ACT.Copy).then_inc(ready, 1)

                    def norm(i, t, q, a, o, free, n):
                        act.wait_ge(rooted[i], t + 1)
                        if from_tile(t, 2):
                            act.wait_ge(free, n)
                        act.activation(o[:, :], a[:, :], ACT.Identity, bias=rstd[i][q][:, 1:2],
                                       scale=rstd[i][q][:, 0:1]).then_inc(normed[i], 1)

                    def step(s, k):
                        tf, qf = s - FEED, (k - FEED) % 2
                        if on(tf):
                            evacuate(tf, x1T[qf], 1, x1_turned, h_done, x1T_ready)
                        t, q = s - ATTEND, (k - ATTEND) % 2
                        if on(t):
                            evacuate(t, aT[q], 0, a_turned, o_done, aT_ready)
                        if on(tf):
                            act.wait_ge(h_done, tf + 1)
                            if from_tile(tf, 2):
                                act.wait_ge(f_done, tf - 1)
                            for f in range(2):
                                act.activation(hT[qf][:, f, :], bank[4][:, f * P:(f + 1) * P], ACT.Relu,
                                               bias=b1_sb[:, f:f + 1]).then_inc(hT_ready, 1)
                        t, q = s - NORM1, (k - NORM1) % 2
                        if on(t):
                            if from_tile(t, 2):
                                act.wait_ge(x1_turned, t - 1)
                            norm(0, t, q, r1[q], x1[q], x1b_ready, t - 1)
                        t, q = s - NORM2, (k - NORM2) % 2
                        if on(t):
                            norm(1, t, q, y[q], y2[q], added[2], t - 1)
                        t, q = s - NORM3, (k - NORM3) % 2
                        if on(t):
                            norm(2, t, q, z3[q], o_sb[q], o_stored[q], seen(t, q) - 16)
                        t, q = s - MERGE, (k - MERGE) % 2
                        if on(t):
                            act.wait_ge(diff5, t + 1)
                            if from_tile(t, 2):
                                act.wait_ge(attn_ready, t - 1)
                            act.activation(wgt[q][:, :, :], diff[q][:, :, :], ACT.Exp).then_inc(exp5, 1)

                    loop5(act, step)

                @block.vector
                def _(v):
                    chain = Chain(v, d5)
                    chain(v.memset(sign[:, 0:1], -1.0))
                    chain(v.memset(sign[:, 1:2], 1.0))
                    heads = lambda a: a.rearrange("p (h d) -> p h d", h=H)
                    wide = lambda a: a.unsqueeze(2).to_broadcast([P, H, DK])

                    def add_and_measure(i, t, q, o, a, b):
                        v.tensor_tensor(out=o[:, :], in0=a, in1=b, op=ALU.add).then_inc(added[i], 1)
                        v.wait_ge(added[i], t + 1)
                        chain(v.bn_stats(out=stats[i][q][:, :], in_=o[:, :]))
                        v.sem_inc(d5_turn, 1)
                        chain(v.bn_aggr(out=mv[i][q][:, :], in_=stats[i][q][:, :]))
                        chain(v.tensor_tensor(out=mv[i][q][:, :], in0=mv[i][q][:, :], in1=sign[:, :], op=ALU.mult))
                        v.tensor_scalar(out=mv[i][q][:, 1:2], in0=mv[i][q][:, 1:2], scalar1=EPS, scalar2=None,
                                        op0=ALU.add).then_inc(moments[i], 1)

                    def compare(t, q):
                        v.wait_ge(a_in[q], seen(t, q))
                        v.wait_ge(more_in[q], seen(t, q))
                        v.wait_ge(b_in[q], seen(t, q))
                        chain(v.tensor_tensor(out=top_m[q][:, :], in0=pa[q][:, DM + H:W], in1=pb[q][:, DM + H:W], op=ALU.max))
                        chain(v.tensor_tensor(out=diff[q][:, 0, :], in0=pa[q][:, DM + H:W], in1=top_m[q][:, :],
                                              op=ALU.subtract))
                        v.tensor_tensor(out=diff[q][:, 1, :], in0=pb[q][:, DM + H:W], in1=top_m[q][:, :],
                                        op=ALU.subtract).then_inc(diff5, 1)

                    def merge(t, q):
                        v.wait_ge(exp5, t + 1)
                        chain(v.tensor_tensor(out=zz[q][:, 0, :], in0=pa[q][:, DM:DM + H], in1=wgt[q][:, 0, :], op=ALU.mult))
                        chain(v.tensor_tensor(out=zz[q][:, 1, :], in0=pb[q][:, DM:DM + H], in1=wgt[q][:, 1, :], op=ALU.mult))
                        chain(v.tensor_tensor(out=zz[q][:, 0, :], in0=zz[q][:, 0, :], in1=zz[q][:, 1, :], op=ALU.add))
                        chain(v.tensor_scalar(out=zz[q][:, 0, :], in0=zz[q][:, 0, :], scalar1=1e-30, scalar2=None, op0=ALU.max))
                        chain(v.reciprocal(zz[q][:, 1, :], zz[q][:, 0, :]))
                        chain(v.tensor_tensor(out=wgt[q][:, :, :], in0=wgt[q][:, :, :],
                                              in1=zz[q][:, 1:2, :].to_broadcast([P, 2, H]), op=ALU.mult))
                        chain(v.tensor_tensor(out=heads(pa[q][:, 0:DM]), in0=heads(pa[q][:, 0:DM]),
                                              in1=wide(wgt[q][:, 0, :]), op=ALU.mult))
                        chain(v.tensor_tensor(out=heads(pb[q][:, 0:DM]), in0=heads(pb[q][:, 0:DM]),
                                              in1=wide(wgt[q][:, 1, :]), op=ALU.mult))
                        if from_tile(t, 2):
                            v.wait_ge(a_turned, t - 1)
                        v.tensor_tensor(out=attn[q][:, :], in0=pa[q][:, 0:DM], in1=pb[q][:, 0:DM],
                                        op=ALU.add).then_inc(attn_ready, 1)

                    def step(s, k):
                        if on(s - MERGE):
                            compare(s - MERGE, (k - MERGE) % 2)
                        t, q = s - NORM1, (k - NORM1) % 2
                        if on(t):
                            v.wait_ge(o_done, t + 1)
                            v.wait_ge(one_in[q], seen(t, q))
                            if from_tile(t, 2):
                                v.wait_ge(normed[0], t - 1)
                            add_and_measure(0, t, q, r1[q], x_one[q][:, :], bank[2 + q][:, :])
                        t, q = s - NORM2, (k - NORM2) % 2
                        if on(t):
                            v.wait_ge(f_done, t + 1)
                            if from_tile(t, 2):
                                v.wait_ge(normed[1], t - 1)
                            add_and_measure(1, t, q, y[q], x1b[(k - NORM2) % 4][:, :], bank[5 + q][:, :])
                        t, q = s - NORM3, (k - NORM3) % 2
                        if on(t):
                            v.wait_ge(y2_ready, t + 1)
                            v.wait_ge(two_in[q], seen(t, q))
                            if from_tile(t, 2):
                                v.wait_ge(normed[2], t - 1)
                            add_and_measure(2, t, q, z3[q], x_two[q][:, :], y2[q][:, :])
                        if on(s - MERGE):
                            merge(s - MERGE, (k - MERGE) % 2)
                        t, q = s - NORM1, (k - NORM1) % 2
                        if on(t):
                            v.wait_ge(x1_ready, t + 1)
                            if from_tile(t, 4):
                                v.wait_ge(added[1], t - 3)
                            v.tensor_tensor(out=x1b[(k - NORM1) % 4][:, :], in0=x1[q][:, :], in1=vec["b2"][:, :],
                                            op=ALU.add).then_inc(x1b_ready, 1)

                    v.wait_ge(w5_in, 9 * 16)
                    loop5(v, step, chain, 2 + 8 + 9)


_INS = ['x', 'src', 'dst', 'L0_gnn_Wq', 'L0_gnn_Wk', 'L0_gnn_Wv', 'L0_gnn_Wo', 'L0_gnn_ln1_g', 'L0_gnn_ln1_b',
        'L0_gnn_ln2_g', 'L0_gnn_ln2_b', 'L0_gnn_W1', 'L0_gnn_b1', 'L0_gnn_W2', 'L0_gnn_b2']
_OUTS = [((6250, 512), 'float32')]


def kernel(**inputs):
    import numpy as _np
    import concourse.bacc as _bacc
    from concourse import mybir as _mybir
    from concourse.bass_utils import run_bass_kernel_spmd as _run

    nc = _bacc.Bacc("TRN2", target_bir_lowering=False, num_devices=1)
    arrays, args = {}, []
    for name in _INS:
        a = _np.ascontiguousarray(inputs[name])
        arrays[f"in_{name}_dram"] = a
        args.append(nc.dram_tensor(f"in_{name}_dram", a.shape, _mybir.dt.from_np(a.dtype), kind="ExternalInput").ap())
    for i, (shape, dtype) in enumerate(_OUTS):
        dt = _mybir.dt.from_np(_np.dtype(dtype))
        args.append(nc.dram_tensor(f"out_{i}_dram", shape, dt, kind="ExternalOutput").ap())
    build(nc, *args)
    r = _run(nc, [arrays], core_ids=[0])
    return r.results[0]["out_0_dram"]
```

```python
import concourse.bass as bass
from concourse import mybir
from contextlib import ExitStack

N, E, DM, H, DFF = 6250, 106250, 512, 8, 256
DK = DM // H
P = 128

GT = 8
NSLOT = 3
GROUPS = 105
TILES = GROUPS * GT
BLOCKS, BROWS = 7, 120
FULL_ROWS = E // P
TAIL = E % P
LAST_ROWS = FULL_ROWS - (BLOCKS - 1) * BROWS
NT = (N + P - 1) // P
LAST_START = N - P
W = DM + 2 * H
FEW = P // GT
MORE = P - FEW
NULL_A = TILES * FEW
NULL_MORE = TILES * MORE
NULL_B = TILES
BIG = 1.0e30
FAR = 1.0e6
EPS = 1e-5
assert TILES * P >= E and GROUPS % NSLOT == 0 and BLOCKS * BROWS == TILES


class Chain:

    def __init__(self, eng, sem):
        self.eng, self.sem, self.base, self.n = eng, sem, 0, 0

    def __call__(self, ins):
        ins.then_inc(self.sem, 1)
        self.n += 1
        self.eng.wait_ge(self.sem, self.base + self.n)


def build(nc, x, src, dst, Wq, Wk, Wv, Wo, ln1_g, ln1_b, ln2_g, ln2_b, W1, b1, W2, b2, out):
    f32, i32, f32r, bf16 = mybir.dt.float32, mybir.dt.int32, mybir.dt.float32r, mybir.dt.bfloat16
    ALU, ACT, AX = mybir.AluOpType, mybir.ActivationFunctionType, mybir.AxisListType
    ds = bass.ds

    with ExitStack() as ctx:
        def sb(name, shape, dt=f32, scope=ctx):
            return scope.enter_context(nc.sbuf_tensor(name, shape, dt))

        in_use = []

        def sem(name):
            in_use.append(nc.alloc_semaphore(name=name))
            return in_use[-1]

        def end_of_stage():
            nc.clear_and_free_semaphores(list(in_use))
            in_use.clear()
            nc.all_engine_barrier()

        def dram(name, shape, dt=f32):
            return nc.dram_tensor(name, shape, dt).ap()

        q_rows = dram("q_rows", [N, DM])
        kv_rows = dram("kv_rows", [N, 2 * DM])
        breaks_rows = dram("breaks_rows", [TILES * H, 132])
        starts_rows = dram("starts_rows", [TILES, P])
        key_rows = dram("key_rows", [TILES, P], bf16)
        run_rows = dram("run_rows", [TILES, FEW])
        parts = dram("parts", [TILES * FEW + 1, W])
        more_parts = dram("more_parts", [TILES * MORE, W])
        firsts = dram("firsts", [TILES + 1, W])

        bank = [ctx.enter_context(nc.psum_tensor(f"bank{i}", [P, 512], f32)) for i in range(8)]
        ident = sb("ident", [P, P])
        ones_row = sb("ones_row", [1, P])
        ones_b = sb("ones_b", [1, P], bf16)
        iota_row = sb("iota_row", [P, P])
        edge_nodes = sb("edge_nodes", [P, TILES, 2], i32)
        edge_runs = sb("edge_runs", [P, TILES, 2])
        run_nodes = sb("run_nodes", [P, GROUPS], i32)
        group_runs = sb("group_runs", [P, GT])
        minus_p = sb("minus_p", [P, 1])
        first_dst = sb("first_dst", [P, TILES])
        node_id = sb("node_id", [P, NT])
        node_rows = sb("node_rows", [P, NT, 3], i32)
        most_runs = sb("most_runs", [P, 1], i32)

        early = ctx.enter_context(ExitStack())
        runs = sb("runs", [BROWS, BLOCKS, P], f32, early)
        begin_dst = sb("begin_dst", [BROWS, BLOCKS, P], f32, early)
        hit = sb("hit", [BROWS, BLOCKS, P], f32, early)
        run_dst = sb("run_dst", [BROWS, BLOCKS, FEW], f32, early)
        run_id = sb("run_id", [BROWS, FEW], f32, early)
        missing = sb("missing", [BROWS, BLOCKS, FEW], f32, early)
        run_turn = sb("run_turn", [GROUPS, P], f32, early)
        w_high = [sb(n, [P, 4, DM], f32r, early) for n in ("wq_high", "wk_high", "wv_high")]
        w_rest = [sb(n, [P, 4, DM], f32r, early) for n in ("wq_rest", "wk_rest", "wv_rest")]
        with ExitStack() as st:
            w_sb = [sb(n, [P, 4, DM], f32, st) for n in ("wq_sb", "wk_sb", "wv_sb")]
            weights_in = [sem(f"weights_in{m}") for m in range(3)]
            w_high_ready, w_split = sem("w_high_ready"), sem("w_split")
            dst_i = sb("dst_i", [BROWS, BLOCKS, P], i32, st)
            src_i = sb("src_i", [BROWS, BLOCKS, P], i32, st)
            dst_f = sb("dst_f", [BROWS, BLOCKS, P], f32, st)
            src_f = sb("src_f", [BROWS, BLOCKS, P], f32, st)
            begins = sb("begins", [BROWS, BLOCKS, 132], f32, st)
            breaks = sb("breaks", [BROWS, BLOCKS, 132], f32, st)
            keys = sb("keys", [BROWS, BLOCKS, P], f32, st)
            keys_b = sb("keys_b", [BROWS, BLOCKS, P], bf16, st)
            row_i = sb("row_i", [BROWS, 1], i32, st)
            row_key = sb("row_key", [BROWS, 1], f32, st)
            most_f = sb("most_f", [P, 1], f32, st)
            last_f = sb("last_f", [P, GROUPS, GT], f32, st)
            starts = sb("starts", [BROWS, BLOCKS, P], f32, st)
            ones = sb("ones", [BROWS, P], f32, st)
            first_row = sb("first_row", [1, TILES], f32, st)
            null_row = sb("null_row", [1, W], f32, st)
            padded = sem("padded")
            edges_in = sem("edges_in")
            consts = sem("consts")
            tabled = sem("tabled")
            rows_ready = sem("rows_ready")
            turned = sem("turned")
            turned_used = sem("turned_used")
            spread = sem("spread")
            d1 = sem("d1")
            with nc.Block() as block:
                @block.sync
                def _(sp):
                    sp.wait_ge(padded, 2)
                    for dram_list, rows in ((src, src_i), (dst, dst_i)):
                        whole = (BLOCKS - 1) * BROWS * P
                        sp.dma_start(rows[:, 0:BLOCKS - 1, :], dram_list[0:whole].rearrange(
                            "(b p j) -> p b j", p=BROWS, j=P)).then_inc(edges_in, 16)
                        sp.dma_start(rows[0:LAST_ROWS, BLOCKS - 1, :], dram_list[whole:FULL_ROWS * P].rearrange(
                            "(p j) -> p j", j=P)).then_inc(edges_in, 16)
                        sp.dma_start(rows[LAST_ROWS:LAST_ROWS + 1, BLOCKS - 1, 0:TAIL],
                                     dram_list[FULL_ROWS * P:E].rearrange("(p j) -> p j", p=1)).then_inc(edges_in, 16)
                    for m, w in enumerate((Wq, Wk, Wv)):
                        sp.dma_start(w_sb[m][:, :, :], w.rearrange("(c p) n -> p c n", p=P)).then_inc(weights_in[m], 16)
                    sp.wait_ge(rows_ready, 4)
                    sp.dma_start(key_rows.rearrange("(b p) f -> p b f", p=BROWS), keys_b[:, :, :]).then_inc(tabled, 16)
                    by_head = breaks_rows.rearrange("(b p h) f -> h p b f", p=BROWS, h=H)
                    for h in range(H):
                        sp.dma_start(by_head[h], breaks[:, :, :]).then_inc(tabled, 16)
                    sp.dma_start(starts_rows.rearrange("(b p) f -> p b f", p=BROWS), starts[:, :, :]).then_inc(tabled, 16)
                    sp.dma_start(parts[NULL_A:NULL_A + 1, :], null_row[:, :]).then_inc(tabled, 16)
                    sp.dma_start(firsts[NULL_B:NULL_B + 1, :], null_row[:, :]).then_inc(tabled, 16)
                    sp.wait_ge(tabled, 12 * 16)

                @block.gpsimd
                def _(g):
                    chain = Chain(g, consts)
                    chain(g.memset(ident[:, :], 0.0))
                    chain(g.affine_select(out=ident[:, :], in_=ident[:, :], compare_op=ALU.not_equal, fill=1.0,
                                          base=0, pattern=[[-1, P]], channel_multiplier=1))
                    chain(g.memset(ones_row[:, :], 1.0))
                    chain(g.memset(ones_b[:, :], 1.0))
                    chain(g.iota(iota_row[:, :], pattern=[[1, P]], base=0, channel_multiplier=0,
                                 allow_small_or_imprecise_dtypes=True))
                    chain(g.iota(node_id[:, 0:NT - 1], pattern=[[P, NT - 1]], base=0, channel_multiplier=1,
                                 allow_small_or_imprecise_dtypes=True))
                    chain(g.iota(node_id[:, NT - 1:NT], pattern=[[0, 1]], base=LAST_START, channel_multiplier=1,
                                 allow_small_or_imprecise_dtypes=True))
                    chain(g.iota(row_i[:, :], pattern=[[0, 1]], base=0, channel_multiplier=1))
                    chain(g.iota(run_id[:, :], pattern=[[1, FEW]], base=0, channel_multiplier=0,
                                 allow_small_or_imprecise_dtypes=True))
                    chain(g.iota(group_runs[:, :], pattern=[[FEW, GT]], base=0, channel_multiplier=0,
                                 allow_small_or_imprecise_dtypes=True))
                    chain(g.iota(minus_p[:, :], pattern=[[0, 1]], base=0, channel_multiplier=-1,
                                 allow_small_or_imprecise_dtypes=True))
                    for m in range(3):
                        g.wait_ge(w_high_ready, m + 1)
                        g.tensor_tensor(out=w_rest[m][:, :, :], in0=w_sb[m][:, :, :], in1=w_high[m][:, :, :].bitcast(f32),
                                        op=ALU.subtract).then_inc(w_split, 1)

                @block.scalar
                def _(act):
                    for m in range(3):
                        act.wait_ge(weights_in[m], 16)
                        act.activation(w_high[m][:, :, :], w_sb[m][:, :, :], ACT.Copy).then_inc(w_high_ready, 1)

                @block.vector
                def _(v):
                    chain = Chain(v, d1)
                    v.memset(src_i[:, BLOCKS - 1, :], 0).then_inc(padded, 1)
                    v.memset(dst_i[:, BLOCKS - 1, :], N).then_inc(padded, 1)
                    chain(v.memset(null_row[:, :], 0.0))
                    v.memset(null_row[:, DM + H:W], -BIG).then_inc(rows_ready, 1)
                    chain(v.memset(ones[:, :], 1.0))
                    chain(v.memset(begins[:, :, :], 1.0))
                    v.wait_ge(edges_in, 96)
                    chain(v.tensor_copy(src_f[:, :, :], src_i[:, :, :]))
                    chain(v.tensor_copy(dst_f[:, :, :], dst_i[:, :, :]))
                    chain(v.tensor_tensor(out=begins[:, :, 1:P], in0=dst_f[:, :, 1:P], in1=dst_f[:, :, 0:P - 1],
                                          op=ALU.not_equal))
                    v.tensor_scalar(out=breaks[:, :, :], in0=begins[:, :, :], scalar1=-BIG, scalar2=None,
                                    op0=ALU.mult).then_inc(rows_ready, 1)
                    chain(v.tensor_scalar(out=starts[:, :, :], in0=begins[:, :, 0:P], scalar1=-FAR, scalar2=FAR,
                                          op0=ALU.mult, op1=ALU.add))
                    chain(v.tensor_tensor(out=starts[:, :, :], in0=starts[:, :, :], in1=dst_f[:, :, :], op=ALU.add))
                    v.memset(starts[:, :, 0:1], FAR).then_inc(rows_ready, 1)
                    for b in range(BLOCKS):
                        chain(v.tensor_tensor_scan(out=runs[:, b, :], data0=ones[:, :], data1=begins[:, b, 0:P],
                                                   initial=-1.0, op0=ALU.mult, op1=ALU.add))
                    v.wait_ge(consts, 11)
                    chain(v.tensor_scalar(out=row_i[:, :], in0=row_i[:, :], scalar1=GT - 1, scalar2=None,
                                          op0=ALU.bitwise_and))
                    chain(v.tensor_copy(row_key[:, :], row_i[:, :]))
                    chain(v.tensor_scalar(out=row_key[:, :], in0=row_key[:, :], scalar1=float(FEW), scalar2=None,
                                          op0=ALU.mult))
                    chain(v.tensor_scalar(out=keys[:, :, :], in0=runs[:, :, :], scalar1=row_key[:, 0:1], scalar2=None,
                                          op0=ALU.add))
                    v.tensor_copy(keys_b[:, :, :], keys[:, :, :]).then_inc(rows_ready, 1)
                    chain(v.tensor_tensor(out=begin_dst[:, :, :], in0=begins[:, :, 0:P], in1=dst_f[:, :, :], op=ALU.mult))
                    for b in range(BLOCKS):
                        v.wait_ge(turned, b + 1)
                        t = bank[b % 2][:, 0:4 * BROWS].rearrange("p (a t) -> p a t", a=4)
                        cols = slice(b * BROWS, (b + 1) * BROWS)
                        v.tensor_copy(edge_nodes[:, cols, 0], t[:, 0, :]).then_inc(turned_used, 1)
                        v.tensor_scalar(out=edge_nodes[:, cols, 1], in0=t[:, 1, :], scalar1=float(N - 1),
                                        scalar2=None, op0=ALU.min).then_inc(turned_used, 1)
                        v.tensor_copy(edge_runs[:, cols, 0], t[:, 2, :]).then_inc(turned_used, 1)
                        v.tensor_copy(edge_runs[:, cols, 1], t[:, 3, :]).then_inc(turned_used, 1)
                        v.tensor_copy(first_row[:, cols], t[0:1, 1, :]).then_inc(turned_used, 1)
                    v.wait_ge(turned_used, 5 * BLOCKS)
                    v.wait_ge(spread, 1)
                    half = TILES // 2
                    chain(v.tensor_copy(first_dst[:, 0:half], bank[2][:, 0:half]))
                    chain(v.tensor_copy(first_dst[:, half:TILES], bank[3][:, 0:half]))
                    chain(v.tensor_tensor(out=last_f[96:P, :, :],
                                          in0=edge_runs[96:P, :, 0].rearrange("p (g t) -> p g t", t=GT),
                                          in1=group_runs[96:P, :].unsqueeze(1).to_broadcast([32, GROUPS, GT]),
                                          op=ALU.subtract))
                    chain(v.tensor_reduce(out=most_f[96:P, :], in_=last_f[96:P, :, :], axis=AX.XY, op=ALU.max))
                    chain(v.tensor_copy(most_runs[96:P, :], most_f[96:P, :]))

                @block.tensor
                def _(pe):
                    pe.wait_ge(consts, 11)
                    pe.wait_ge(d1, 12 + BLOCKS)
                    for b in range(BLOCKS):
                        if b >= 2:
                            pe.wait_ge(turned_used, 5 * (b - 1))
                        for a, rows in enumerate((src_f[:, b, :], dst_f[:, b, :], keys[:, b, :], begins[:, b, 0:P])):
                            last = pe.transpose(bank[b % 2][:, a * BROWS:(a + 1) * BROWS], rows, ident[0:BROWS, 0:BROWS])
                        last.then_inc(turned, 1)
                    pe.wait_ge(turned_used, 5 * BLOCKS)
                    half = TILES // 2
                    pe.matmul(bank[2][:, 0:half], ones_row[:, :], first_row[:, 0:half], start=True, stop=True)
                    pe.matmul(bank[3][:, 0:half], ones_row[:, :], first_row[:, half:TILES], start=True,
                              stop=True).then_inc(spread, 1)

        end_of_stage()

        with ExitStack() as st:
            xt = [sb(f"xt{i}", [P, DM], f32, st) for i in range(2)]
            xT_high = [sb(f"xT_high{i}", [P, 4, P], f32r, st) for i in range(2)]
            xT_rest = [sb(f"xT_rest{i}", [P, 4, P], f32r, st) for i in range(2)]
            q_out = [sb(f"q_out{i}", [P, DM], f32, st) for i in range(2)]
            kv_out = [sb(f"kv_out{i}", [P, 2 * DM], f32, st) for i in range(2)]
            below = sb("below", [P, TILES], f32, st)
            nid = [sb(f"nid{i}", [P, 1], f32, st) for i in range(2)]
            cnt = [sb(f"cnt{i}", [P, 2], f32, st) for i in range(2)]
            tile_i = [sb(f"tile_i{i}", [P, 1], i32, st) for i in range(2)]
            tile_f = [sb(f"tile_f{i}", [P, 1], f32, st) for i in range(2)]
            row_of = [sb(f"row_of{i}", [P, P], f32, st) for i in range(2)]
            counts = sb("counts", [P, NT, 4], f32, st)
            used = sb("used", [P, NT, 3], f32, st)
            over = sb("over", [P, NT], f32, st)
            row_f = sb("row_f", [P, NT, 3], f32, st)
            x_in = [sem(f"x_in{i}") for i in range(2)]
            x_turned = sem("x_turned")
            xT_high_ready, xT_ready = sem("xT_high_ready"), sem("xT_ready")
            qkv_done = sem("qkv_done")
            q_ready = sem("q_ready")
            k_ready = sem("k_ready")
            v_ready = sem("v_ready")
            q_stored = [sem(f"q_stored{i}") for i in range(2)]
            kv_stored = [sem(f"kv_stored{i}") for i in range(2)]
            tile_ready = sem("tile_ready")
            go = sem("go")
            row_in = [sem(f"row_in{i}") for i in range(2)]
            d2 = sem("d2")
            run_dst_ready, runs_stored, runs_back, runs_turned = (
                sem(n) for n in ("run_dst_ready", "runs_stored", "runs_back", "runs_turned"))
            FIRST = 2 + FEW

            def rows_at(t):
                return slice(LAST_START, N) if isinstance(t, int) and t == NT - 1 else ds(t * P, P)

            def steps(eng, one):
                one(0, 0)
                one(1, 1)
                with eng.Fori(2, NT - 2, 2) as t:
                    one(t, 0)
                    one(t + 1, 1)
                one(NT - 1, 0)

            def nth(t, par):
                return t - par + 2

            with nc.Block() as block:
                @block.sync
                def _(sp):

                    def load(t, par):
                        if not isinstance(t, int) or t >= 2:
                            sp.wait_ge(x_turned, t - 1)
                        sp.dma_start(xt[par][:, :], x[rows_at(t), :]).then_inc(x_in[par], 16)

                    def store(t, par):
                        if isinstance(t, int) and t == NT - 1:
                            sp.wait_ge(q_stored[1], 8 * (NT - 1))
                            sp.wait_ge(kv_stored[1], 8 * (NT - 1))
                        sp.wait_ge(q_ready, t + 1)
                        sp.dma_start(q_rows[rows_at(t), :], q_out[par][:, :]).then_inc(q_stored[par], 16)
                        sp.wait_ge(k_ready, t + 1)
                        sp.wait_ge(v_ready, t + 1)
                        sp.dma_start(kv_rows[rows_at(t), :], kv_out[par][:, :]).then_inc(kv_stored[par], 16)

                    load(0, 0)
                    load(1, 1)

                    def pair(t):
                        load(t, 0)
                        store(t - 2, 0)
                        load(t + 1, 1)
                        store(t - 1, 1)

                    for t in range(2, FIRST + 4, 2):
                        pair(t)
                    sp.wait_ge(run_dst_ready, 1)
                    sp.dma_start(run_rows.rearrange("(b p) f -> p b f", p=BROWS), run_dst[:, :, :]).then_inc(runs_stored, 16)
                    pair(FIRST + 4)
                    sp.wait_ge(runs_stored, 16)
                    sp.dma_start(run_turn[:, :], run_rows.rearrange("(g t) f -> g (t f)", t=GT)).then_inc(runs_back, 16)
                    with sp.Fori(FIRST + 6, NT - 2, 2) as t:
                        pair(t)
                    load(NT - 1, 0)
                    store(NT - 3, 0)
                    store(NT - 2, 1)
                    store(NT - 1, 0)
                    sp.wait_ge(q_stored[0], 16 * (NT // 2 + 1))
                    sp.wait_ge(kv_stored[0], 16 * (NT // 2 + 1))

                @block.tensor
                def _(pe):
                    def turn(t, par):
                        pe.wait_ge(x_in[par], 8 * nth(t, par))
                        if not isinstance(t, int) or t >= 2:
                            pe.wait_ge(xT_ready, t - 1)
                        for c in range(4):
                            last = pe.transpose(bank[par][:, c * P:(c + 1) * P], xt[par][:, c * P:(c + 1) * P], ident[:, :])
                        last.then_inc(x_turned, 1)

                    def project(t, par):
                        pe.wait_ge(xT_ready, t + 1)
                        if not isinstance(t, int) or t >= 2:
                            pe.wait_ge(q_ready, t - 1)
                            pe.wait_ge(k_ready, t - 1)
                            pe.wait_ge(v_ready, t - 1)
                        for m in range(3):
                            pairs = ((xT_high[par], w_high[m]), (xT_rest[par], w_high[m]), (xT_high[par], w_rest[m]))
                            for n, (a, b) in enumerate(pairs):
                                for c in range(4):
                                    last = pe.matmul(bank[2 + 3 * par + m][:, :], a[:, c, :], b[:, c, :],
                                                     start=n == 0 and c == 0, stop=n == 2 and c == 3)
                            last.then_inc(qkv_done, 1)

                    turn(0, 0)
                    turn(1, 1)
                    project(0, 0)
                    with pe.Fori(2, NT - 2, 2) as t:
                        turn(t, 0)
                        project(t - 1, 1)
                        turn(t + 1, 1)
                        project(t, 0)
                    turn(NT - 1, 0)
                    project(NT - 2, 1)
                    project(NT - 1, 0)
                    pe.wait_ge(runs_back, 16)
                    pe.transpose(bank[1][:, 0:GROUPS], run_turn[:, :], ident[0:GROUPS, 0:GROUPS]).then_inc(runs_turned, 1)

                @block.scalar
                def _(act):
                    def evacuate(t, par):
                        late = not isinstance(t, int) or t >= 2
                        act.wait_ge(qkv_done, 3 * t + 1)
                        if late:
                            act.wait_ge(q_stored[par], 8 * nth(t, par) - 16)
                        act.activation(q_out[par][:, :], bank[2 + 3 * par][:, :], ACT.Copy,
                                       scale=1.0 / DK ** 0.5).then_inc(q_ready, 1)
                        act.wait_ge(qkv_done, 3 * t + 2)
                        if late:
                            act.wait_ge(kv_stored[par], 8 * nth(t, par) - 16)
                        act.activation(kv_out[par][:, 0:DM], bank[3 + 3 * par][:, :], ACT.Copy).then_inc(k_ready, 1)
                        act.wait_ge(qkv_done, 3 * t + 3)
                        act.activation(kv_out[par][:, DM:2 * DM], bank[4 + 3 * par][:, :], ACT.Copy).then_inc(v_ready, 1)

                    def high_xT(t, par):
                        act.wait_ge(x_turned, t + 1)
                        if not isinstance(t, int) or t >= 2:
                            act.wait_ge(qkv_done, 3 * t - 3)
                        act.activation(xT_high[par][:, :, :], bank[par][:, :].rearrange("p (c n) -> p c n", c=4),
                                       ACT.Copy).then_inc(xT_high_ready, 1)

                    high_xT(0, 0)
                    high_xT(1, 1)
                    evacuate(0, 0)
                    with act.Fori(2, NT - 2, 2) as t:
                        high_xT(t, 0)
                        evacuate(t - 1, 1)
                        high_xT(t + 1, 1)
                        evacuate(t, 0)
                    high_xT(NT - 1, 0)
                    evacuate(NT - 2, 1)
                    evacuate(NT - 1, 0)

                @block.vector
                def _(v):
                    chain = Chain(v, d2)

                    def rest_xT(t, par):
                        v.wait_ge(xT_high_ready, t + 1)
                        if not isinstance(t, int) or t >= 2:
                            v.wait_ge(qkv_done, 3 * t - 3)
                        v.tensor_tensor(out=xT_rest[par][:, :, :], in0=bank[par][:, :].rearrange("p (c n) -> p c n", c=4),
                                        in1=xT_high[par][:, :, :].bitcast(f32), op=ALU.subtract).then_inc(xT_ready, 1)

                    def count_tiles(t, par):
                        chain(v.tensor_copy(nid[par][:, :], node_id[:, ds(t, 1)]))
                        for a, op in ((0, ALU.is_lt), (1, ALU.is_le)):
                            chain(v.tensor_scalar(out=below[:, :], in0=first_dst[:, :], scalar1=nid[par][:, 0:1],
                                                  scalar2=None, op0=op))
                            chain(v.tensor_reduce(out=cnt[par][:, a:a + 1], in_=below[:, :], axis=AX.X, op=ALU.add))
                        chain(v.tensor_copy(counts[:, ds(t, 1), 0:2], cnt[par][:, :].unsqueeze(1)))
                        chain(v.tensor_scalar(out=tile_f[par][:, :], in0=cnt[par][:, 0:1], scalar1=-1.0, scalar2=0.0,
                                              op0=ALU.add, op1=ALU.max))
                        chain(v.tensor_copy(tile_i[par][:, :], tile_f[par][:, :]))
                        v.tensor_copy(tile_f[par][:, :], tile_f[par][:, :]).then_inc(tile_ready, 1)

                    def count_runs(t, par):
                        v.wait_ge(row_in[par], 8 * nth(t, par))
                        for a, op in ((0, ALU.is_lt), (1, ALU.is_le)):
                            chain(v.tensor_scalar(out=below[:, 0:P], in0=row_of[par][:, :], scalar1=nid[par][:, 0:1],
                                                  scalar2=None, op0=op))
                            chain(v.tensor_reduce(out=cnt[par][:, a:a + 1], in_=below[:, 0:P], axis=AX.X, op=ALU.add))
                        chain(v.tensor_copy(counts[:, ds(t, 1), 2:4], cnt[par][:, :].unsqueeze(1)))

                    COUNT = 8 + 5
                    rest_xT(0, 0)
                    rest_xT(1, 1)
                    count_tiles(0, 0)
                    count_tiles(1, 1)
                    count_runs(0, 0)
                    for t in range(2, FIRST):
                        r = t - 2
                        rest_xT(t, t % 2)
                        count_tiles(t, t % 2)
                        count_runs(t - 1, 1 - t % 2)
                        chain(v.scalar_tensor_tensor(out=hit[:, :, :], in0=runs[:, :, :], scalar=float(r),
                                                     in1=begin_dst[:, :, :], op0=ALU.is_equal, op1=ALU.mult))
                        chain(v.tensor_reduce(out=run_dst[:, :, r], in_=hit[:, :, :], axis=AX.X, op=ALU.add))
                    for b in range(BLOCKS):
                        chain(v.tensor_scalar(out=missing[:, b, :], in0=run_id[:, :], scalar1=runs[:, b, P - 1:P],
                                              scalar2=FAR, op0=ALU.is_gt, op1=ALU.mult))
                    v.tensor_tensor(out=run_dst[:, :, :], in0=run_dst[:, :, :], in1=missing[:, :, :],
                                    op=ALU.add).then_inc(run_dst_ready, 1)
                    before = chain.n
                    with v.Fori(FIRST, NT - 2, 2) as t:
                        for k in range(2):
                            chain.base, chain.n = (t + k - FIRST) * COUNT + before, 0
                            rest_xT(t + k, k)
                            count_tiles(t + k, k)
                            count_runs(t + k - 1, 1 - k)
                            assert chain.n == COUNT
                    chain.base, chain.n = 0, before + (NT - 1 - FIRST) * COUNT
                    rest_xT(NT - 1, 0)
                    count_tiles(NT - 1, 0)
                    count_runs(NT - 2, 1)
                    count_runs(NT - 1, 0)
                    chain(v.tensor_tensor(out=used[:, :, 0], in0=counts[:, :, 3], in1=counts[:, :, 2], op=ALU.is_gt))
                    chain(v.tensor_tensor(out=used[:, :, 1], in0=counts[:, :, 1], in1=counts[:, :, 0], op=ALU.is_gt))
                    chain(v.tensor_scalar(out=over[:, :], in0=counts[:, :, 3], scalar1=float(FEW), scalar2=None,
                                          op0=ALU.is_ge))
                    chain(v.tensor_tensor(out=used[:, :, 2], in0=used[:, :, 0], in1=over[:, :], op=ALU.mult))
                    chain(v.tensor_tensor(out=used[:, :, 0], in0=used[:, :, 0], in1=used[:, :, 2], op=ALU.subtract))
                    for a, rows, run_0, none in ((0, FEW, 0, NULL_A), (2, MORE, FEW, NULL_MORE)):
                        chain(v.tensor_scalar(out=row_f[:, :, a], in0=counts[:, :, 0], scalar1=float(rows),
                                              scalar2=float(-rows - run_0 - none), op0=ALU.mult, op1=ALU.add))
                        chain(v.tensor_tensor(out=row_f[:, :, a], in0=row_f[:, :, a], in1=counts[:, :, 3], op=ALU.add))
                    chain(v.tensor_scalar(out=row_f[:, :, 1], in0=counts[:, :, 1], scalar1=float(-1 - NULL_B),
                                          scalar2=None, op0=ALU.add))
                    chain(v.tensor_tensor(out=row_f[:, :, :], in0=row_f[:, :, :], in1=used[:, :, :], op=ALU.mult))
                    for a, none in ((0, NULL_A), (1, NULL_B), (2, NULL_MORE)):
                        chain(v.tensor_scalar(out=row_f[:, :, a], in0=row_f[:, :, a], scalar1=float(none), scalar2=None,
                                              op0=ALU.add))
                    chain(v.tensor_copy(node_rows[:, :, :], row_f[:, :, :]))
                    v.wait_ge(runs_turned, 1)
                    chain(v.tensor_copy(run_nodes[:, :], bank[1][:, 0:GROUPS]))

                @block.gpsimd
                def _(g):
                    top = g.to_reg(TILES - 1)

                    def fetch(t, par):
                        g.wait_ge(tile_ready, t + 1)
                        g.sem_inc(go, 1)
                        g.indirect_dma_start(out=row_of[par][:, :], out_offset=None, in_=starts_rows[:, :],
                                             in_offset=bass.IndirectOffsetOnAxis(ap=tile_i[par][:, 0:1], axis=0),
                                             bounds_check=top, oob_is_err=False).then_inc(row_in[par], 16)

                    steps(g, fetch)

        early.close()
        end_of_stage()

        with ExitStack() as st:
            kv = [sb(f"g_kv{i}", [P, GT, 2 * DM], f32, st) for i in range(NSLOT)]
            qd = [sb(f"g_qd{i}", [P, DM], f32, st) for i in range(4)]
            prod = [sb(f"g_prod{i}", [P, DM], f32, st) for i in range(3)]
            score = [sb(f"g_score{i}", [P, GT, H], f32, st) for i in range(NSLOT)]
            idx = [sb(f"g_idx{i}", [P, GT, 2], i32, st) for i in range(NSLOT)]
            runs_g = [sb(f"g_runs_g{i}", [P, GT, 2], f32, st) for i in range(NSLOT)]
            breaks_g = [sb(f"g_breaks_g{i}", [GT * H, 132], f32, st) for i in range(NSLOT)]
            up = [sb(f"g_up{i}", [GT * H, P], f32, st) for i in range(2)]
            peak = [sb(f"g_peak{i}", [GT * H, P], f32, st) for i in range(2)]
            below_peak = [sb(f"g_below_peak{i}", [P, GT, H], f32, st) for i in range(NSLOT)]
            zm = [sb(f"g_zm{i}", [P, GT, 2 * H], f32, st) for i in range(NSLOT)]
            wv = [sb(f"g_wv{i}", [P, DM], f32, st) for i in range(4)]
            pick = [sb(f"g_pick{i}", [P, P], f32, st) for i in range(4)]
            part_sb = [sb(f"g_part_sb{i}", [P, W], f32, st) for i in range(4)]

            kv_in = [[sem(f"g_kv_in{s}_{j}") for j in range(GT)] for s in range(NSLOT)]
            q_in = [sem(f"g_q_in{i}") for i in range(4)]
            breaks_in = [sem(f"g_breaks_in{i}") for i in range(NSLOT)]
            idx_ready = sem("g_idx_ready")
            issue = sem("g_issue")
            prod_done = sem("g_prod_done")
            score_done = sem("g_score_done")
            score_turned = sem("g_score_turned")
            up_done = sem("g_up_done")
            peak_done = sem("g_peak_done")
            peak_back = sem("g_peak_back")
            below_ready = sem("g_below_ready")
            m_ready = sem("g_m_ready")
            z_ready = sem("g_z_ready")
            runs_ready = sem("g_runs_ready")
            pick_ready = sem("g_pick_ready")
            wv_ready = sem("g_wv_ready")
            sums_done = sem("g_sums_done")
            zsum_done = sem("g_zsum_done")
            part_ready = sem("g_part_ready")
            part_out = [sem(f"g_part_out{i}") for i in range(4)]
            part_more = [sem(f"g_part_more{i}") for i in range(4)]
            pe_turn = sem("g_pe_turn")

            def late(s, k):
                return not isinstance(s, int) or s >= k

            def group_steps(eng, one):
                for s in range(NSLOT):
                    one(s, s)
                with eng.Fori(NSLOT, GROUPS - NSLOT + 1, NSLOT) as s:
                    for k in range(NSLOT):
                        one(s + k, k)

            def uses(s, k):
                if isinstance(s, int):
                    return 16 * (s // NSLOT + 1)
                return None

            with nc.Block() as block:
                @block.gpsimd
                def _(g):
                    with g.If(g.value_load(most_runs[P - 1:P, 0:1]) >= FEW):
                        top = g.to_reg(N - 1)

                        def gather(s, k):
                            if late(s, NSLOT):
                                g.wait_ge(wv_ready, (s - (NSLOT - 1)) * GT)
                                g.sem_inc(issue, 1)
                            g.tensor_copy(idx[k][:, :, :], edge_nodes[:, ds(s * GT, GT), :]).then_inc(idx_ready, 1)
                            g.wait_ge(idx_ready, s + 1)
                            g.sem_inc(issue, 1)
                            for j in range(GT):
                                g.indirect_dma_start(out=kv[k][:, j, :], out_offset=None, in_=kv_rows[:, :],
                                                     in_offset=bass.IndirectOffsetOnAxis(ap=idx[k][:, j, 0:1], axis=0),
                                                     bounds_check=top, oob_is_err=False).then_inc(kv_in[k][j], 16)
                                if late(s, 1) or j >= 4:
                                    g.wait_ge(prod_done, s * GT + (j - 3))
                                    g.sem_inc(issue, 1)
                                g.indirect_dma_start(out=qd[j % 4][:, :], out_offset=None, in_=q_rows[:, :],
                                                     in_offset=bass.IndirectOffsetOnAxis(ap=idx[k][:, j, 1:2], axis=0),
                                                     bounds_check=top, oob_is_err=False).then_inc(q_in[j % 4], 16)

                        group_steps(g, gather)

                @block.vector
                def _(v):
                    with v.If(v.value_load(most_runs[P - 1:P, 0:1]) >= FEW):
                        def product(s, k, j, r):
                            v.wait_ge(kv_in[k][j], r)
                            v.wait_ge(q_in[j % 4], s * 32 + (16 * (j // 4) + 16))
                            if late(s, 1) or j >= 3:
                                v.wait_ge(score_done, s * GT + (j - 2))
                            v.tensor_tensor(out=prod[(k * GT + j) % 3][:, :], in0=kv[k][:, j, 0:DM], in1=qd[j % 4][:, :],
                                            op=ALU.mult).then_inc(prod_done, 1)

                        def reduce(s, k, j):
                            v.wait_ge(prod_done, s * GT + (j + 1))
                            if j == 0 and late(s, NSLOT):
                                v.wait_ge(below_ready, s - (NSLOT - 1))
                            v.tensor_reduce(out=score[k][:, j, :],
                                            in_=prod[(k * GT + j) % 3][:, :].rearrange("p (h d) -> p h d", h=H),
                                            axis=AX.X, op=ALU.add).then_inc(score_done, 1)

                        def scans(s, k, r):
                            turned = bank[3][0:GT * H, 0:P]
                            v.wait_ge(score_turned, s + 1)
                            v.wait_ge(breaks_in[k], r)
                            if late(s, 1):
                                v.wait_ge(peak_done, s)
                            v.tensor_tensor_scan(out=up[0][:, :], data0=breaks_g[k][:, 0:P], data1=turned, initial=-BIG,
                                                 op0=ALU.add, op1=ALU.max).then_inc(up_done, 1)
                            v.wait_ge(up_done, s + 1)
                            if late(s, 1):
                                v.wait_ge(peak_back, s)
                            v.tensor_tensor_scan(out=peak[0][:, ::-1], data0=breaks_g[k][:, 1:P + 1][:, ::-1],
                                                 data1=up[0][:, ::-1], initial=-BIG,
                                                 op0=ALU.add, op1=ALU.max).then_inc(peak_done, 1)

                        def subtract(s, k):
                            m = bank[4][:, 0:GT * H].rearrange("p (t h) -> p t h", t=GT)
                            v.wait_ge(peak_back, s + 1)
                            if late(s, NSLOT):
                                v.wait_ge(z_ready, s - (NSLOT - 1))
                                v.wait_ge(zsum_done, (s - (NSLOT - 1)) * GT)
                            v.tensor_tensor(out=below_peak[k][:, :, :], in0=score[k][:, :, :], in1=m,
                                            op=ALU.subtract).then_inc(below_ready, 1)
                            v.tensor_copy(runs_g[k][:, :, :], edge_runs[:, ds(s * GT, GT), :]).then_inc(runs_ready, 1)
                            v.wait_ge(runs_ready, s + 1)
                            v.tensor_tensor(out=zm[k][:, :, H:2 * H], in0=m,
                                            in1=runs_g[k][:, :, 1:2].to_broadcast([P, GT, H]), op=ALU.mult).then_inc(m_ready, 1)

                        def weigh(s, k, j):
                            if late(s, 1) or j >= 4:
                                v.wait_ge(zsum_done, s * GT + (j - 3))
                            v.tensor_scalar(out=pick[j % 4][:, :], in0=iota_row[:, :], scalar1=float(FEW * j),
                                            scalar2=runs_g[k][:, j, 0:1], op0=ALU.add, op1=ALU.is_equal).then_inc(pick_ready, 1)
                            if j == 0:
                                v.wait_ge(z_ready, s + 1)
                            v.tensor_tensor(out=wv[j % 4][:, :].rearrange("p (h d) -> p h d", h=H),
                                            in0=kv[k][:, j, DM:2 * DM].rearrange("p (h d) -> p h d", h=H),
                                            in1=zm[k][:, j, 0:H].unsqueeze(2).to_broadcast([P, H, DK]),
                                            op=ALU.mult).then_inc(wv_ready, 1)

                        def step(s, k, r, rp):
                            score_it = not isinstance(s, int) or s < GROUPS
                            weigh_it = late(s, 1)
                            p = (k - 1) % NSLOT
                            after = {1: lambda: scans(s - 1, p, rp), 3: lambda: subtract(s - 1, p)}
                            take = {5: (0, 1), 6: (2, 3, 4), 7: (5, 6, 7)}
                            if score_it:
                                product(s, k, 0, r)
                            for j in range(GT):
                                if score_it:
                                    if j + 1 < GT:
                                        product(s, k, j + 1, r)
                                    reduce(s, k, j)
                                if weigh_it:
                                    if j in after:
                                        after[j]()
                                    for i in take.get(j, ()):
                                        weigh(s - 1, p, i)

                        for s in range(NSLOT):
                            step(s, s, 16, 16)
                        with v.Fori(1, GROUPS // NSLOT) as i:
                            for k in range(NSLOT):
                                step(i * NSLOT + k, k, i * 16 + 16, i * 16 if k == 0 else i * 16 + 16)
                        step(GROUPS, 0, 0, 16 * (GROUPS // NSLOT))

                @block.tensor
                def _(pe):
                    with pe.If(pe.value_load(most_runs[P - 1:P, 0:1]) >= FEW):
                        def turn_scores(s, k):
                            pe.wait_ge(score_done, s * GT + GT)
                            if late(s, 1):
                                pe.wait_ge(up_done, s)
                            pe.sem_inc(pe_turn, 1)
                            pe.transpose(bank[3][0:GT * H, 0:P], score[k][:, :, :].rearrange("p t h -> p (t h)"),
                                         ident[:, :]).then_inc(score_turned, 1)

                        def turn_back(s, k):
                            pe.wait_ge(peak_done, s + 1)
                            if late(s, 1):
                                pe.wait_ge(m_ready, s)
                            pe.sem_inc(pe_turn, 1)
                            pe.transpose(bank[4][:, 0:GT * H], peak[0][:, :], ident[0:GT * H, 0:GT * H]).then_inc(peak_back, 1)

                        def sums(s, k, j):
                            pe.wait_ge(wv_ready, s * GT + (j + 1))
                            if late(s, 1) or j >= 2:
                                pe.wait_ge(part_ready, s * (2 * GT) + (2 * j - 2))
                            if j == 0:
                                pe.wait_ge(m_ready, s + 1)
                            pe.matmul(bank[j % 2][:, :], pick[j % 4][:, :], wv[j % 4][:, :], start=True,
                                      stop=True).then_inc(sums_done, 1)
                            pe.matmul(bank[5 + j % 2][:, 0:2 * H], pick[j % 4][:, :], zm[k][:, j, :], start=True,
                                      stop=True).then_inc(zsum_done, 1)

                        def step(s, k):
                            if not isinstance(s, int) or s < GROUPS:
                                pass
                            p = (k - 1) % NSLOT
                            if late(s, 1):
                                turn_scores(s - 1, p)
                                turn_back(s - 1, p)
                                for j in range(GT):
                                    sums(s - 1, p, j)

                        for s in range(NSLOT):
                            step(s, s)
                        with pe.Fori(NSLOT, GROUPS - NSLOT + 1, NSLOT) as s:
                            for k in range(NSLOT):
                                step(s + k, k)
                        step(GROUPS, 0)

                @block.scalar
                def _(act):
                    with act.If(act.value_load(most_runs[P - 1:P, 0:1]) >= FEW):
                        def exps(s, k):
                            act.wait_ge(below_ready, s + 1)
                            if late(s, NSLOT):
                                act.wait_ge(zsum_done, (s - (NSLOT - 1)) * GT)
                            act.activation(zm[k][:, :, 0:H], below_peak[k][:, :, :], ACT.Exp).then_inc(z_ready, 1)

                        def evacuate(s, k, j, r):
                            act.wait_ge(sums_done, s * GT + (j + 1))
                            if r is not None:
                                act.wait_ge(part_out[j % 4], r)
                                act.wait_ge(part_more[j % 4], r)
                            act.activation(part_sb[j % 4][:, 0:DM], bank[j % 2][:, :], ACT.Copy).then_inc(part_ready, 1)
                            act.wait_ge(zsum_done, s * GT + (j + 1))
                            act.activation(part_sb[j % 4][:, DM:W], bank[5 + j % 2][:, 0:2 * H], ACT.Copy).then_inc(part_ready, 1)

                        def step(s, k):
                            exps(s, k)
                            for j in range(GT):
                                r = s * 32 + 16 * (j // 4) if late(s, 1) or j >= 4 else None
                                evacuate(s, k, j, r)

                        group_steps(act, step)

                @block.sync
                def _(sp):
                    with sp.If(sp.value_load(most_runs[P - 1:P, 0:1]) >= FEW):
                        def load_breaks(s, k):
                            if late(s, NSLOT):
                                sp.wait_ge(peak_done, s - (NSLOT - 1))
                            sp.dma_start(breaks_g[k][:, :], breaks_rows[ds(s * (GT * H), GT * H), :]).then_inc(breaks_in[k], 16)

                        def store(s, k, j):
                            sp.wait_ge(part_ready, s * (2 * GT) + (2 * j + 2))
                            sp.dma_start(parts[ds((s * GT + j) * FEW, FEW), :], part_sb[j % 4][0:FEW, :]).then_inc(part_out[j % 4], 16)
                            sp.dma_start(more_parts[ds((s * GT + j) * MORE, MORE), :], part_sb[j % 4][FEW:P, :]).then_inc(part_more[j % 4], 16)

                        load_breaks(0, 0)

                        def step(s, k):
                            nxt = (k + 1) % NSLOT
                            if not isinstance(s, int) or s + 1 < GROUPS:
                                load_breaks(s + 1, nxt)
                            for j in range(GT):
                                store(s, k, j)

                        for s in range(NSLOT):
                            step(s, s)
                        with sp.Fori(NSLOT, GROUPS - 2 * NSLOT + 1, NSLOT) as s:
                            for k in range(NSLOT):
                                step(s + k, k)
                        for k in range(NSLOT):
                            step(GROUPS - NSLOT + k, k)
                        for i in range(4):
                            sp.wait_ge(part_out[i], 16 * (TILES // 4))
                            sp.wait_ge(part_more[i], 16 * (TILES // 4))

        end_of_stage()

        with ExitStack() as st:
            three = lambda name, shape, dt=f32: [sb(f"{name}{i}", shape, dt, st) for i in range(NSLOT)]
            kv = three("kv", [P, GT, 2 * DM])
            q_f = three("q_f", [P, DM])
            q_g = three("q_g", [P, 2 * DM], f32r)
            key_row = three("key_row", [1, GT * P], bf16)
            idx = three("idx", [P, GT, 1], i32)
            q_idx = three("q_idx", [P, 1], i32)
            away = [sb(f"away{h}", [P, GT // 2 * P], bf16, st) for h in range(2)]
            expand = [[sb(f"expand{i}_{h}", [P, GT // 2 * P], f32r, st) for h in range(2)] for i in range(NSLOT)]
            prod = three("prod", [P, DM])
            score = three("score", [P, GT, H])
            runs_g = three("runs_g", [P, GT, 2])
            breaks_g = three("breaks_g", [GT * H, 132])
            up = sb("up", [GT * H, P], f32, st)
            peak = sb("peak", [GT * H, P], f32, st)
            below_peak = three("below_peak", [P, GT, H])
            zm = three("zm", [P, GT, 2 * H])
            pick = three("pick", [P, GT, P])
            wv = [sb(f"wv{j}", [P, DM], f32, st) for j in range(GT)]
            part_sb = three("part_sb", [P, W])
            KEY, TURNS, EXPANDED, SUMS, SMALL = bank[0], bank[1], bank[2:4], bank[4:6], bank[6:8]

            kv_in = [[sem(f"kv_in{i}_{j}") for j in range(GT)] for i in range(NSLOT)]
            q_in, key_in, breaks_in, part_out = (
                [sem(f"{n}{i}") for i in range(NSLOT)] for n in ("q_in", "key_in", "breaks_in", "part_out"))
            q_high, q_split = sem("q_high"), sem("q_split")
            q_clear, idx_ready, issue = sem("q_clear"), sem("idx_ready"), sem("issue")
            key_spread, away_ready, expand_ready, expanded = (
                sem("key_spread"), sem("away_ready"), sem("expand_ready"), sem("expanded"))
            prod_done, score_done, score_turned = sem("prod_done"), sem("score_done"), sem("score_turned")
            up_done, peak_done, peak_back = sem("up_done"), sem("peak_done"), sem("peak_back")
            below_ready, m_ready, z_ready, runs_ready = sem("below_ready"), sem("m_ready"), sem("z_ready"), sem("runs_ready")
            pick_ready, wv_act, wv_pool, wv_dve = sem("pick_ready"), sem("wv_act"), sem("wv_pool"), sem("wv_dve")
            sums_done, zsum_done, part_ready, pe_turn = sem("sums_done"), sem("zsum_done"), sem("part_ready"), sem("pe_turn")

            ACT_TILES, POOL_TILES, DVE_TILES = (0, 2, 4, 6), (1, 3, 5), (7,)
            AHEAD, BEHIND = 2, 2
            STEPS = GROUPS + BEHIND
            UNROLL = NSLOT * 2
            heads = lambda a: a.rearrange("p (h d) -> p h d", h=H)

            class Group:

                def __init__(self, i, k, d):
                    self.s, self.slot, self.half = i * UNROLL + k + d, (k + d) % NSLOT, (k + d) % 2
                    self.round = i * 2 + (k + d) // NSLOT
                    self.exists = not isinstance(i, int) or 0 <= self.s < GROUPS
                    self.landed = self.round * 16 + 16

                def past(self, n):
                    return not isinstance(self.s, int) or self.s >= n

                def tiles(self, n):
                    return self.s * GT + n

            def run_steps(eng, one):
                for k in range(UNROLL):
                    one(0, k)
                whole = (GROUPS - AHEAD) // UNROLL
                with eng.Fori(1, whole) as i:
                    for k in range(UNROLL):
                        one(i, k)
                for s in range(whole * UNROLL, STEPS):
                    one(s // UNROLL, s % UNROLL)

            def usual(eng):
                return eng.If(eng.value_load(most_runs[P - 1:P, 0:1]) < FEW)

            with nc.Block() as block:
                @block.sync
                def _(sp):
                    def load_keys(a):
                        if a.past(NSLOT):
                            sp.wait_ge(key_spread, a.s * 2 - 2 * (NSLOT - 1))
                        sp.dma_start(key_row[a.slot][:, :], key_rows[ds(a.tiles(0), GT), :].rearrange(
                            "t e -> (t e)").unsqueeze(0)).then_inc(key_in[a.slot], 16)

                    def step(i, k):
                        a, c, e = Group(i, k, AHEAD), Group(i, k, 0), Group(i, k, -BEHIND)
                        if a.exists:
                            load_keys(a)
                        if c.exists:
                            if c.past(NSLOT):
                                sp.wait_ge(peak_done, c.s - (NSLOT - 1))
                            sp.dma_start(breaks_g[c.slot][:, :],
                                         breaks_rows[ds(c.s * (GT * H), GT * H), :]).then_inc(breaks_in[c.slot], 16)
                        if e.exists:
                            sp.wait_ge(part_ready, e.s * 2 + 2)
                            sp.dma_start(parts[ds(e.s * P, P), :], part_sb[e.slot][:, :]).then_inc(part_out[e.slot], 16)

                    with usual(sp):
                        for k in range(AHEAD):
                            load_keys(Group(0, k, 0))
                        run_steps(sp, step)
                        for n in range(NSLOT):
                            sp.wait_ge(part_out[n], 16 * (GROUPS // NSLOT))

                @block.gpsimd
                def _(g):
                    def gather_queries(a, top):
                        if a.past(NSLOT):
                            g.wait_ge(prod_done, a.tiles(-(NSLOT - 1) * GT))
                            g.wait_ge(q_split, a.s - (NSLOT - 1))
                            g.sem_inc(issue, 1)
                        g.tensor_copy(q_idx[a.slot][:, :], run_nodes[:, ds(a.s, 1)]).then_inc(idx_ready, 1)
                        g.tensor_copy(idx[a.slot][:, :, :], edge_nodes[:, ds(a.tiles(0), GT), 0:1]).then_inc(idx_ready, 1)
                        g.wait_ge(idx_ready, a.s * 2 + 2)
                        g.sem_inc(issue, 1)
                        g.indirect_dma_start(out=q_f[a.slot][:, :], out_offset=None,
                                             in_=q_rows[:, :],
                                             in_offset=bass.IndirectOffsetOnAxis(ap=q_idx[a.slot][:, 0:1], axis=0),
                                             bounds_check=top, oob_is_err=False).then_inc(q_in[a.slot], 16)

                    def gather(a, j, top):
                        if a.past(NSLOT):
                            g.wait_ge(sums_done, a.tiles(j + 1 - NSLOT * GT))
                            g.sem_inc(issue, 1)
                        g.indirect_dma_start(out=kv[a.slot][:, j, :], out_offset=None, in_=kv_rows[:, :],
                                             in_offset=bass.IndirectOffsetOnAxis(ap=idx[a.slot][:, j, 0:1], axis=0),
                                             bounds_check=top, oob_is_err=False).then_inc(kv_in[a.slot][j], 16)

                    def weigh(b, j):
                        g.wait_ge(z_ready, b.s + 1)
                        if b.past(1):
                            g.wait_ge(sums_done, b.tiles(j + 1 - GT))
                        g.tensor_tensor(out=heads(wv[j][:, :]), in0=heads(kv[b.slot][:, j, DM:2 * DM]),
                                        in1=zm[b.slot][:, j, 0:H].unsqueeze(2).to_broadcast([P, H, DK]),
                                        op=ALU.mult).then_inc(wv_pool, 1)

                    def step(i, k, top):
                        a, b = Group(i, k, 1), Group(i, k, -1)
                        if a.exists:
                            gather_queries(a, top)
                        plan = (0, 1, 2, 3, "w1", 4, "w3", 5, 6, "w5", 7)
                        for p in plan:
                            if isinstance(p, int):
                                if a.exists:
                                    gather(a, p, top)
                            elif b.exists:
                                weigh(b, int(p[1]))

                    with usual(g):
                        for n in range(NSLOT):
                            g.memset(q_f[n][:, :], 0.0).then_inc(q_clear, 1)
                        g.wait_ge(q_clear, NSLOT)
                        top = g.to_reg(N - 1)
                        first = Group(0, 0, 0)
                        gather_queries(first, top)
                        for j in range(GT):
                            gather(first, j, top)
                        run_steps(g, lambda i, k: step(i, k, top))

                @block.scalar
                def _(act):
                    def make_expand(a, h):
                        act.wait_ge(key_spread, a.s * 2 + (h + 1))
                        if a.past(1):
                            act.wait_ge(expand_ready, a.s * 2 + (h - 1))
                        act.activation(away[h][:, :], KEY[:, :], ACT.Abs, bias=minus_p[:, 0:1]).then_inc(away_ready, 1)
                        act.wait_ge(away_ready, a.s * 2 + (h + 1))
                        if a.past(NSLOT):
                            act.wait_ge(expanded, a.tiles(4 * h + 4 - NSLOT * GT))
                        act.activation(expand[a.slot][h][:, :], away[h][:, :], ACT.Relu, bias=1.0,
                                       scale=-1.0).then_inc(expand_ready, 1)

                    def split_queries(a):
                        act.wait_ge(q_in[a.slot], a.landed)
                        if a.past(NSLOT):
                            act.wait_ge(expanded, a.tiles(-(NSLOT - 1) * GT))
                        act.activation(q_g[a.slot][:, 0:DM], q_f[a.slot][:, :], ACT.Copy).then_inc(q_high, 1)

                    def weigh(b, n):
                        j = ACT_TILES[n]
                        if n == 0:
                            act.wait_ge(z_ready, b.s + 1)
                        if b.past(1):
                            act.wait_ge(sums_done, b.tiles(j + 1 - GT))
                        for h in range(H):
                            cols = slice(h * DK, (h + 1) * DK)
                            last = act.activation(wv[j][:, cols], kv[b.slot][:, j, DM + h * DK:DM + (h + 1) * DK], ACT.Copy,
                                                  scale=zm[b.slot][:, j, h:h + 1])
                        last.then_inc(wv_act, 1)

                    def evacuate(e):
                        act.wait_ge(sums_done, e.tiles(GT))
                        if e.past(NSLOT):
                            act.wait_ge(part_out[e.slot], e.round * 16)
                        act.activation(part_sb[e.slot][:, 0:DM], SUMS[e.half][:, :], ACT.Copy).then_inc(part_ready, 1)
                        act.wait_ge(zsum_done, e.tiles(GT))
                        act.activation(part_sb[e.slot][:, DM:W], SMALL[e.half][:, 0:2 * H],
                                       ACT.Copy).then_inc(part_ready, 1)

                    def step(i, k):
                        a, b, e = Group(i, k, 1), Group(i, k, -1), Group(i, k, -BEHIND)
                        if a.exists:
                            make_expand(a, 0)
                        if b.exists:
                            act.wait_ge(below_ready, b.s + 1)
                            if b.past(NSLOT):
                                act.wait_ge(zsum_done, b.tiles(-(NSLOT - 1) * GT))
                            act.activation(zm[b.slot][:, :, 0:H], below_peak[b.slot][:, :, :], ACT.Exp).then_inc(z_ready, 1)
                            weigh(b, 0)
                        if a.exists:
                            make_expand(a, 1)
                            split_queries(a)
                        if b.exists:
                            weigh(b, 1)
                        if e.exists:
                            evacuate(e)
                        if b.exists:
                            weigh(b, 2)
                            weigh(b, 3)

                    with usual(act):
                        first = Group(0, 0, 0)
                        make_expand(first, 0)
                        make_expand(first, 1)
                        split_queries(first)
                        run_steps(act, step)

                @block.tensor
                def _(pe):
                    def spread_keys(a, h):
                        if h == 0:
                            pe.wait_ge(key_in[a.slot], a.landed)
                        if a.past(1) or h == 1:
                            pe.wait_ge(away_ready, a.s * 2 + h)
                        n = GT // 2 * P
                        pe.matmul(KEY[:, :], ones_b[:, :], key_row[a.slot][:, h * n:(h + 1) * n], start=True,
                                  stop=True).then_inc(key_spread, 1)

                    def expand_queries(c, j):
                        h, m = j // 4, j % 4
                        if m == 0:
                            pe.wait_ge(expand_ready, c.s * 2 + (h + 1))
                        if j == 0:
                            pe.wait_ge(q_split, c.s + 1)
                        if c.past(1) or j >= 2:
                            pe.wait_ge(prod_done, c.tiles(j - 1))
                        pe.matmul(EXPANDED[j % 2][:, :], expand[c.slot][h][:, m * P:(m + 1) * P], q_g[c.slot][:, 0:DM],
                                  start=True, stop=False)
                        pe.matmul(EXPANDED[j % 2][:, :], expand[c.slot][h][:, m * P:(m + 1) * P], q_g[c.slot][:, DM:2 * DM],
                                  start=False, stop=True).then_inc(expanded, 1)

                    def turn_scores(b):
                        pe.wait_ge(score_done, b.tiles(GT))
                        if b.past(1):
                            pe.wait_ge(up_done, b.s)
                        pe.sem_inc(pe_turn, 1)
                        pe.transpose(TURNS[0:GT * H, 0:P], score[b.slot][:, :, :].rearrange("p t h -> p (t h)"),
                                     ident[:, :]).then_inc(score_turned, 1)

                    def turn_back(b):
                        pe.wait_ge(peak_done, b.s + 1)
                        if b.past(1):
                            pe.wait_ge(m_ready, b.s)
                        pe.sem_inc(pe_turn, 1)
                        pe.transpose(TURNS[:, P:P + GT * H], peak[:, :], ident[0:GT * H, 0:GT * H]).then_inc(peak_back, 1)

                    def sums(b, j):
                        for tiles, weighed in ((ACT_TILES, wv_act), (POOL_TILES, wv_pool), (DVE_TILES, wv_dve)):
                            if j in tiles:
                                pe.wait_ge(weighed, b.s * len(tiles) + (tiles.index(j) + 1))
                        if j == 0:
                            pe.wait_ge(pick_ready, b.s + 1)
                            pe.wait_ge(m_ready, b.s + 1)
                            if b.past(2):
                                pe.wait_ge(part_ready, b.s * 2 - 2)
                        pe.matmul(SUMS[b.half][:, :], pick[b.slot][:, j, :], wv[j][:, :], start=j == 0,
                                  stop=j == GT - 1).then_inc(sums_done, 1)
                        pe.matmul(SMALL[b.half][:, 0:2 * H], pick[b.slot][:, j, :], zm[b.slot][:, j, :], start=j == 0,
                                  stop=j == GT - 1).then_inc(zsum_done, 1)

                    def step(i, k):
                        a, b, c, e = Group(i, k, 1), Group(i, k, -1), Group(i, k, 0), Group(i, k, -BEHIND)
                        plan = "x0 x1 T e3 x2 B x3 k0 e4 x4 e5 k1 x5 e6 x6 e7 x7 s0 s1 s2"
                        for p in plan.split():
                            if p[0] == "e" and e.exists:
                                sums(e, int(p[1]))
                            if p[0] == "x" and c.exists:
                                expand_queries(c, int(p[1]))
                            if p[0] == "k" and a.exists:
                                spread_keys(a, int(p[1]))
                            if p[0] == "s" and b.exists:
                                sums(b, int(p[1]))
                            if p == "T" and b.exists:
                                turn_scores(b)
                            if p == "B" and b.exists:
                                turn_back(b)

                    with usual(pe):
                        first = Group(0, 0, 0)
                        spread_keys(first, 0)
                        spread_keys(first, 1)
                        run_steps(pe, step)

                @block.vector
                def _(v):
                    def product(c, j):
                        v.wait_ge(kv_in[c.slot][j], c.landed)
                        v.wait_ge(expanded, c.tiles(j + 1))
                        if c.past(1) or j >= 3:
                            v.wait_ge(score_done, c.tiles(j - 2))
                        v.tensor_tensor(out=prod[(c.slot * GT + j) % 3][:, :], in0=kv[c.slot][:, j, 0:DM],
                                        in1=EXPANDED[j % 2][:, :], op=ALU.mult).then_inc(prod_done, 1)

                    def split_queries(a):
                        v.wait_ge(q_high, a.s + 1)
                        v.tensor_tensor(out=q_g[a.slot][:, DM:2 * DM], in0=q_f[a.slot][:, :],
                                        in1=q_g[a.slot][:, 0:DM].bitcast(f32), op=ALU.subtract).then_inc(q_split, 1)

                    def reduce(c, j):
                        v.wait_ge(prod_done, c.tiles(j + 1))
                        if j == 0 and c.past(NSLOT):
                            v.wait_ge(below_ready, c.s - (NSLOT - 1))
                        v.tensor_reduce(out=score[c.slot][:, j, :], in_=heads(prod[(c.slot * GT + j) % 3][:, :]),
                                        axis=AX.X, op=ALU.add).then_inc(score_done, 1)

                    def scans(b):
                        v.wait_ge(score_turned, b.s + 1)
                        v.wait_ge(breaks_in[b.slot], b.landed)
                        if b.past(1):
                            v.wait_ge(peak_done, b.s)
                        v.tensor_tensor_scan(out=up[:, :], data0=breaks_g[b.slot][:, 0:P], data1=TURNS[0:GT * H, 0:P],
                                             initial=-BIG, op0=ALU.add, op1=ALU.max).then_inc(up_done, 1)
                        v.wait_ge(up_done, b.s + 1)
                        if b.past(1):
                            v.wait_ge(peak_back, b.s)
                        v.tensor_tensor_scan(out=peak[:, ::-1], data0=breaks_g[b.slot][:, 1:P + 1][:, ::-1],
                                             data1=up[:, ::-1], initial=-BIG,
                                             op0=ALU.add, op1=ALU.max).then_inc(peak_done, 1)

                    def subtract(b):
                        m = TURNS[:, P:P + GT * H].rearrange("p (t h) -> p t h", t=GT)
                        v.wait_ge(peak_back, b.s + 1)
                        if b.past(NSLOT):
                            v.wait_ge(z_ready, b.s - (NSLOT - 1))
                            v.wait_ge(zsum_done, b.tiles(-(NSLOT - 1) * GT))
                        v.tensor_tensor(out=below_peak[b.slot][:, :, :], in0=score[b.slot][:, :, :], in1=m,
                                        op=ALU.subtract).then_inc(below_ready, 1)
                        v.tensor_tensor(out=zm[b.slot][:, :, H:2 * H], in0=m,
                                        in1=runs_g[b.slot][:, :, 1:2].to_broadcast([P, GT, H]),
                                        op=ALU.mult).then_inc(m_ready, 1)

                    def make_picks(b):
                        if b.past(NSLOT):
                            v.wait_ge(zsum_done, b.tiles(-(NSLOT - 1) * GT))
                        v.tensor_tensor(out=pick[b.slot][:, :, :], in0=iota_row[:, :].unsqueeze(1).to_broadcast([P, GT, P]),
                                        in1=runs_g[b.slot][:, :, 0:1].to_broadcast([P, GT, P]),
                                        op=ALU.is_equal).then_inc(pick_ready, 1)

                    def weigh(b, j):
                        v.wait_ge(z_ready, b.s + 1)
                        if b.past(1):
                            v.wait_ge(sums_done, b.tiles(j + 1 - GT))
                        v.tensor_tensor(out=heads(wv[j][:, :]), in0=heads(kv[b.slot][:, j, DM:2 * DM]),
                                        in1=zm[b.slot][:, j, 0:H].unsqueeze(2).to_broadcast([P, H, DK]),
                                        op=ALU.mult).then_inc(wv_dve, 1)

                    def step(i, k):
                        a, b, c = Group(i, k, 1), Group(i, k, -1), Group(i, k, 0)
                        plan = "p0 copy p1 scans r0 p2 r1 subtract p3 r2 p4 r3 picks p5 r4 p6 r5 weigh p7 r6 split r7"
                        for p in plan.split():
                            if p[0] == "p" and p != "picks" and c.exists:
                                product(c, int(p[1]))
                            if p[0] == "r" and c.exists:
                                reduce(c, int(p[1]))
                            if p == "split" and a.exists:
                                split_queries(a)
                            if not b.exists:
                                continue
                            if p == "copy":
                                v.tensor_copy(runs_g[b.slot][:, :, :],
                                              edge_runs[:, ds(b.tiles(0), GT), :]).then_inc(runs_ready, 1)
                            if p == "scans":
                                scans(b)
                            if p == "subtract":
                                v.wait_ge(runs_ready, b.s + 1)
                                subtract(b)
                            if p == "picks":
                                v.wait_ge(runs_ready, b.s + 1)
                                make_picks(b)
                            if p == "weigh":
                                for t in DVE_TILES:
                                    weigh(b, t)

                    with usual(v):
                        split_queries(Group(0, 0, 0))
                        run_steps(v, step)

        end_of_stage()

        wo_sb = sb("wo_sb", [P, 4, DM])
        w1_sb = sb("w1_sb", [P, 4, DFF])
        w2_sb = sb("w2_sb", [P, 2, DM])
        b1_sb = sb("b1_sb", [P, 2])
        vec = {n: sb(f"{n}_sb", [P, DM]) for n in ("g1", "h1", "g2", "h2", "b2")}
        with ExitStack() as st:
            w5_in = sem("w5_in")
            crow = sb("crow", [BROWS, BLOCKS, W], f32, st)
            orow = sb("orow", [BROWS, BLOCKS, W], f32, st)
            CT = [sb(f"CT{c}", [P, TILES], f32, st) for c in range(4)]
            zT = sb("zT", [H, TILES], f32, st)
            mT = sb("mT", [H, TILES], f32, st)
            same = sb("same", [H, TILES], f32, st)
            penal = sb("penal", [H, TILES], f32, st)
            mrun = sb("mrun", [H, TILES], f32, st)
            keep = sb("keep", [H, TILES], f32, st)
            take = sb("take", [H, TILES], f32, st)
            zrun = sb("zrun", [H, TILES], f32, st)
            head_of = sb("head_of", [H, DM], f32, st)
            c_in = sem("c_in")
            head_ready = sem("head_ready")
            c_turned = sem("c_turned")
            c_taken = sem("c_taken")
            diff_ready = sem("diff_ready")
            exp_ready = sem("exp_ready")
            spread4 = sem("spread4")
            run_ready = sem("run_ready")
            back = sem("back")
            back_taken = sem("back_taken")
            c_out = sem("c_out")
            d4 = sem("d4")
            half = TILES // 2
            with nc.Block() as block:
                @block.sync
                def _(sp):
                    first_of = parts[0:TILES * FEW, :].rearrange("(b p r) f -> r p b f", p=BROWS, r=FEW)
                    sp.dma_start(crow[:, :, :], first_of[0]).then_inc(c_in, 16)
                    sp.dma_start(wo_sb[:, :, :], Wo.rearrange("(c p) n -> p c n", p=P)).then_inc(w5_in, 16)
                    sp.dma_start(w1_sb[:, :, :], W1.rearrange("(c p) n -> p c n", p=P)).then_inc(w5_in, 16)
                    sp.dma_start(w2_sb[:, :, :], W2.rearrange("(c p) n -> p c n", p=P)).then_inc(w5_in, 16)
                    with nc.allow_non_contiguous_dma(reason="256 biases, once"):
                        sp.dma_start(b1_sb[:, :], b1.rearrange("(c p) -> p c", p=P)).then_inc(w5_in, 16)
                    for n, a in (("g1", ln1_g), ("h1", ln1_b), ("g2", ln2_g), ("h2", ln2_b), ("b2", b2)):
                        sp.dma_start(vec[n][:, :], a.unsqueeze(0).to_broadcast([P, DM])).then_inc(w5_in, 16)
                    sp.wait_ge(w5_in, 9 * 16)
                    sp.wait_ge(back_taken, 2 * BLOCKS)
                    sp.dma_start(firsts[0:TILES, :].rearrange("(b p) f -> p b f", p=BROWS), orow[:, :, :]).then_inc(c_out, 16)
                    sp.wait_ge(c_out, 16)

                @block.gpsimd
                def _(g):
                    chain = Chain(g, head_ready)
                    chain(g.memset(head_of[:, :], 1.0))
                    chain(g.affine_select(out=head_of[:, :], in_=head_of[:, :], compare_op=ALU.is_ge, fill=0.0,
                                          base=0, pattern=[[1, DM]], channel_multiplier=-DK))
                    chain(g.affine_select(out=head_of[:, :], in_=head_of[:, :], compare_op=ALU.is_ge, fill=0.0,
                                          base=DK - 1, pattern=[[-1, DM]], channel_multiplier=DK))

                @block.tensor
                def _(pe):
                    pe.wait_ge(c_in, 16)
                    for b in range(BLOCKS):
                        if b >= 2:
                            pe.wait_ge(c_taken, 6 * (b - 1))
                        for c in range(4):
                            pe.transpose(bank[b % 2][:, c * BROWS:(c + 1) * BROWS], crow[:, b, c * P:(c + 1) * P],
                                         ident[0:BROWS, 0:BROWS])
                        pe.transpose(bank[2 + b % 2][0:H, 0:BROWS], crow[:, b, DM:DM + H], ident[0:BROWS, 0:BROWS])
                        pe.transpose(bank[2 + b % 2][0:H, 256:256 + BROWS], crow[:, b, DM + H:W],
                                     ident[0:BROWS, 0:BROWS]).then_inc(c_turned, 1)
                    pe.wait_ge(head_ready, 3)
                    pe.wait_ge(c_taken, 6 * BLOCKS)
                    pe.wait_ge(exp_ready, 3)
                    for c in range(4):
                        if c >= 2:
                            pe.wait_ge(run_ready, c - 1)
                        for a, rows in enumerate((keep, take)):
                            for i in range(2):
                                last = pe.matmul(bank[4 * (c % 2) + 2 * a + i][:, 0:half], head_of[:, c * P:(c + 1) * P],
                                                 rows[:, i * half:(i + 1) * half], start=True, stop=True)
                        last.then_inc(spread4, 1)
                    pe.wait_ge(run_ready, 5)
                    for b in range(BLOCKS):
                        if b >= 2:
                            pe.wait_ge(back_taken, 2 * (b - 1))
                        cols = slice(b * BROWS, (b + 1) * BROWS)
                        for c in range(4):
                            pe.transpose(bank[b % 2][0:BROWS, c * P:(c + 1) * P], CT[c][:, cols], ident[:, :])
                        pe.transpose(bank[2 + b % 2][0:BROWS, 0:H], zrun[:, cols], ident[0:H, 0:H])
                        pe.transpose(bank[2 + b % 2][0:BROWS, H:2 * H], mrun[:, cols], ident[0:H, 0:H]).then_inc(back, 1)

                @block.scalar
                def _(act):
                    act.wait_ge(diff_ready, 2)
                    act.activation(keep[:, :], keep[:, :], ACT.Exp).then_inc(exp_ready, 1)
                    act.activation(take[:, :], take[:, :], ACT.Exp).then_inc(exp_ready, 1)

                @block.vector
                def _(v):
                    chain = Chain(v, d4)
                    for b in range(BLOCKS):
                        v.wait_ge(c_turned, b + 1)
                        cols = slice(b * BROWS, (b + 1) * BROWS)
                        for c in range(4):
                            v.tensor_copy(CT[c][:, cols], bank[b % 2][:, c * BROWS:(c + 1) * BROWS]).then_inc(c_taken, 1)
                        v.tensor_copy(zT[:, cols], bank[2 + b % 2][0:H, 0:BROWS]).then_inc(c_taken, 1)
                        v.tensor_copy(mT[:, cols], bank[2 + b % 2][0:H, 256:256 + BROWS]).then_inc(c_taken, 1)
                    v.wait_ge(c_taken, 6 * BLOCKS)
                    chain(v.memset(same[:, 0:1], 0.0))
                    chain(v.tensor_tensor(out=same[:, 1:TILES], in0=first_dst[0:H, 1:TILES],
                                          in1=first_dst[0:H, 0:TILES - 1], op=ALU.is_equal))
                    chain(v.tensor_scalar(out=penal[:, :], in0=same[:, :], scalar1=-1.0, scalar2=BIG, op0=ALU.add,
                                          op1=ALU.mult))
                    chain(v.tensor_tensor_scan(out=mrun[:, :], data0=penal[:, :], data1=mT[:, :], initial=-BIG,
                                               op0=ALU.add, op1=ALU.max))
                    chain(v.memset(keep[:, 0:1], 0.0))
                    chain(v.tensor_tensor(out=keep[:, 1:TILES], in0=mrun[:, 0:TILES - 1], in1=mrun[:, 1:TILES],
                                          op=ALU.subtract))
                    v.tensor_scalar(out=keep[:, :], in0=keep[:, :], scalar1=0.0, scalar2=None,
                                    op0=ALU.min).then_inc(diff_ready, 1)
                    v.tensor_tensor(out=take[:, :], in0=mT[:, :], in1=mrun[:, :], op=ALU.subtract).then_inc(diff_ready, 1)
                    v.wait_ge(exp_ready, 2)
                    v.tensor_tensor(out=keep[:, :], in0=keep[:, :], in1=same[:, :], op=ALU.mult).then_inc(exp_ready, 1)
                    v.wait_ge(exp_ready, 3)
                    chain(v.tensor_tensor(out=zT[:, :], in0=zT[:, :], in1=take[:, :], op=ALU.mult))
                    for c in range(4):
                        v.wait_ge(spread4, c + 1)
                        for i in range(2):
                            cols = slice(i * half, (i + 1) * half)
                            chain(v.tensor_tensor(out=CT[c][:, cols], in0=CT[c][:, cols], in1=bank[4 * (c % 2) + 2 + i][:, 0:half],
                                                  op=ALU.mult))
                        chain(v.tensor_tensor_scan(out=CT[c][:, 0:half], data0=bank[4 * (c % 2)][:, 0:half], data1=CT[c][:, 0:half],
                                                   initial=0.0, op0=ALU.mult, op1=ALU.add))
                        v.tensor_tensor_scan(out=CT[c][:, half:TILES], data0=bank[4 * (c % 2) + 1][:, 0:half],
                                             data1=CT[c][:, half:TILES], initial=CT[c][:, half - 1:half],
                                             op0=ALU.mult, op1=ALU.add).then_inc(run_ready, 1)
                    v.tensor_tensor_scan(out=zrun[:, :], data0=keep[:, :], data1=zT[:, :], initial=0.0,
                                         op0=ALU.mult, op1=ALU.add).then_inc(run_ready, 1)
                    for b in range(BLOCKS):
                        v.wait_ge(back, b + 1)
                        v.tensor_copy(orow[:, b, 0:DM], bank[b % 2][0:BROWS, :]).then_inc(back_taken, 1)
                        v.tensor_copy(orow[:, b, DM:W], bank[2 + b % 2][0:BROWS, 0:2 * H]).then_inc(back_taken, 1)

        end_of_stage()

        with ExitStack() as st:
            half_neg = sb("half_neg", [P, 1], f32, st)
            ring = lambda n, name, shape, dt=f32: [sb(f"{name}{i}", shape, dt, st) for i in range(n)]
            rows5 = ring(2, "rows5_", [P, 3], i32)
            pa, pb = ring(2, "pa", [P, W]), ring(2, "pb", [P, W])
            x_one, x_two = ring(2, "x_one", [P, DM]), ring(2, "x_two", [P, DM])
            top_m = ring(2, "top_m", [P, H])
            diff, wgt, zz = ring(2, "diff", [P, 2, H]), ring(2, "wgt", [P, 2, H]), ring(2, "zz", [P, 2, H])
            attn = ring(2, "attn", [P, DM])
            aT, x1T, hT = ring(2, "aT", [P, 4, P]), ring(2, "x1T", [P, 4, P]), ring(2, "hT", [P, 2, P])
            r1 = ring(2, "r1", [P, DM])
            x1 = ring(2, "x1_", [P, DM])
            x1b = ring(4, "x1b", [P, DM])
            y = ring(2, "y", [P, DM])
            y2 = ring(2, "y2_", [P, DM])
            z3 = ring(2, "z3_", [P, DM])
            o_sb = ring(2, "o_sb", [P, DM])
            stats = [ring(2, f"stats{i}", [P, 6]) for i in range(3)]
            mv = [ring(2, f"mv{i}_", [P, 2]) for i in range(3)]
            rstd = [ring(2, f"rstd{i}_", [P, 2]) for i in range(3)]
            go5 = sem("go5")
            a_in, b_in, more_in, one_in, two_in, o_stored = (
                [sem(f"{n}{i}") for i in range(2)] for n in ("a_in", "b_in", "more_in", "one_in", "two_in", "o_stored"))
            diff5, exp5, attn_ready = sem("diff5"), sem("exp5"), sem("attn_ready")
            a_turned, aT_ready, o_done = sem("a_turned"), sem("aT_ready"), sem("o_done")
            added, moments, powered, rooted, normed = (
                [sem(f"{n}{i}") for i in range(3)] for n in ("added", "moments", "powered", "rooted", "normed"))
            x1_ready, x1b_ready, y2_ready = sem("x1_ready"), sem("x1b_ready"), sem("y2_ready")
            x1_turned, x1T_ready = sem("x1_turned"), sem("x1T_ready")
            h_done, hT_ready, f_done = sem("h_done"), sem("hT_ready"), sem("f_done")
            pconst = sem("pconst")
            rows_copied, gained, d5_turn = sem("rows_copied"), sem("gained"), sem("d5_turn")
            topped, shifted, sum_step = sem("topped"), sem("shifted"), sem("sum_step")
            weighted, scaled = sem("weighted"), sem("scaled")
            measured, joined = ([sem(f"{n}{i}") for i in range(3)] for n in ("measured", "joined"))

            MERGE, ATTEND, NORM1, FEED, NORM2, NORM3, FINISH = 1, 2, 3, 4, 5, 6, 7
            STEPS = NT + FINISH
            RING5 = 4

            def loop5(eng, one):
                for s in range(2 * RING5):
                    one(s, s % RING5)
                with eng.Fori(2 * RING5, NT - RING5, RING5) as s:
                    for k in range(RING5):
                        one(s + k, k)
                for s in range(NT - 1, STEPS):
                    one(s, s % RING5)

            assert (NT - 1) % RING5 == 0

            def on(t):
                return not isinstance(t, int) or 0 <= t < NT

            def from_tile(t, n):
                return not isinstance(t, int) or t >= n

            def rows_of(t):
                return slice(LAST_START, N) if isinstance(t, int) and t == NT - 1 else ds(t * P, P)

            def seen(t, q):
                return (t - q) * 8 + 16

            with nc.Block() as block:
                @block.sync
                def _(sp):
                    def step(s, k):
                        t, q = s - ATTEND, (k - ATTEND) % 2
                        if on(t):
                            if from_tile(t, 2):
                                sp.wait_ge(added[0], t - 1)
                            sp.dma_start(x_one[q][:, :], x[rows_of(t), :]).then_inc(one_in[q], 16)
                        t, q = s - NORM2, (k - NORM2) % 2
                        if on(t):
                            if from_tile(t, 2):
                                sp.wait_ge(added[2], t - 1)
                            sp.dma_start(x_two[q][:, :], x[rows_of(t), :]).then_inc(two_in[q], 16)
                        t, q = s - FINISH, (k - FINISH) % 2
                        if on(t):
                            if isinstance(t, int) and t == NT - 1:
                                sp.wait_ge(o_stored[1], 8 * (NT - 1))
                            sp.wait_ge(normed[2], t + 1)
                            sp.dma_start(out[rows_of(t), :], o_sb[q][:, :]).then_inc(o_stored[q], 16)

                    loop5(sp, step)
                    sp.wait_ge(o_stored[0], 16 * (NT // 2 + 1))

                @block.gpsimd
                def _(g):
                    g.memset(half_neg[:, :], -0.5).then_inc(pconst, 1)
                    topa, topb, topm = g.to_reg(NULL_A), g.to_reg(NULL_B), g.to_reg(NULL_MORE - 1)
                    most = g.value_load(most_runs[P - 1:P, 0:1])
                    g.wait_ge(pconst, 1)

                    def fetch(t, q):
                        if from_tile(t, 2):
                            g.wait_ge(attn_ready, t - 1)
                            g.sem_inc(go5, 1)
                        g.tensor_copy(rows5[q][:, :],
                                      node_rows[:, ds(t, 1), :].rearrange("p a b -> p (a b)")).then_inc(rows_copied, 1)
                        g.wait_ge(rows_copied, t + 1)
                        g.sem_inc(go5, 1)
                        g.indirect_dma_start(out=pa[q][:, :], out_offset=None, in_=parts[:, :],
                                             in_offset=bass.IndirectOffsetOnAxis(ap=rows5[q][:, 0:1], axis=0),
                                             bounds_check=topa, oob_is_err=False).then_inc(a_in[q], 16)
                        with g.If(most >= FEW):
                            g.wait_ge(a_in[q], seen(t, q))
                            g.sem_inc(go5, 1)
                            g.indirect_dma_start(out=pa[q][:, :], out_offset=None, in_=more_parts[:, :],
                                                 in_offset=bass.IndirectOffsetOnAxis(ap=rows5[q][:, 2:3], axis=0),
                                                 bounds_check=topm, oob_is_err=False).then_inc(more_in[q], 16)
                        with g.Else():
                            g.sem_inc(more_in[q], 16)
                        g.indirect_dma_start(out=pb[q][:, :], out_offset=None, in_=firsts[:, :],
                                             in_offset=bass.IndirectOffsetOnAxis(ap=rows5[q][:, 1:2], axis=0),
                                             bounds_check=topb, oob_is_err=False).then_inc(b_in[q], 16)

                    def inverse_root(i, t, q):
                        g.wait_ge(moments[i], 2 * t + 2)
                        g.tensor_tensor(out=rstd[i][q][:, 0:1], in0=mv[i][q][:, 1:2], in1=half_neg[:, :],
                                        op=ALU.pow).then_inc(powered[i], 1)
                        g.wait_ge(powered[i], t + 1)
                        g.tensor_tensor(out=rstd[i][q][:, 1:2], in0=mv[i][q][:, 0:1], in1=rstd[i][q][:, 0:1],
                                        op=ALU.mult).then_inc(rooted[i], 1)

                    def step(s, k):
                        if on(s):
                            fetch(s, k % 2)
                        t1, q1 = s - NORM1, (k - NORM1) % 2
                        t2, q2 = s - NORM2, (k - NORM2) % 2
                        t3, q3 = s - NORM3, (k - NORM3) % 2
                        if on(t1):
                            inverse_root(0, t1, q1)
                        if on(t2):
                            inverse_root(1, t2, q2)
                        if on(t1):
                            g.wait_ge(normed[0], t1 + 1)
                            g.tensor_tensor(out=x1[q1][:, :], in0=x1[q1][:, :], in1=vec["g1"][:, :],
                                            op=ALU.mult).then_inc(gained, 1)
                            g.wait_ge(gained, t1 + 1)
                            g.tensor_tensor(out=x1[q1][:, :], in0=x1[q1][:, :], in1=vec["h1"][:, :],
                                            op=ALU.add).then_inc(x1_ready, 1)
                        if on(t2):
                            g.wait_ge(normed[1], t2 + 1)
                            g.tensor_tensor(out=y2[q2][:, :], in0=y2[q2][:, :], in1=vec["g2"][:, :],
                                            op=ALU.mult).then_inc(y2_ready, 1)
                        if on(t3):
                            inverse_root(2, t3, q3)

                    loop5(g, step)

                @block.tensor
                def _(pe):

                    def turn(src_, bk, turned):
                        for c in range(4):
                            last = pe.transpose(bank[bk][:, c * P:(c + 1) * P], src_[:, c * P:(c + 1) * P], ident[:, :])
                        last.then_inc(turned, 1)

                    def step(s, k):
                        tf, qf = s - FEED, (k - FEED) % 2
                        ta, qa = s - ATTEND, (k - ATTEND) % 2
                        if on(tf):
                            pe.wait_ge(x1_ready, tf + 1)
                            if from_tile(tf, 1):
                                pe.wait_ge(x1T_ready, tf)
                            turn(x1[qf], 1, x1_turned)
                        if on(ta):
                            pe.wait_ge(attn_ready, ta + 1)
                            if from_tile(ta, 1):
                                pe.wait_ge(aT_ready, ta)
                            turn(attn[qa], 0, a_turned)
                        if on(tf):
                            pe.wait_ge(x1T_ready, tf + 1)
                            if from_tile(tf, 1):
                                pe.wait_ge(hT_ready, 2 * tf)
                            for f in range(2):
                                for c in range(4):
                                    last = pe.matmul(bank[4][:, f * P:(f + 1) * P], w1_sb[:, c, f * P:(f + 1) * P],
                                                     x1T[qf][:, c, :], start=c == 0, stop=c == 3)
                            last.then_inc(h_done, 1)
                        if on(ta):
                            pe.wait_ge(aT_ready, ta + 1)
                            if from_tile(ta, 2):
                                pe.wait_ge(added[0], ta - 1)
                            for c in range(4):
                                last = pe.matmul(bank[2 + qa][:, :], aT[qa][:, c, :], wo_sb[:, c, :], start=c == 0, stop=c == 3)
                            last.then_inc(o_done, 1)
                        if on(tf):
                            pe.wait_ge(hT_ready, 2 * tf + 2)
                            if from_tile(tf, 2):
                                pe.wait_ge(added[1], tf - 1)
                            for f in range(2):
                                last = pe.matmul(bank[5 + qf][:, :], hT[qf][:, f, :], w2_sb[:, f, :], start=f == 0, stop=f == 1)
                            last.then_inc(f_done, 1)

                    loop5(pe, step)

                @block.scalar
                def _(act):

                    def evacuate(t, dst_, bk, turned, used_, ready):
                        act.wait_ge(turned, t + 1)
                        if from_tile(t, 2):
                            act.wait_ge(used_, t - 1)
                        act.activation(dst_[:, :, :], bank[bk][:, :].rearrange("p (c n) -> p c n", c=4),
                                       ACT.Copy).then_inc(ready, 1)

                    def norm(i, t, q, a, o, free, n):
                        act.wait_ge(rooted[i], t + 1)
                        if from_tile(t, 2):
                            act.wait_ge(free, n)
                        act.activation(o[:, :], a[:, :], ACT.Identity, bias=rstd[i][q][:, 1:2],
                                       scale=rstd[i][q][:, 0:1]).then_inc(normed[i], 1)

                    def step(s, k):
                        tf, qf = s - FEED, (k - FEED) % 2
                        t, q = s - MERGE, (k - MERGE) % 2
                        if on(t):
                            act.wait_ge(diff5, 2 * t + 2)
                            if from_tile(t, 2):
                                act.wait_ge(scaled, 2 * t - 2)
                            act.activation(wgt[q][:, :, :], diff[q][:, :, :], ACT.Exp).then_inc(exp5, 1)
                        if on(tf):
                            evacuate(tf, x1T[qf], 1, x1_turned, h_done, x1T_ready)
                        t, q = s - ATTEND, (k - ATTEND) % 2
                        if on(t):
                            evacuate(t, aT[q], 0, a_turned, o_done, aT_ready)
                        t, q = s - FINISH, (k - FINISH) % 2
                        if on(t):
                            norm(2, t, q, z3[q], o_sb[q], o_stored[q], seen(t, q) - 16)
                        t, q = s - NORM1, (k - NORM1) % 2
                        if on(t):
                            if from_tile(t, 2):
                                act.wait_ge(x1_turned, t - 1)
                            norm(0, t, q, r1[q], x1[q], x1b_ready, t - 1)
                        if on(tf):
                            act.wait_ge(h_done, tf + 1)
                            if from_tile(tf, 2):
                                act.wait_ge(f_done, tf - 1)
                            for f in range(2):
                                act.activation(hT[qf][:, f, :], bank[4][:, f * P:(f + 1) * P], ACT.Relu,
                                               bias=b1_sb[:, f:f + 1]).then_inc(hT_ready, 1)
                        t, q = s - NORM2, (k - NORM2) % 2
                        if on(t):
                            norm(1, t, q, y[q], y2[q], added[2], t - 1)

                    loop5(act, step)

                @block.vector
                def _(v):
                    heads = lambda a: a.rearrange("p (h d) -> p h d", h=H)
                    wide = lambda a: a.unsqueeze(2).to_broadcast([P, H, DK])

                    def step(s, k):
                        t1, q1 = s - NORM1, (k - NORM1) % 2
                        t2, q2 = s - NORM2, (k - NORM2) % 2
                        t3, q3 = s - NORM3, (k - NORM3) % 2
                        tm, qm = s - MERGE, (k - MERGE) % 2
                        rows = ((t1, q1, r1), (t2, q2, y), (t3, q3, z3))
                        a, b, w, z = pa[qm], pb[qm], wgt[qm], zz[qm]

                        def add(i, in0, in1):
                            t, q, o = rows[i]
                            if from_tile(t, 2):
                                v.wait_ge(normed[i], t - 1)
                            v.tensor_tensor(out=o[q][:, :], in0=in0, in1=in1, op=ALU.add).then_inc(added[i], 1)

                        def measure(i):
                            t, q, o = rows[i]
                            v.wait_ge(added[i], t + 1)
                            v.bn_stats(out=stats[i][q][:, :], in_=o[q][:, :]).then_inc(measured[i], 1)

                        def join(i):
                            t, q, _ = rows[i]
                            v.wait_ge(measured[i], t + 1)
                            if from_tile(t, 2):
                                v.wait_ge(rooted[i], t - 1)
                            v.sem_inc(d5_turn, 1)
                            v.bn_aggr(out=mv[i][q][:, :], in_=stats[i][q][:, :]).then_inc(joined[i], 1)

                        def moment(i):
                            t, q, _ = rows[i]
                            v.wait_ge(joined[i], t + 1)
                            v.tensor_scalar(out=mv[i][q][:, 0:1], in0=mv[i][q][:, 0:1], scalar1=-1.0, scalar2=None,
                                            op0=ALU.mult).then_inc(moments[i], 1)
                            v.tensor_scalar(out=mv[i][q][:, 1:2], in0=mv[i][q][:, 1:2], scalar1=EPS, scalar2=None,
                                            op0=ALU.add).then_inc(moments[i], 1)

                        if on(t1):
                            v.wait_ge(o_done, t1 + 1)
                            v.wait_ge(one_in[q1], seen(t1, q1))
                            add(0, x_one[q1][:, :], bank[2 + q1][:, :])
                        if on(tm):
                            v.wait_ge(a_in[qm], seen(tm, qm))
                            v.wait_ge(more_in[qm], seen(tm, qm))
                            v.wait_ge(b_in[qm], seen(tm, qm))
                            if from_tile(tm, 2):
                                v.wait_ge(diff5, 2 * tm - 2)
                            v.tensor_tensor(out=top_m[qm][:, :], in0=a[:, DM + H:W], in1=b[:, DM + H:W],
                                            op=ALU.max).then_inc(topped, 1)
                        if on(t1):
                            measure(0)
                        if on(tm):
                            v.wait_ge(topped, tm + 1)
                            if from_tile(tm, 2):
                                v.wait_ge(exp5, tm - 1)
                            v.tensor_tensor(out=diff[qm][:, 0, :], in0=a[:, DM + H:W], in1=top_m[qm][:, :],
                                            op=ALU.subtract).then_inc(diff5, 1)
                            v.tensor_tensor(out=diff[qm][:, 1, :], in0=b[:, DM + H:W], in1=top_m[qm][:, :],
                                            op=ALU.subtract).then_inc(diff5, 1)
                        if on(t1):
                            join(0)
                        if on(t2):
                            v.wait_ge(f_done, t2 + 1)
                            v.wait_ge(x1b_ready, t2 + 1)
                            add(1, x1b[(k - NORM2) % 4][:, :], bank[5 + q2][:, :])
                        if on(t1):
                            moment(0)
                        if on(t3):
                            v.wait_ge(two_in[q3], seen(t3, q3))
                            v.tensor_tensor(out=x_two[q3][:, :], in0=x_two[q3][:, :], in1=vec["h2"][:, :],
                                            op=ALU.add).then_inc(shifted, 1)
                        if on(t2):
                            measure(1)
                        if on(tm):
                            v.wait_ge(exp5, tm + 1)
                            if from_tile(tm, 2):
                                v.wait_ge(scaled, 2 * tm - 2)
                            v.tensor_tensor(out=z[:, 0, :], in0=a[:, DM:DM + H], in1=w[:, 0, :],
                                            op=ALU.mult).then_inc(sum_step, 1)
                            v.tensor_tensor(out=z[:, 1, :], in0=b[:, DM:DM + H], in1=w[:, 1, :],
                                            op=ALU.mult).then_inc(sum_step, 1)
                        if on(t2):
                            join(1)
                        if on(t3):
                            v.wait_ge(shifted, t3 + 1)
                            v.wait_ge(y2_ready, t3 + 1)
                            add(2, x_two[q3][:, :], y2[q3][:, :])
                        if on(t2):
                            moment(1)
                        if on(tm):
                            v.wait_ge(sum_step, tm * 5 + 2)
                            v.tensor_tensor(out=z[:, 0, :], in0=z[:, 0, :], in1=z[:, 1, :],
                                            op=ALU.add).then_inc(sum_step, 1)
                        if on(t3):
                            measure(2)
                        if on(tm):
                            v.wait_ge(sum_step, tm * 5 + 3)
                            v.tensor_scalar(out=z[:, 0, :], in0=z[:, 0, :], scalar1=1e-30, scalar2=None,
                                            op0=ALU.max).then_inc(sum_step, 1)
                        if on(t3):
                            join(2)
                        if on(tm):
                            v.wait_ge(sum_step, tm * 5 + 4)
                            v.reciprocal(z[:, 1, :], z[:, 0, :]).then_inc(sum_step, 1)
                        if on(t3):
                            moment(2)
                        if on(tm):
                            v.wait_ge(sum_step, tm * 5 + 5)
                            v.tensor_tensor(out=w[:, :, :], in0=w[:, :, :], in1=z[:, 1:2, :].to_broadcast([P, 2, H]),
                                            op=ALU.mult).then_inc(weighted, 1)
                        t, q = s - NORM1, (k - NORM1) % 2
                        if on(t - 1):
                            v.wait_ge(x1_ready, t)
                            if from_tile(t - 1, 4):
                                v.wait_ge(added[1], t - 4)
                            v.tensor_tensor(out=x1b[(k - NORM1 - 1) % 4][:, :], in0=x1[1 - q][:, :], in1=vec["b2"][:, :],
                                            op=ALU.add).then_inc(x1b_ready, 1)
                        if on(tm):
                            v.wait_ge(weighted, tm + 1)
                            v.tensor_tensor(out=heads(a[:, 0:DM]), in0=heads(a[:, 0:DM]), in1=wide(w[:, 0, :]),
                                            op=ALU.mult).then_inc(scaled, 1)
                            v.tensor_tensor(out=heads(b[:, 0:DM]), in0=heads(b[:, 0:DM]), in1=wide(w[:, 1, :]),
                                            op=ALU.mult).then_inc(scaled, 1)
                            v.wait_ge(scaled, 2 * tm + 2)
                            if from_tile(tm, 2):
                                v.wait_ge(a_turned, tm - 1)
                            v.tensor_tensor(out=attn[qm][:, :], in0=a[:, 0:DM], in1=b[:, 0:DM],
                                            op=ALU.add).then_inc(attn_ready, 1)

                    loop5(v, step)


_INS = ['x', 'src', 'dst', 'L0_gnn_Wq', 'L0_gnn_Wk', 'L0_gnn_Wv', 'L0_gnn_Wo', 'L0_gnn_ln1_g', 'L0_gnn_ln1_b',
        'L0_gnn_ln2_g', 'L0_gnn_ln2_b', 'L0_gnn_W1', 'L0_gnn_b1', 'L0_gnn_W2', 'L0_gnn_b2']
_OUTS = [((6250, 512), 'float32')]


def kernel(**inputs):
    import numpy as _np
    import concourse.bacc as _bacc
    from concourse import mybir as _mybir
    from concourse.bass_utils import run_bass_kernel_spmd as _run

    nc = _bacc.Bacc("TRN2", target_bir_lowering=False, num_devices=1)
    arrays, args = {}, []
    for name in _INS:
        a = _np.ascontiguousarray(inputs[name])
        arrays[f"in_{name}_dram"] = a
        args.append(nc.dram_tensor(f"in_{name}_dram", a.shape, _mybir.dt.from_np(a.dtype), kind="ExternalInput").ap())
    for i, (shape, dtype) in enumerate(_OUTS):
        dt = _mybir.dt.from_np(_np.dtype(dtype))
        args.append(nc.dram_tensor(f"out_{i}_dram", shape, dt, kind="ExternalOutput").ap())
    build(nc, *args)
    r = _run(nc, [arrays], core_ids=[0])
    return r.results[0]["out_0_dram"]
```
